# Optimizing a Trainium2 kernel written in Bass

```python
import numpy as np
import jax
import jax.numpy as jnp

def _softmax(x, axis=-1):
    return jax.nn.softmax(x, axis=axis)

def _gelu(x):
    return jax.nn.gelu(x, approximate=True)

def _silu(x):
    return jax.nn.silu(x)

def _sigmoid(x):
    return jax.nn.sigmoid(x)

def _layernorm(x, axis=-1, eps=1e-05):
    m = jnp.mean(x, axis=axis, keepdims=True)
    v = jnp.var(x, axis=axis, keepdims=True)
    return (x - m) / jnp.sqrt(v + eps)

def _scatter_add(tgt, idx, src, axis=0):
    return tgt.at[idx].add(src)

def _segment_sum(src, seg, n):
    return jax.ops.segment_sum(src, seg, n)
kernel_name = 'mk_gps_d1_gnn_r8_992164'

def setup_inputs(seed: int=0):
    np.random.seed(seed)
    _w = jnp.asarray

    def _rec_inputs():
        import jax
        import jax.numpy as jnp
        _gk = jax.random.key(seed)
        x = -0.0002117 + 1 * jax.random.normal(jax.random.fold_in(_gk, 1), (6250, 512), jnp.float32)
        src = jax.random.randint(jax.random.fold_in(_gk, 2), (100000,), 0, 6250, jnp.int32)
        dst = jnp.minimum((6250 * jax.random.uniform(jax.random.fold_in(_gk, 3), (100000,)) ** 2.0).astype(jnp.int32), 49999)
        _o = jnp.argsort(dst, stable=True)
        src = src[_o]
        dst = dst[_o]
        return (x, src, dst)
    x, src, dst = _rec_inputs()

    def _L0_gnn_setup():
        import jax, jax.numpy as jnp
        import numpy as np
        N = 6250
        E = 50000
        IN_FEATS = 512
        HEADS = 8
        OUT_FEATS = 64
        NEG_SLOPE = 0.2
        key = jax.random.key(seed)
        ks = jax.random.split(key, 12)
        HF = HEADS * OUT_FEATS
        s = 1.0 / np.sqrt(IN_FEATS)
        inp = {'feat': jax.random.normal(ks[0], (N, IN_FEATS), dtype=jnp.float32), 'src': jax.random.randint(ks[1], (E,), 0, N, dtype=jnp.int32), 'dst': jax.random.randint(ks[2], (E,), 0, N, dtype=jnp.int32), 'W_src': jax.random.normal(ks[3], (IN_FEATS, HF), dtype=jnp.float32) * s, 'b_src': jax.random.normal(ks[4], (HF,), dtype=jnp.float32) * 0.01, 'W_dst': jax.random.normal(ks[5], (IN_FEATS, HF), dtype=jnp.float32) * s, 'b_dst': jax.random.normal(ks[6], (HF,), dtype=jnp.float32) * 0.01, 'W_val': jax.random.normal(ks[7], (IN_FEATS, HF), dtype=jnp.float32) * s, 'b_val': jax.random.normal(ks[8], (HF,), dtype=jnp.float32) * 0.01, 'attn_l': jax.random.normal(ks[9], (HEADS, OUT_FEATS), dtype=jnp.float32) * 0.1, 'attn_r': jax.random.normal(ks[10], (HEADS, OUT_FEATS), dtype=jnp.float32) * 0.1}
        return inp
    _L0_gnn_all = _L0_gnn_setup()
    _L0_gnn_in = {k: v for k, v in _L0_gnn_all.items() if k in ('W_src', 'b_src', 'W_dst', 'b_dst', 'W_val', 'b_val', 'attn_l', 'attn_r')}
    del _L0_gnn_all

    def _L0_mix_setup():
        import jax, jax.numpy as jnp
        import numpy as np
        import math
        E = 512
        H = 8
        D = E // H
        M = 64
        EPS = 1e-08
        CLAMP_MAX = 50.0

        def _make_omega(key):
            w = jax.random.normal(key, (D, M), dtype=jnp.float32) / np.sqrt(D)
            q, _ = jnp.linalg.qr(w)
            return q

        def _positive_random_feature_map(v, omega):
            f = jnp.minimum(v @ omega, CLAMP_MAX)
            l2 = jnp.maximum(jnp.linalg.norm(v, axis=-1, keepdims=True), EPS)
            norm_term = jnp.maximum(jnp.exp(-0.5 * l2 * l2), EPS)
            return norm_term * jnp.exp(f)
        key = jax.random.key(seed)
        ks = jax.random.split(key, 8)
        B, S = (2, 2048)
        x = jax.random.normal(ks[0], (B, S, E), dtype=jnp.float32)
        sc = 1.0 / np.sqrt(E)
        Wq = jax.random.normal(ks[1], (E, E), dtype=jnp.float32) * sc
        Wk = jax.random.normal(ks[2], (E, E), dtype=jnp.float32) * sc
        Wv = jax.random.normal(ks[3], (E, E), dtype=jnp.float32) * sc
        Wo = jax.random.normal(ks[4], (E, E), dtype=jnp.float32) * sc
        omega_q = _make_omega(ks[5])
        omega_k = _make_omega(ks[6])
        return {'x': x, 'Wq': Wq, 'Wk': Wk, 'Wv': Wv, 'Wo': Wo, 'omega_q': omega_q, 'omega_k': omega_k}
    _L0_mix_all = _L0_mix_setup()
    _L0_mix_in = {k: v for k, v in _L0_mix_all.items() if k in ('Wq', 'Wk', 'Wv', 'Wo', 'omega_q', 'omega_k')}
    del _L0_mix_all

    def _L0_ffn_setup():
        import math
        import jax, jax.numpy as jnp
        import numpy as np
        B, T, H, E, K, F = (4, 512, 512, 8, 2, 256)
        CAP_FACTOR, ROUND_TO = (0.3125, 128)

        def _capacity(num_tokens):
            cap = math.ceil(CAP_FACTOR * num_tokens)
            cap = ROUND_TO * math.ceil(cap / ROUND_TO)
            return max(1, min(cap, num_tokens))
        key = jax.random.key(seed)
        k0, k1, k2, k3 = jax.random.split(key, 4)
        x = jax.random.normal(k0, (B, T, H), jnp.float32)
        router_w = jax.random.normal(k1, (H, E), jnp.float32) * 0.02
        w1 = jax.random.normal(k2, (E, H, F), jnp.float32) * (1.0 / np.sqrt(H))
        b1 = jnp.zeros((E, F), jnp.float32)
        w2 = jax.random.normal(k3, (E, F, H), jnp.float32) * (1.0 / np.sqrt(F))
        b2 = jnp.zeros((E, H), jnp.float32)
        return {'x': x, 'router_w': router_w, 'w1': w1, 'b1': b1, 'w2': w2, 'b2': b2}
    _L0_ffn_all = _L0_ffn_setup()
    _L0_ffn_in = {k: v for k, v in _L0_ffn_all.items() if k in ('router_w', 'w1', 'b1', 'w2', 'b2')}
    del _L0_ffn_all
    return {'x': x, 'src': src, 'dst': dst, 'L0_gnn_W_src': _L0_gnn_in['W_src'], 'L0_gnn_b_src': _L0_gnn_in['b_src'], 'L0_gnn_W_dst': _L0_gnn_in['W_dst'], 'L0_gnn_b_dst': _L0_gnn_in['b_dst'], 'L0_gnn_W_val': _L0_gnn_in['W_val'], 'L0_gnn_b_val': _L0_gnn_in['b_val'], 'L0_gnn_attn_l': _L0_gnn_in['attn_l'], 'L0_gnn_attn_r': _L0_gnn_in['attn_r'], 'L0_mix_Wq': _L0_mix_in['Wq'], 'L0_mix_Wk': _L0_mix_in['Wk'], 'L0_mix_Wv': _L0_mix_in['Wv'], 'L0_mix_Wo': _L0_mix_in['Wo'], 'L0_mix_omega_q': _L0_mix_in['omega_q'], 'L0_mix_omega_k': _L0_mix_in['omega_k'], 'L0_ffn_router_w': _L0_ffn_in['router_w'], 'L0_ffn_w1': _L0_ffn_in['w1'], 'L0_ffn_b1': _L0_ffn_in['b1'], 'L0_ffn_w2': _L0_ffn_in['w2'], 'L0_ffn_b2': _L0_ffn_in['b2']}

def reference(x, src, dst, L0_gnn_W_src, L0_gnn_b_src, L0_gnn_W_dst, L0_gnn_b_dst, L0_gnn_W_val, L0_gnn_b_val, L0_gnn_attn_l, L0_gnn_attn_r, L0_mix_Wq, L0_mix_Wk, L0_mix_Wv, L0_mix_Wo, L0_mix_omega_q, L0_mix_omega_k, L0_ffn_router_w, L0_ffn_w1, L0_ffn_b1, L0_ffn_w2, L0_ffn_b2):
    import jax
    import jax.numpy as jnp

    def _L0_gnn_ref(feat, src, dst, W_src, b_src, W_dst, b_dst, W_val, b_val, attn_l, attn_r):
        import jax, jax.numpy as jnp
        import numpy as np
        N = 6250
        E = 50000
        IN_FEATS = 512
        HEADS = 8
        OUT_FEATS = 64
        NEG_SLOPE = 0.2
        feat_src = (feat @ W_src + b_src).reshape(N, HEADS, OUT_FEATS)
        feat_dst = (feat @ W_dst + b_dst).reshape(N, HEADS, OUT_FEATS)
        feat_v = (feat @ W_val + b_val).reshape(N, HEADS, OUT_FEATS)
        el = jnp.einsum('nhf,hf->nh', feat_src, attn_l)
        er = jnp.einsum('nhf,hf->nh', feat_dst, attn_r)
        e = el[src] + er[dst]
        e = jnp.where(e >= 0, e, NEG_SLOPE * e)
        e_max = jax.ops.segment_max(e, dst, num_segments=N)
        e_max = jnp.where(jnp.isfinite(e_max), e_max, 0.0)
        exp_e = jnp.exp(e - e_max[dst])
        denom = jax.ops.segment_sum(exp_e, dst, num_segments=N)
        a = exp_e / jnp.maximum(denom[dst], 1e-16)
        msg = feat_v[src] * a[:, :, None]
        rst = jax.ops.segment_sum(msg, dst, num_segments=N)
        return rst.reshape(N, HEADS * OUT_FEATS)

    def _L0_mix_ref(x, Wq, Wk, Wv, Wo, omega_q, omega_k):
        import jax, jax.numpy as jnp
        import numpy as np
        import math
        E = 512
        H = 8
        D = E // H
        M = 64
        EPS = 1e-08
        CLAMP_MAX = 50.0

        def _make_omega(key):
            w = jax.random.normal(key, (D, M), dtype=jnp.float32) / np.sqrt(D)
            q, _ = jnp.linalg.qr(w)
            return q

        def _positive_random_feature_map(v, omega):
            f = jnp.minimum(v @ omega, CLAMP_MAX)
            l2 = jnp.maximum(jnp.linalg.norm(v, axis=-1, keepdims=True), EPS)
            norm_term = jnp.maximum(jnp.exp(-0.5 * l2 * l2), EPS)
            return norm_term * jnp.exp(f)
        B, S, _ = x.shape
        scale = 1.0 / np.sqrt(D)

        def heads(y):
            return y.reshape(B, S, H, D).transpose(0, 2, 1, 3)
        Q = heads(x @ Wq) * scale
        K = heads(x @ Wk) * scale
        V = heads(x @ Wv)
        Q_phi = _positive_random_feature_map(Q, omega_q)
        K_phi = _positive_random_feature_map(K, omega_k)
        KV = jnp.einsum('bhsm,bhsd->bhmd', K_phi, V)
        QKV = jnp.einsum('bhsm,bhmd->bhsd', Q_phi, KV)
        K_ones = K_phi.sum(axis=2)
        QK_ones = jnp.einsum('bhsm,bhm->bhs', Q_phi, K_ones)
        attn = QKV / QK_ones[..., None]
        out = attn.transpose(0, 2, 1, 3).reshape(B, S, E)
        return out @ Wo

    def _L0_ffn_ref(x, router_w, w1, b1, w2, b2):
        import math
        import jax, jax.numpy as jnp
        import numpy as np
        B, T, H, E, K, F = (4, 512, 512, 8, 2, 256)
        CAP_FACTOR, ROUND_TO = (0.3125, 128)

        def _capacity(num_tokens):
            cap = math.ceil(CAP_FACTOR * num_tokens)
            cap = ROUND_TO * math.ceil(cap / ROUND_TO)
            return max(1, min(cap, num_tokens))
        Bc, Tc, Hc = x.shape
        n = Bc * Tc
        cap = _capacity(n)
        flat = x.reshape(n, Hc)
        logits = (flat @ router_w).astype(jnp.float32)
        sel_logits, expert_idx = jax.lax.top_k(logits, K)
        weights = jax.nn.softmax(sel_logits, axis=-1)
        fe = expert_idx.reshape(-1).astype(jnp.int32)
        fw = weights.reshape(-1)
        tok = jnp.broadcast_to(jnp.arange(n, dtype=jnp.int32)[:, None], expert_idx.shape).reshape(-1)
        order = jnp.argsort(fe)
        se, st, sw = (fe[order], tok[order], fw[order])
        counts = jnp.bincount(se, length=E)
        offsets = (jnp.cumsum(counts) - counts).astype(jnp.int32)
        slot = jnp.arange(se.shape[0], dtype=jnp.int32) - offsets[se]
        keep = slot < cap
        sw = jnp.where(keep, sw, 0.0)
        sx = flat[st]
        expert_inputs = jnp.zeros((E, cap, Hc), flat.dtype).at[se, slot].set(sx, mode='drop')
        h = jax.nn.gelu(jnp.einsum('ech,ehf->ecf', expert_inputs, w1) + b1[:, None, :])
        out = jnp.einsum('ecf,efh->ech', h, w2) + b2[:, None, :]
        clipped = jnp.minimum(counts, cap)
        valid = (jnp.arange(cap, dtype=jnp.int32)[None, :] < clipped[:, None])[..., None]
        out = jnp.where(valid, out, 0)
        slot_c = jnp.minimum(slot, cap - 1)
        gathered = out[se, slot_c] * sw[:, None].astype(out.dtype)
        combined = jnp.zeros((n, Hc), out.dtype).at[st].add(gathered)
        return combined.reshape(Bc, Tc, Hc)
    xn = _layernorm(x, axis=-1)
    x = x + _L0_gnn_ref(xn, src, dst, L0_gnn_W_src, L0_gnn_b_src, L0_gnn_W_dst, L0_gnn_b_dst, L0_gnn_W_val, L0_gnn_b_val, L0_gnn_attn_l, L0_gnn_attn_r) + _L0_mix_ref(xn[None], L0_mix_Wq, L0_mix_Wk, L0_mix_Wv, L0_mix_Wo, L0_mix_omega_q, L0_mix_omega_k)[0]
    x = x + _L0_ffn_ref(_layernorm(x, axis=-1)[None], L0_ffn_router_w, L0_ffn_w1, L0_ffn_b1, L0_ffn_w2, L0_ffn_b2)[0]
    return x

_drawn_inputs = setup_inputs


def setup_inputs(seed=0):
    import zlib

    import numpy as np

    out = dict(_drawn_inputs(seed))
    spreads = {'L0_ffn_b1': (0.0, 0.1), 'L0_ffn_b2': (0.0, 0.1)}
    factors = {'L0_gnn_b_src': 24.001,
     'L0_gnn_b_dst': 23.591,
     'L0_mix_Wq': 8.0,
     'L0_mix_Wk': 4.902,
     'L0_mix_omega_q': 8.0,
     'L0_mix_omega_k': 8.0}
    for name, (base, spread) in spreads.items():
        noise = np.random.default_rng([zlib.crc32(name.encode()), seed]).standard_normal(out[name].shape)
        drawn = base * np.exp(spread * noise) if base else spread * noise
        out[name] = jnp.asarray(drawn.astype(out[name].dtype))
    for name, factor in factors.items():
        out[name] = (out[name] * factor).astype(out[name].dtype)
    return out
```

```python
import math
from contextlib import ExitStack

import concourse.bass as bass
from concourse import mybir

F32 = mybir.dt.float32
I32 = mybir.dt.int32
U32 = mybir.dt.uint32
ALU = mybir.AluOpType
ACT = mybir.ActivationFunctionType
AX = mybir.AxisListType

N, D, H, HF = 6250, 512, 8, 64
P = 128
KC = D // P
TM = 7
NT = -(-N // P)
NM = NT // TM
NP = NT * P
MW = TM * P
HW = MW // 2
assert NM * TM == NT and NM % 2
E = 100000
GT = 4
GE = GT * P
BT = 16
BG = BT // GT
NG = -(-E // (2 * BT * P)) * 2 * BG
ET = NG * GT
EP = ET * P
GH = NG // 2
assert GH <= P
VW = D + H
AW = D + 2 * H
XW = 2 * H + 1
BIG = float(1 << 20)
LOW = -1.0e30
LN_EPS = 1e-5
SLOPE = 0.2
CLAMP = 50.0
FLOOR = 1e-8
NORM_TOP, NORM_LOW = -0.5 * FLOOR ** 2, math.log(FLOOR)
DEN_LOW = 1e-16
EX, FF = 8, 256
FC = FF // P
CAP = min(N, P * math.ceil(math.ceil(0.3125 * N) / P))
SW = 512
ST = SW // P
assert CAP % (2 * SW) == 0 and NT * EX <= 512


def fixed(ctx, nc, name, shape, dt=F32):
    return ctx.enter_context(nc.sbuf_tensor(name, list(shape), dt))


def psum(ctx, nc, name, cols=512):
    return ctx.enter_context(nc.psum_tensor(name, [P, cols], F32))


def sems(ctx, nc, prefix, names):
    taken = [nc.alloc_semaphore(f"{prefix}_{n}") for n in names.split()]
    ctx.taken += taken
    return taken


class Stage(ExitStack):

    def __init__(self, nc):
        super().__init__()
        self.taken = []

        def give_back():
            nc.clear_and_free_semaphores(self.taken)
            nc.all_engine_barrier()
        self.callback(give_back)


def bc(ap, shape):
    return ap.to_broadcast(list(shape))


def hold(eng, passed):
    eng.sem_inc(passed, 1)


def over_macros(eng, body):
    with eng.Fori(0, NM // 2) as i:
        body(i * 2, 0, i)
        body(i * 2 + 1, 1, i)
    body(NM - 1, 0, NM // 2)


def prep_weights(nc, C, dram):
    with Stage(nc) as ctx:
        wsrc = fixed(ctx, nc, "pw_wsrc", [P, KC, D])
        wdst = fixed(ctx, nc, "pw_wdst", [P, KC, D])
        rows = fixed(ctx, nc, "pw_rows", [P, 4, D])
        prod = fixed(ctx, nc, "pw_prod", [P, 2, D])
        loaded, wv_loaded, zeroed, const, mult, folded, paired = sems(
            ctx, nc, "pw", "loaded wv zeroed const mult folded paired")
        block = ctx.enter_context(nc.Block())

        @block.sync
        def _(sp):
            sp.dma_start(wsrc[:, :, :], dram["W_src"].rearrange("(k p) n -> p k n", p=P)).then_inc(loaded, 16)
            sp.dma_start(wdst[:, :, :], dram["W_dst"].rearrange("(k p) n -> p k n", p=P)).then_inc(loaded, 16)
            for r, name in enumerate(("attn_l", "attn_r", "b_src", "b_dst")):
                sp.dma_start(rows[:, r, :], dram[name].partition_broadcast(P)).then_inc(loaded, 16)
            for k in range(KC):
                sp.dma_start(C["wval"][:, k, 0:D], dram["W_val"][k * P:(k + 1) * P, :]).then_inc(wv_loaded, 16)
            sp.dma_start(C["vbias"][:, 0:D], dram["b_val"].partition_broadcast(P)).then_inc(wv_loaded, 16)
            sp.wait_ge(wv_loaded, 16 * (KC + 1))

        @block.gpsimd
        def _(pool):
            pool.memset(C["ident"][:, :], 0.0).then_inc(zeroed, 1)
            pool.memset(C["before"][:, :], 1.0).then_inc(zeroed, 1)
            pool.memset(C["ones"][:, :], 1.0)
            pool.iota(C["cols"][:, :], [[1, P]], base=0, channel_multiplier=0,
                      allow_small_or_imprecise_dtypes=True).then_inc(const, 1)
            pool.memset(C["after"][:, :], 1.0).then_inc(zeroed, 1)
            pool.wait_ge(zeroed, 3)
            pool.affine_select(out=C["ident"][:, :], in_=C["ident"][:, :], compare_op=ALU.not_equal, fill=1.0,
                               base=0, pattern=[[-1, P]], channel_multiplier=1).then_inc(const, 1)
            pool.affine_select(out=C["before"][:, :], in_=C["before"][:, :], compare_op=ALU.is_gt, fill=0.0,
                               base=0, pattern=[[1, P]], channel_multiplier=-1).then_inc(const, 1)
            pool.affine_select(out=C["after"][:, :], in_=C["after"][:, :], compare_op=ALU.is_gt, fill=0.0,
                               base=0, pattern=[[-1, P]], channel_multiplier=1).then_inc(const, 1)
            pool.memset(C["valid"][:, :], 1.0).then_inc(zeroed, 1)
            pool.wait_ge(zeroed, 4)
            pool.affine_select(out=C["valid"][:, :], in_=C["valid"][:, :], compare_op=ALU.is_gt, fill=0.0,
                               base=N, pattern=[[-P, NT]], channel_multiplier=-1).then_inc(const, 1)
            pool.wait_ge(const, 5)

        @block.vector
        def _(dve):
            nc.vector.memset(C["pair"][:, :], 0.0).then_inc(paired, 1)
            dve.wait_ge(paired, 1)
            nc.vector.memset(C["pair"][0:HF, 0:HF], 1.0)
            nc.vector.memset(C["pair"][HF:P, HF:P], 1.0).then_inc(paired, 1)
            dve.wait_ge(loaded, 6 * 16)
            done = 0
            for k in range(KC):
                for s, w in enumerate((wsrc, wdst)):
                    if done >= 2:
                        dve.wait_ge(folded, done - 1)
                    nc.vector.tensor_tensor(prod[:, s, :], w[:, k, :], rows[:, s, :], ALU.mult).then_inc(mult, 1)
                    dve.wait_ge(mult, done + 1)
                    nc.vector.tensor_reduce(C["wval"][:, k, D + s * H:D + (s + 1) * H],
                                            prod[:, s, :].rearrange("p (h f) -> p h f", f=HF), AX.X, ALU.add).then_inc(folded, 1)
                    done += 1
            for s in range(2):
                dve.wait_ge(folded, done - 1)
                nc.vector.tensor_tensor(prod[:, s, :], rows[:, 2 + s, :], rows[:, s, :], ALU.mult).then_inc(mult, 1)
                dve.wait_ge(mult, done + 1)
                nc.vector.tensor_reduce(C["vbias"][:, D + s * H:D + (s + 1) * H],
                                        prod[:, s, :].rearrange("p (h f) -> p h f", f=HF), AX.X, ALU.add).then_inc(folded, 1)
                done += 1
            dve.wait_ge(folded, done)
            dve.wait_ge(paired, 2)


def norm_stats(nc, C, dram, source, out_stats, prefix):
    with Stage(nc) as ctx:
        xs = fixed(ctx, nc, prefix + "_x", [P, TM, D])
        st = fixed(ctx, nc, prefix + "_st", [P, NT, 6])
        loaded = sems(ctx, nc, prefix, " ".join(f"ld{j}" for j in range(TM)))
        read, stats, aggr = sems(ctx, nc, prefix, "read stats aggr")
        block = ctx.enter_context(nc.Block())
        rows = source.rearrange("(n p) d -> n p d", p=P)

        @block.sync
        def _(sp):
            with sp.Fori(0, NM) as m:
                for j in range(TM):
                    sp.wait_ge(read, m * TM + j + 1)
                    sp.dma_start(xs[:, j, :], rows[m * TM + j]).then_inc(loaded[j], 16)

        @block.vector
        def _(dve):
            dve.sem_inc(read, TM)
            with dve.Fori(0, NM) as m:
                for j in range(TM):
                    dve.wait_ge(loaded[j], m * 16 + 16)
                    nc.vector.bn_stats(st[:, m * TM + j, :], xs[:, j, :]).then_inc(read, 1)
            dve.wait_ge(read, NT + TM)
            for n in range(NT):
                ins = nc.vector.bn_aggr(out_stats[:, n, :], st[:, n, :])
            ins.then_inc(stats, 1)
            dve.wait_ge(stats, 1)
            nc.vector.tensor_scalar(out_stats[:, :, 1], out_stats[:, :, 1], LN_EPS, None, ALU.add).then_inc(aggr, 1)
            dve.wait_ge(aggr, 2)
            nc.vector.reciprocal(out_stats[:, :, 1], out_stats[:, :, 1]).then_inc(aggr, 1)
            dve.wait_ge(aggr, 3)

        @block.scalar
        def _(act):
            act.wait_ge(aggr, 1)
            nc.scalar.activation(out_stats[:, :, 1], out_stats[:, :, 1], ACT.Sqrt).then_inc(aggr, 1)



def project_nodes(nc, C, dram):
    with Stage(nc) as ctx:
        xs = fixed(ctx, nc, "pn_x", [P, TM, D])
        xT = fixed(ctx, nc, "pn_xT", [P, TM, KC, P])
        vr = fixed(ctx, nc, "pn_v", [P, TM, D + 2 * H])
        pT = [psum(ctx, nc, f"pn_pT{i}") for i in range(2)]
        pV = [psum(ctx, nc, f"pn_pV{i}") for i in range(2)]
        pE = [psum(ctx, nc, f"pn_pE{i}") for i in range(2)]
        x_loaded = sems(ctx, nc, "pn", " ".join(f"ld{j}" for j in range(TM)))
        t_stored = sems(ctx, nc, "pn", " ".join(f"ts{j}" for j in range(TM)))
        v_stored = sems(ctx, nc, "pn", " ".join(f"vs{j}" for j in range(TM)))
        normed, turned, kept, projected, biased = sems(ctx, nc, "pn", "normed turned kept projected biased")
        block = ctx.enter_context(nc.Block())
        rows = dram["x"].rearrange("(n p) d -> n p d", p=P)
        v_rows = dram["vtab"].rearrange("(n p) w -> n p w", p=P)
        er_rows = dram["ertab"].rearrange("(n p) w -> n p w", p=P)

        @block.sync
        def _(sp):
            def macro(m, q, u):
                for j in range(TM):
                    n = m * TM + j
                    sp.wait_ge(turned, n + 1)
                    sp.dma_start(xs[:, j, :], rows[n]).then_inc(x_loaded[j], 16)
            over_macros(sp, macro)

        @block.gpsimd
        def _(pool):
            def macro(m, q, u):
                for j in range(TM):
                    n = m * TM + j
                    pool.wait_ge(kept, n + 1 + 2)
                    pool.dma_start(dram["xnT"][m, :, :, j * P:(j + 1) * P], xT[:, j, :, :]).then_inc(t_stored[j], 16)
                    pool.wait_ge(biased, n + 1 + 2)
                    pool.dma_start(v_rows[n], vr[:, j, 0:VW]).then_inc(v_stored[j], 16)
                    pool.dma_start(er_rows[n], vr[:, j, VW:VW + H]).then_inc(v_stored[j], 16)
            over_macros(pool, macro)
            for j in range(TM):
                pool.wait_ge(t_stored[j], 16 * NM)
                pool.wait_ge(v_stored[j], 32 * NM)

        @block.scalar
        def _(act):
            act.sem_inc(kept, 2)

            def macro(m, q, u):
                for j in range(TM):
                    n = m * TM + j
                    act.wait_ge(turned, n + 1 + TM)
                    act.wait_ge(projected, n + 1)
                    act.wait_ge(t_stored[j], m * 16)
                    nc.scalar.activation(xT[:, j, :, :].rearrange("p k t -> p (k t)"),
                                         pT[(q + j) % 2][:, :], ACT.Copy).then_inc(kept, 1)
            over_macros(act, macro)

        @block.vector
        def _(dve):
            dve.sem_inc(biased, 2)

            def norm(m, j):
                n = m * TM + j
                dve.wait_ge(x_loaded[j], m * 16 + 16)
                nc.vector.tensor_scalar(xs[:, j, :], xs[:, j, :], C["stats1"][:, n, 0:1], C["stats1"][:, n, 1:2],
                                        ALU.subtract, ALU.mult).then_inc(normed, 1)

            def macro(m, q, u):
                norm(m, 0)
                for j in range(TM):
                    n = m * TM + j
                    if j + 1 < TM:
                        norm(m, j + 1)
                    s = (q + j) % 2
                    dve.wait_ge(projected, n + 1 + TM)
                    dve.wait_ge(v_stored[j], m * 32)
                    nc.vector.tensor_tensor(vr[:, j, 0:D], pV[s][:, :], C["vbias"][:, 0:D], ALU.add)
                    nc.vector.tensor_tensor(vr[:, j, D:D + 2 * H], pE[s][:, 0:2 * H], C["vbias"][:, D:D + 2 * H],
                                            ALU.add).then_inc(biased, 1)
            over_macros(dve, macro)

        @block.tensor
        def _(pe):
            pe.sem_inc(turned, TM)
            pe.sem_inc(projected, TM)

            def turn(m, q, j):
                n = m * TM + j
                pe.wait_ge(normed, n + 1)
                pe.wait_ge(kept, n + 1)
                for k in range(KC):
                    last = nc.tensor.transpose(pT[(q + j) % 2][:, k * P:(k + 1) * P], xs[:, j, k * P:(k + 1) * P],
                                               C["ident"][:, :])
                last.then_inc(turned, 1)

            def macro(m, q, u):
                turn(m, q, 0)
                for j in range(TM):
                    n = m * TM + j
                    if j + 1 < TM:
                        turn(m, q, j + 1)
                    s = (q + j) % 2
                    pe.wait_ge(kept, n + 1 + 2)
                    pe.wait_ge(biased, n + 1)
                    for k in range(KC):
                        nc.tensor.matmul(pV[s][:, :], xT[:, j, k, :], C["wval"][:, k, 0:D],
                                         start=(k == 0), stop=(k == KC - 1))
                    for k in range(KC):
                        last = nc.tensor.matmul(pE[s][:, 0:2 * H], xT[:, j, k, :], C["wval"][:, k, D:D + 2 * H],
                                                start=(k == 0), stop=(k == KC - 1))
                    last.then_inc(projected, 1)
            over_macros(pe, macro)


def prep_edges(nc, C, dram):
    with Stage(nc) as ctx:
        ints = fixed(ctx, nc, "pe_ints", [GH, 2, 2, GE], I32)
        dst = fixed(ctx, nc, "pe_dst", [GH, 2, GE])
        bef = fixed(ctx, nc, "pe_bef", [GH, 2, GE])
        first = fixed(ctx, nc, "pe_first", [GH, 2, GE + 1])
        pen = fixed(ctx, nc, "pe_pen", [GH, 2, GE + 1])
        rank = fixed(ctx, nc, "pe_rank", [GH, 2, GE])
        zero = fixed(ctx, nc, "pe_zero", [GH, GE])
        tgt = fixed(ctx, nc, "pe_tgt", [GH, 2, GE])
        cont = fixed(ctx, nc, "pe_cont", [GH, 2, 3])
        row = fixed(ctx, nc, "pe_row", [GH, 2])
        blank = fixed(ctx, nc, "pe_blank", [P, AW])
        pt = [psum(ctx, nc, f"pe_pt{i}") for i in range(2)]
        loaded, rows_made, step, turned, kept, pen_stored, blanks, blanked = sems(
            ctx, nc, "pe", "loaded rows step turned kept pens blanks blanked")
        block = ctx.enter_context(nc.Block())
        NS = NP + NG
        whole = NS // P * P

        @block.sync
        def _(sp):
            for a, name in enumerate(("dst", "dst_before")):
                for hf in range(2):
                    sp.dma_start(ints[:, a, hf, :], dram[name].rearrange("(c p e) -> c p e", c=2, p=GH)[hf]).then_inc(loaded, 16)
            sp.wait_ge(blanks, 2)
            sp.dma_start(dram["acc"][0:whole, :].rearrange("(n p) w -> p n w", p=P),
                         bc(blank[:, :].unsqueeze(1), [P, whole // P, AW])).then_inc(blanked, 16)
            sp.dma_start(dram["acc"][whole:NS, :], blank[0:NS - whole, :]).then_inc(blanked, 16)
            sp.wait_ge(step, 6)
            sp.dma_start(dram["pen"].rearrange("(c p) e -> p c e", p=GH), pen[:, :, :]).then_inc(pen_stored, 16)
            sp.wait_ge(pen_stored, 16)
            sp.wait_ge(blanked, 32)

        @block.gpsimd
        def _(pool):
            pool.iota(row[:, :], [[GH, 2]], base=NP, channel_multiplier=1,
                      allow_small_or_imprecise_dtypes=True).then_inc(rows_made, 1)

        @block.vector
        def _(dve):
            nc.vector.memset(blank[:, 0:D + H], 0.0).then_inc(blanks, 1)
            nc.vector.memset(blank[:, D + H:AW], LOW).then_inc(blanks, 1)
            nc.vector.memset(zero[:, :], 0.0)
            dve.wait_ge(loaded, 64)
            nc.vector.tensor_copy(dst[:, :, :], ints[:, 0, :, :])
            nc.vector.tensor_copy(bef[:, :, :], ints[:, 1, :, :]).then_inc(step, 1)
            dve.wait_ge(step, 1)
            nc.vector.tensor_tensor(first[:, :, 0:GE], dst[:, :, :], bef[:, :, :], ALU.not_equal)
            nc.vector.tensor_tensor(cont[:, :, 0], dst[:, :, 0], bef[:, :, 0], ALU.is_equal).then_inc(step, 1)
            dve.wait_ge(step, 2)
            dve.wait_ge(rows_made, 1)
            nc.vector.memset(first[:, :, 0:1], 1.0)
            nc.vector.memset(first[:, :, GE:GE + 1], 1.0)
            nc.vector.tensor_tensor(cont[:, :, 1], row[:, :], dst[:, :, 0], ALU.subtract).then_inc(step, 1)
            dve.wait_ge(step, 3)
            for hf in range(2):
                nc.vector.tensor_tensor_scan(rank[:, hf, :], first[:, hf, 0:GE], zero[:, :], -1.0, ALU.add, ALU.max)
            nc.vector.tensor_tensor(cont[:, :, 1], cont[:, :, 1], cont[:, :, 0], ALU.mult).then_inc(step, 1)
            dve.wait_ge(step, 4)
            nc.vector.tensor_scalar(tgt[:, :, :], dst[:, :, :], -BIG, None, ALU.add).then_inc(step, 1)
            dve.wait_ge(step, 5)
            nc.vector.tensor_scalar(pen[:, :, :], first[:, :, :], LOW, None, ALU.mult).then_inc(step, 1)
            nc.vector.tensor_tensor(cont[:, :, 2], tgt[:, :, 0], cont[:, :, 0], ALU.mult).then_inc(step, 1)
            dve.wait_ge(step, 7)
            nc.vector.tensor_scalar(C["own"][:, :], cont[:, :, 2], BIG, None, ALU.add).then_inc(step, 1)
            nc.vector.tensor_tensor(tgt[:, :, 0], tgt[:, :, 0], cont[:, :, 1], ALU.add).then_inc(step, 1)
            dve.wait_ge(step, 9)
            nc.vector.tensor_tensor(tgt[:, :, :], tgt[:, :, :], first[:, :, 0:GE], ALU.mult).then_inc(step, 1)
            for t in range(4):
                hf, a = divmod(t, 2)
                dve.wait_ge(turned, t + 1)
                out = (C["rank"], C["target"])[a]
                nc.vector.tensor_copy(out[:, hf * GH * GT:(hf + 1) * GH * GT].rearrange("q (p s) -> q s p", s=GT),
                                      pt[t % 2][:, 0:GT * GH].rearrange("q (s p) -> q s p", s=GT)).then_inc(kept, 1)
            dve.wait_ge(kept, 4)
            nc.vector.tensor_scalar(C["first"][:, :], C["target"][:, :], 0.0, None, ALU.not_equal).then_inc(step, 1)
            dve.wait_ge(step, 11)

        @block.tensor
        def _(pe):
            pe.wait_ge(step, 10)
            for t in range(4):
                hf, a = divmod(t, 2)
                if t >= 2:
                    pe.wait_ge(kept, t - 1)
                for s in range(GT):
                    last = nc.tensor.transpose(pt[t % 2][:, s * GH:(s + 1) * GH], (rank, tgt)[a][:, hf, s * P:(s + 1) * P],
                                               C["ident"][0:GH, 0:GH])
                last.then_inc(turned, 1)


def edge_attention(nc, C, dram):
    with Stage(nc) as ctx:
        GC = BG * H
        ix = fixed(ctx, nc, "ea_ix", [P, 2, 2, BT], I32)
        rows = fixed(ctx, nc, "ea_rows", [P, 2, BT, VW])
        er = fixed(ctx, nc, "ea_er", [P, 2, BT, H])
        z = fixed(ctx, nc, "ea_z", [P, 2, BT * H])
        e = fixed(ctx, nc, "ea_e", [P, 2, BT * H])
        pen = fixed(ctx, nc, "ea_pen", [GC, 2, GE + 1])
        run = fixed(ctx, nc, "ea_run", [GC, 2, GE])
        top = fixed(ctx, nc, "ea_top", [GC, 2, GE])
        wt = fixed(ctx, nc, "ea_wt", [GC, 2, GE])
        ext = fixed(ctx, nc, "ea_ext", [P, 2, BT, XW])
        hot = fixed(ctx, nc, "ea_hot", [P, 2, GT, P])
        sums = fixed(ctx, nc, "ea_sums", [P, BG, AW])
        at = fixed(ctx, nc, "ea_at", [P, BG, 1], I32)
        pz = psum(ctx, nc, "ea_pz")
        pb = psum(ctx, nc, "ea_pb")
        pn = [psum(ctx, nc, f"ea_pn{i}") for i in range(2)]
        px = [psum(ctx, nc, f"ea_px{i}") for i in range(2)]
        ix_loaded = sems(ctx, nc, "ea", "ix0 ix1")
        gathered = sems(ctx, nc, "ea", "ga0 ga1")
        scattered = sems(ctx, nc, "ea", " ".join(f"sc{g}" for g in range(BG)))
        (raw, scored, turned, ran, topped, scanned, weighted, back, extras, scaled, hotted, grouped,
         evacuated) = sems(ctx, nc, "ea", "raw scored turned ran topped scanned weighted back extras scaled hotted "
                                          "grouped evacuated")
        pool_passed, sp_passed, pe_passed = sems(ctx, nc, "ea", "pool_passed sp_passed pe_passed")
        block = ctx.enter_context(nc.Block())
        NB = ET // BT
        GS = 2 * BT * 16

        def pipelined(eng, head, step):
            head(0, 0, 0)
            with eng.Fori(0, NB // 2 - 1) as i:
                step(i * 2, 0, i, True)
                step(i * 2 + 1, 1, i, True)
            step(NB - 2, 0, NB // 2 - 1, True)
            step(NB - 1, 1, NB // 2 - 1, False)

        def after(q, u):
            return (1, u) if q == 0 else (0, u + 1)

        @block.sync
        def _(sp):
            def batch(b, q, u):
                sp.wait_ge(gathered[q], u * GS)
                hold(sp, sp_passed)
                sp.wait_ge(scanned, b + 1)
                hold(sp, sp_passed)
                sp.dma_start(ix[:, q, 0, :], dram["src_em"][b]).then_inc(ix_loaded[q], 16)
                sp.dma_start(ix[:, q, 1, :], dram["dst_em"][b]).then_inc(ix_loaded[q], 16)
                for g in range(BG):
                    sp.dma_start(pen[g * H:(g + 1) * H, q, :],
                                 dram["pen"][b * BG + g, :].partition_broadcast(H)).then_inc(ix_loaded[q], 16)
            with sp.Fori(0, NB // 2) as i:
                batch(i * 2, 0, i)
                batch(i * 2 + 1, 1, i)

        @block.gpsimd
        def _(pool):
            def gather(b, q, u, old):
                pool.wait_ge(ix_loaded[q], u * 96 + 96)
                if old:
                    pool.wait_ge(raw, b - 1)
                hold(pool, pool_passed)
                for t in range(BT):
                    pool.indirect_dma_start(out=er[:, q, t, :], out_offset=None, in_=dram["ertab"],
                                            in_offset=bass.IndirectOffsetOnAxis(ap=ix[:, q, 1, t:t + 1], axis=0)).then_inc(gathered[q], 16)
                for t in range(BT):
                    if old and t % GT == 0:
                        pool.wait_ge(grouped, (b - 2) * BG + t // GT + 1 + 2)
                        hold(pool, pool_passed)
                    pool.indirect_dma_start(out=rows[:, q, t, :], out_offset=None, in_=dram["vtab"],
                                            in_offset=bass.IndirectOffsetOnAxis(ap=ix[:, q, 0, t:t + 1], axis=0)).then_inc(gathered[q], 16)
                    if old and t % GT == GT - 1 and t >= GT:
                        scatter(b - 2, t // GT - 1)
                if old:
                    scatter(b - 2, BG - 1)

            def scatter(b, g):
                pool.wait_ge(evacuated, b * BG + g + 1 + 2)
                hold(pool, pool_passed)
                pool.indirect_dma_start(out=dram["acc"], out_offset=bass.IndirectOffsetOnAxis(ap=at[:, g, 0:1], axis=0),
                                        in_=sums[:, g, :], in_offset=None, bounds_check=NP + NG - 1,
                                        oob_is_err=False).then_inc(scattered[g], 16)
            gather(0, 0, 0, False)
            gather(1, 1, 0, False)
            with pool.Fori(1, NB // 2) as i:
                gather(i * 2, 0, i, True)
                gather(i * 2 + 1, 1, i, True)
            for b in (NB - 2, NB - 1):
                for g in range(BG):
                    scatter(b, g)
            for g in range(BG):
                pool.wait_ge(scattered[g], NB * 16)

        @block.vector
        def _(dve):
            dve.sem_inc(scanned, 2)

            def score(b, q, u):
                dve.wait_ge(gathered[q], u * GS + GS)
                nc.vector.tensor_tensor(z[:, q, :].rearrange("p (s g h) -> p s g h", s=GT, g=BG),
                                        rows[:, q, :, D:VW].rearrange("p (g s) h -> p s g h", s=GT),
                                        er[:, q, :, :].rearrange("p (g s) h -> p s g h", s=GT), ALU.add).then_inc(raw, 1)
                dve.wait_ge(raw, b + 1)
                nc.vector.scalar_tensor_tensor(e[:, q, :], z[:, q, :], SLOPE, z[:, q, :], ALU.mult, ALU.max).then_inc(scored, 1)

            def scan(b, q, u):
                dve.wait_ge(turned, b + 1)
                dve.wait_ge(ix_loaded[q], u * 96 + 96)
                nc.vector.tensor_tensor_scan(run[:, q, :], pen[:, q, 0:GE], pz[0:GC, :], LOW, ALU.add, ALU.max).then_inc(ran, 1)
                dve.wait_ge(ran, b + 1)
                nc.vector.tensor_tensor_scan(top[:, q, ::-1], pen[:, q, GE:0:-1], run[:, q, ::-1], LOW,
                                             ALU.add, ALU.max).then_inc(topped, 1)
                dve.wait_ge(topped, b + 1)
                nc.vector.tensor_tensor(wt[:, q, :], pz[0:GC, :], top[:, q, :], ALU.subtract).then_inc(scanned, 1)

            def extend(b, q):
                dve.wait_ge(back, b + 1)
                nc.vector.tensor_copy(ext[:, q, :, 0:H].rearrange("p (g s) h -> p s g h", s=GT),
                                      pb[:, 0:BT * H].rearrange("p (s g h) -> p s g h", s=GT, g=BG))
                nc.vector.tensor_tensor(ext[:, q, :, H:2 * H].rearrange("p (g s) h -> p s g h", s=GT),
                                        pb[:, BT * H:2 * BT * H].rearrange("p (s g h) -> p s g h", s=GT, g=BG),
                                        bc(C["first"][:, bass.ds(b * BT, BT)].rearrange("p (g s) -> p s g", s=GT).unsqueeze(3),
                                           [P, GT, BG, H]), ALU.mult)
                nc.vector.tensor_copy(ext[:, q, :, 2 * H], C["target"][:, bass.ds(b * BT, BT)]).then_inc(extras, 1)

            def scale(b, q, g):
                n = b * BG + g
                part = rows[:, q, g * GT:(g + 1) * GT, 0:D].rearrange("p s (h f) -> p s h f", f=HF)
                nc.vector.tensor_tensor(part, part, bc(ext[:, q, g * GT:(g + 1) * GT, 0:H].unsqueeze(3), [P, GT, H, HF]),
                                        ALU.mult).then_inc(scaled, 1)
                dve.wait_ge(grouped, n + 1)
                nc.vector.tensor_tensor(hot[:, g % 2, :, :], bc(C["cols"][:, :].unsqueeze(1), [P, GT, P]),
                                        bc(C["rank"][:, bass.ds(n * GT, GT)].unsqueeze(2), [P, GT, P]),
                                        ALU.is_equal).then_inc(hotted, 1)

            def head(b, q, u):
                score(b, q, u)
                scan(b, q, u)
                extend(b, q)

            def step(b, q, u, more):
                nq, nu = after(q, u)
                dve.wait_ge(extras, b + 1)
                scale(b, q, 0)
                if more:
                    score(b + 1, nq, nu)
                scale(b, q, 1)
                if more:
                    scan(b + 1, nq, nu)
                scale(b, q, 2)
                scale(b, q, 3)
                if more:
                    extend(b + 1, nq)
            pipelined(dve, head, step)

        @block.scalar
        def _(act):
            act.sem_inc(evacuated, 2)

            def head(b, q, u):
                act.wait_ge(scanned, b + 1 + 2)
                nc.scalar.activation(wt[:, q, :], wt[:, q, :], ACT.Exp).then_inc(weighted, 1)

            def step(b, q, u, more):
                nq, nu = after(q, u)
                for g in range(BG):
                    n = b * BG + g
                    act.wait_ge(grouped, n + 1 + 2)
                    act.wait_ge(scattered[g], b * 16)
                    nc.scalar.activation(sums[:, g, 0:D], pn[g % 2][:, :], ACT.Copy)
                    nc.scalar.activation(sums[:, g, D:AW], px[g % 2][:, 0:2 * H], ACT.Copy)
                    nc.scalar.activation(at[:, g, :], px[g % 2][:, 2 * H:XW], ACT.Copy, bias=BIG).then_inc(evacuated, 1)
                    if g == 0 and more:
                        head(b + 1, nq, nu)
            pipelined(act, head, step)

        @block.tensor
        def _(pe):
            pe.sem_inc(grouped, 2)

            def forth(b, q):
                pe.wait_ge(scored, b + 1)
                pe.wait_ge(scanned, b + 2)
                for s in range(GT):
                    last = nc.tensor.transpose(pz[0:GC, s * P:(s + 1) * P], e[:, q, s * GC:(s + 1) * GC], C["ident"][:, :])
                last.then_inc(turned, 1)

            def returned(b, q):
                pe.wait_ge(weighted, b + 1)
                pe.wait_ge(extras, b)
                hold(pe, pe_passed)
                for a, src in enumerate((wt, top)):
                    for s in range(GT):
                        last = nc.tensor.transpose(pb[:, a * BT * H + s * GC:a * BT * H + (s + 1) * GC],
                                                   src[:, q, s * P:(s + 1) * P], C["ident"][0:GC, 0:GC])
                last.then_inc(back, 1)

            def head(b, q, u):
                forth(b, q)
                returned(b, q)

            def step(b, q, u, more):
                nq, nu = after(q, u)
                for g in range(BG):
                    n = b * BG + g
                    pe.wait_ge(scaled, n + 1)
                    pe.wait_ge(hotted, n + 1)
                    pe.wait_ge(evacuated, n + 1)
                    for s in range(GT):
                        t = g * GT + s
                        nc.tensor.matmul(pn[g % 2][:, :], hot[:, g % 2, s, :], rows[:, q, t, 0:D], start=(s == 0), stop=(s == GT - 1))
                        last = nc.tensor.matmul(px[g % 2][:, 0:XW], hot[:, g % 2, s, :], ext[:, q, t, :],
                                                start=(s == 0), stop=(s == GT - 1))
                    last.then_inc(grouped, 1)
                    if g == 0 and more:
                        forth(b + 1, nq)
                    if g == 2 and more:
                        returned(b + 1, nq)
            pipelined(pe, head, step)


def merge_groups(nc, C, dram):
    with Stage(nc) as ctx:
        part = fixed(ctx, nc, "mg_part", [GH, AW])
        own = fixed(ctx, nc, "mg_own", [GH, AW])
        wide = fixed(ctx, nc, "mg_wide", [GH, H + 1, GH])
        same = fixed(ctx, nc, "mg_same", [GH, GH])
        off = fixed(ctx, nc, "mg_off", [GH, GH])
        work = fixed(ctx, nc, "mg_work", [GH, H, GH])
        peak = fixed(ctx, nc, "mg_peak", [GH, 4, H])
        lead = fixed(ctx, nc, "mg_lead", [GH, 4])
        ids = fixed(ctx, nc, "mg_ids", [GH, 2, 1], I32)
        out = fixed(ctx, nc, "mg_out", [GH, AW])
        pt = [psum(ctx, nc, f"mg_pt{i}") for i in range(3)]
        pn = psum(ctx, nc, "mg_pn")
        px = psum(ctx, nc, "mg_px")
        loaded, fetched, stored, v, t, s, m = sems(ctx, nc, "mg", "loaded fetched stored v t s m")
        block = ctx.enter_context(nc.Block())

        V = 13

        @block.sync
        def _(sp):
            for hf in range(2):
                if hf:
                    sp.wait_ge(v, V)
                sp.dma_start(part[:, :], dram["acc"][NP + hf * GH:NP + (hf + 1) * GH, :]).then_inc(loaded, 16)

        @block.gpsimd
        def _(pool):
            for hf in range(2):
                pool.wait_ge(v, V * hf + 1)
                pool.indirect_dma_start(out=own[:, :], out_offset=None, in_=dram["acc"],
                                        in_offset=bass.IndirectOffsetOnAxis(ap=ids[:, 0, :], axis=0),
                                        bounds_check=NP - 1, oob_is_err=False).then_inc(fetched, 16)
                pool.wait_ge(v, V * (hf + 1))
                pool.indirect_dma_start(out=dram["acc"], out_offset=bass.IndirectOffsetOnAxis(ap=ids[:, 1, :], axis=0),
                                        in_=out[:, :], in_offset=None, bounds_check=NP - 1,
                                        oob_is_err=False).then_inc(stored, 16)
                pool.wait_ge(stored, 16 * (hf + 1))

        @block.scalar
        def _(act):
            for hf in range(2):
                act.wait_ge(v, V * hf + 9)
                nc.scalar.activation(peak[:, 2:4, :], peak[:, 2:4, :], ACT.Exp).then_inc(s, 1)

        @block.vector
        def _(dve):
            done = [0]

            def link(ins):
                done[0] += 1
                ins.then_inc(v, 1)
                dve.wait_ge(v, done[0])

            for hf in range(2):
                if hf:
                    dve.wait_ge(stored, 16)
                nc.vector.tensor_copy(ids[:, 0, :], C["own"][:, hf:hf + 1])
                link(nc.vector.memset(own[:, :], 0.0))
                dve.wait_ge(loaded, 16 * (hf + 1))
                nc.vector.tensor_copy(wide[:, 0:H, :], bc(part[:, D + H:AW].unsqueeze(2), [GH, H, GH]))
                link(nc.vector.tensor_copy(wide[:, H, :], bc(C["own"][:, hf:hf + 1], [GH, GH])))
                dve.wait_ge(t, hf + 1)
                link(nc.vector.tensor_scalar(same[:, :], pt[2][0:GH, 0:GH], C["own"][:, hf:hf + 1], None, ALU.is_equal))
                nc.vector.tensor_scalar(off[:, :], same[:, :], -1.0, -LOW, ALU.add, ALU.mult)
                for b in range(2):
                    last = nc.vector.tensor_tensor(work[:, 4 * b:4 * b + 4, :], pt[b][0:GH, 0:4 * GH].rearrange("p (h c) -> p h c", h=4),
                                                   bc(same[:, :].unsqueeze(1), [GH, 4, GH]), ALU.mult)
                link(last)
                link(nc.vector.tensor_tensor(work[:, :, :], work[:, :, :], bc(off[:, :].unsqueeze(1), [GH, H, GH]), ALU.add))
                link(nc.vector.tensor_reduce(peak[:, 0, :], work[:, :, :], AX.X, ALU.max))
                dve.wait_ge(fetched, 16 * (hf + 1))
                link(nc.vector.tensor_tensor(peak[:, 1, :], peak[:, 0, :], own[:, D + H:AW], ALU.max))
                nc.vector.tensor_tensor(peak[:, 2, :], part[:, D + H:AW], peak[:, 1, :], ALU.subtract)
                nc.vector.tensor_tensor(off[:, :], same[:, :], C["after"][0:GH, 0:GH], ALU.mult)
                link(nc.vector.tensor_copy(out[:, D + H:AW], peak[:, 1, :]))
                nc.vector.tensor_reduce(lead[:, 0:1], off[:, :], AX.X, ALU.add)
                link(nc.vector.tensor_tensor(peak[:, 3, :], own[:, D + H:AW], peak[:, 1, :], ALU.subtract))
                dve.wait_ge(s, hf + 1)
                nc.vector.tensor_tensor(part[:, D:D + H], part[:, D:D + H], peak[:, 2, :], ALU.mult)
                nc.vector.tensor_scalar(lead[:, 1:2], lead[:, 0:1], BIG, None, ALU.mult)
                nc.vector.tensor_tensor(own[:, D:D + H], own[:, D:D + H], peak[:, 3, :], ALU.mult)
                nc.vector.tensor_tensor(own[:, 0:D].rearrange("p (h f) -> p h f", f=HF), own[:, 0:D].rearrange("p (h f) -> p h f", f=HF),
                                        bc(peak[:, 3, :].unsqueeze(2), [GH, H, HF]), ALU.mult)
                link(nc.vector.tensor_tensor(part[:, 0:D].rearrange("p (h f) -> p h f", f=HF), part[:, 0:D].rearrange("p (h f) -> p h f", f=HF),
                                             bc(peak[:, 2, :].unsqueeze(2), [GH, H, HF]), ALU.mult))
                link(nc.vector.tensor_tensor(lead[:, 2:3], lead[:, 1:2], C["own"][:, hf:hf + 1], ALU.add))
                dve.wait_ge(m, hf + 1)
                nc.vector.tensor_copy(ids[:, 1, :], lead[:, 2:3])
                nc.vector.tensor_tensor(out[:, D:D + H], px[0:GH, 0:H], own[:, D:D + H], ALU.add)
                link(nc.vector.tensor_tensor(out[:, 0:D], pn[0:GH, :], own[:, 0:D], ALU.add))
                link(nc.vector.memset(lead[:, 3:4], 0.0))
            assert done[0] == 2 * V

        @block.tensor
        def _(pe):
            for hf in range(2):
                pe.wait_ge(v, V * hf + 2)
                for h in range(H + 1):
                    last = nc.tensor.transpose(pt[h // 4][0:GH, (h % 4) * GH:(h % 4 + 1) * GH], wide[:, h, :], C["ident"][0:GH, 0:GH])
                last.then_inc(t, 1)
                pe.wait_ge(v, V * hf + 10)
                nc.tensor.matmul(pn[0:GH, :], same[:, :], part[:, 0:D], start=True, stop=True)
                nc.tensor.matmul(px[0:GH, 0:H], same[:, :], part[:, D:D + H], start=True, stop=True).then_inc(m, 1)


def load_feature_maps(nc, sp, tile, omega, loaded):
    sp.dma_start(tile[0:HF, 0:HF], omega).then_inc(loaded, 16)
    sp.dma_start(tile[HF:P, HF:P], omega).then_inc(loaded, 16)


def key_sums(nc, C, dram):
    with Stage(nc) as ctx:
        xT = fixed(ctx, nc, "ks_xT", [P, 2, KC, MW])
        wk = fixed(ctx, nc, "ks_wk", [P, KC, D])
        wv = fixed(ctx, nc, "ks_wv", [P, KC, D])
        omega = fixed(ctx, nc, "ks_omega", [P, P])
        half = fixed(ctx, nc, "ks_half", [P, 2])
        kT = fixed(ctx, nc, "ks_kT", [P, KC, MW])
        k2 = fixed(ctx, nc, "ks_k2", [P, KC, MW])
        nrm = fixed(ctx, nc, "ks_nrm", [P, 2, H])
        feat = fixed(ctx, nc, "ks_feat", [P, 2, D])
        phi = fixed(ctx, nc, "ks_phi", [P, 2, D])
        vm = fixed(ctx, nc, "ks_vm", [P, 2, D])
        kv = fixed(ctx, nc, "ks_kv", [P, KC, P])
        k1 = fixed(ctx, nc, "ks_k1", [P, KC])
        pk = [psum(ctx, nc, f"ks_pk{i}") for i in range(2)]
        pf = psum(ctx, nc, "ks_pf")
        pq = psum(ctx, nc, "ks_pq")
        pv = [psum(ctx, nc, f"ks_pv{i}") for i in range(2)]
        pkv = psum(ctx, nc, "ks_pkv")
        pk1 = psum(ctx, nc, "ks_pone")
        loaded, wloaded, set_up = sems(ctx, nc, "ks", "loaded wloaded setup")
        x_loaded = sems(ctx, nc, "ks", "x0 x1")
        (projected, kept, featured, normed, bounded, valued, cleared, mapped, copied, added, drained, masked, multiplied,
         moved, passed) = sems(ctx, nc, "ks", "projected kept featured normed bounded valued cleared mapped copied added "
                                              "drained masked multiplied moved passed")
        block = ctx.enter_context(nc.Block())
        NC = 2 * KC

        @block.sync
        def _(sp):
            for w, name in ((wk, "Wk"), (wv, "Wv"), (C["wo"], "Wo")):
                sp.dma_start(w[:, :, :], dram[name].rearrange("(k p) n -> p k n", p=P)).then_inc(wloaded, 16)
            sp.wait_ge(set_up, 1)
            load_feature_maps(nc, sp, omega, dram["omega_k"], loaded)

            sp.dma_start(xT[:, 0, :, :], dram["xnT"][0]).then_inc(x_loaded[0], 16)
            sp.dma_start(xT[:, 1, :, :], dram["xnT"][1]).then_inc(x_loaded[1], 16)
            with sp.Fori(0, (NM - 3) // 2) as i:
                for q in range(2):
                    sp.wait_ge(valued, (i * 2 + q + 1) * TM)
                    hold(sp, passed)
                    sp.dma_start(xT[:, q, :, :], dram["xnT"][i * 2 + q + 2]).then_inc(x_loaded[q], 16)
            sp.wait_ge(valued, (NM - 2) * TM)
            sp.dma_start(xT[:, 0, :, :], dram["xnT"][NM - 1]).then_inc(x_loaded[0], 16)

        @block.scalar
        def _(act):
            act.sem_inc(copied, 1)
            act.sem_inc(mapped, 1)

            def macro(m, q, u):
                act.wait_ge(normed, m * TM)
                for c in range(NC):
                    n = m * NC + c
                    hf, k = divmod(c, KC)
                    act.wait_ge(projected, n + 1)
                    nc.scalar.activation(kT[:, k, hf * HW:(hf + 1) * HW], pk[c % 2][:, 0:HW], ACT.Copy)
                    nc.scalar.activation(k2[:, k, hf * HW:(hf + 1) * HW], pk[c % 2][:, 0:HW], ACT.Square).then_inc(kept, 1)
                for j in range(TM):
                    n = m * TM + j
                    s = (q + j) % 2
                    act.wait_ge(valued, n + 1)
                    act.wait_ge(added, n)
                    nc.scalar.activation(vm[:, s, :], pv[s][:, :], ACT.Copy).then_inc(copied, 1)
                    act.wait_ge(featured, n + 1)
                    nc.scalar.activation(phi[:, s, :], feat[:, s, :], ACT.Exp).then_inc(mapped, 1)
            over_macros(act, macro)

        @block.vector
        def _(dve):
            nc.vector.memset(omega[:, :], 0.0).then_inc(set_up, 1)
            nc.vector.memset(half[:, :], 0.0).then_inc(moved, 1)
            nc.vector.memset(kv[:, :, :], 0.0)
            nc.vector.memset(k1[:, :], 0.0).then_inc(moved, 1)
            dve.wait_ge(moved, 2)
            nc.vector.memset(half[0:HF, 0:1], -0.5 / HF)
            nc.vector.memset(half[HF:P, 1:2], -0.5 / HF).then_inc(moved, 1)
            dve.wait_ge(loaded, 32)
            nc.vector.tensor_scalar(omega[:, :], omega[:, :], HF ** -0.5, None, ALU.mult).then_inc(set_up, 1)

            def macro(m, q, u):
                for j in range(TM):
                    n = m * TM + j
                    s = (q + j) % 2
                    dve.wait_ge(normed, n + 1)
                    nc.vector.tensor_scalar(nrm[:, s, :], pq[:, 0:H], NORM_TOP, NORM_LOW, ALU.min, ALU.max).then_inc(bounded, 1)
                    dve.wait_ge(bounded, n + 1)
                    dve.wait_ge(mapped, n)
                    nc.vector.scalar_tensor_tensor(feat[:, s, :].rearrange("p (h f) -> p h f", f=HF),
                                                   pf[:, :].rearrange("p (h f) -> p h f", f=HF), CLAMP,
                                                   bc(nrm[:, s, :].unsqueeze(2), [P, H, HF]), ALU.min, ALU.add).then_inc(featured, 1)
                dve.wait_ge(added, m * TM + TM + 1)
                nc.vector.tensor_tensor(kv[:, :, :].rearrange("p k c -> p (k c)"), kv[:, :, :].rearrange("p k c -> p (k c)"),
                                        pkv[:, :], ALU.add)
                nc.vector.tensor_tensor(k1[:, :], k1[:, :], pk1[:, 0:KC], ALU.add).then_inc(drained, 1)
            over_macros(dve, macro)
            dve.wait_ge(drained, NM)
            nc.vector.tensor_tensor(kv[:, :, :], kv[:, :, :], bc(C["pair"][:, :].unsqueeze(1), [P, KC, P]), ALU.mult)
            nc.vector.tensor_tensor(C["k1"][:, :, :], bc(k1[:, :].unsqueeze(2), [P, KC, P]),
                                    bc(C["pair"][:, :].unsqueeze(1), [P, KC, P]), ALU.mult).then_inc(masked, 1)
            for c in range(KC):
                dve.wait_ge(multiplied, c + 1)
                nc.vector.tensor_copy(C["g"][:, c, :], pk[c % 2][:, :]).then_inc(cleared, 1)
            dve.wait_ge(cleared, KC)

        @block.tensor
        def _(pe):
            pe.sem_inc(added, 1)
            pe.wait_ge(wloaded, 48)
            pe.wait_ge(set_up, 2)
            pe.wait_ge(moved, 3)

            def add(m, q, j):
                n = m * TM + j
                s = (q + j) % 2
                pe.wait_ge(copied, n + 1 + 1)
                pe.wait_ge(mapped, n + 1 + 1)
                if j == 0:
                    pe.wait_ge(drained, m)
                for c in range(KC):
                    nc.tensor.matmul(pkv[:, c * P:(c + 1) * P], vm[:, s, c * P:(c + 1) * P], phi[:, s, c * P:(c + 1) * P],
                                     start=(j == 0 and c == 0), stop=(j == TM - 1), skip_group_check=True)
                for c in range(KC):
                    last = nc.tensor.matmul(pk1[:, c:c + 1], phi[:, s, c * P:(c + 1) * P], C["valid"][:, bass.ds(n, 1)],
                                            start=(j == 0 and c == 0), stop=(j == TM - 1), skip_group_check=True)
                last.then_inc(added, 1)

            def macro(m, q, u):
                pe.wait_ge(x_loaded[q], u * 16 + 16)
                for c in range(NC):
                    n = m * NC + c
                    hf, kk = divmod(c, KC)
                    if c >= 2:
                        pe.wait_ge(kept, n - 1)
                    else:
                        pe.wait_ge(kept, m * NC)
                    for k in range(KC):
                        last = nc.tensor.matmul(pk[c % 2][:, 0:HW], wk[:, k, kk * P:(kk + 1) * P],
                                                xT[:, q, k, hf * HW:(hf + 1) * HW], start=(k == 0), stop=(k == KC - 1))
                    last.then_inc(projected, 1)
                for j in range(TM):
                    n = m * TM + j
                    s = (q + j) % 2
                    t = slice(j * P, (j + 1) * P)
                    pe.wait_ge(copied, n)
                    for k in range(KC):
                        last = nc.tensor.matmul(pv[s][:, :], xT[:, q, k, t], wv[:, k, :], start=(k == 0), stop=(k == KC - 1))
                    last.then_inc(valued, 1)
                    pe.wait_ge(kept, m * NC + NC)
                    pe.wait_ge(featured, n)
                    for c in range(KC):
                        nc.tensor.matmul(pf[:, c * P:(c + 1) * P], kT[:, c, t], omega[:, :], start=True, stop=True)
                    for c in range(KC):
                        last = nc.tensor.matmul(pq[:, 2 * c:2 * c + 2], k2[:, c, t], half[:, :], start=True, stop=True)
                    last.then_inc(normed, 1)
                    if j:
                        add(m, q, j - 1)
                add(m, q, TM - 1)
            over_macros(pe, macro)
            pe.wait_ge(masked, 1)
            for c in range(KC):
                if c >= 2:
                    pe.wait_ge(cleared, c - 1)
                nc.tensor.matmul(pk[c % 2][:, :], kv[:, c, :], C["wo"][:, c, :], start=True, stop=True).then_inc(multiplied, 1)


def query_rows(nc, C, dram):
    with Stage(nc) as ctx:
        xT = fixed(ctx, nc, "qr_xT", [P, 2, KC, MW])
        wq = fixed(ctx, nc, "qr_wq", [P, KC, D])
        omega = fixed(ctx, nc, "qr_omega", [P, P])
        half = fixed(ctx, nc, "qr_half", [P, P])
        qT = fixed(ctx, nc, "qr_qT", [P, 2, HW])
        q2 = fixed(ctx, nc, "qr_q2", [P, 2, HW])
        nrm = fixed(ctx, nc, "qr_nrm", [P, 2, HW])
        phi = fixed(ctx, nc, "qr_phi", [P, 2, HW])
        rec = fixed(ctx, nc, "qr_rec", [P, 2, HW])
        phin = fixed(ctx, nc, "qr_phin", [P, KC, MW])
        xs = fixed(ctx, nc, "qr_x", [P, 2, D])
        ac = fixed(ctx, nc, "qr_ac", [P, 2, AW])
        rden = fixed(ctx, nc, "qr_rden", [P, 2, 2, H])
        x1 = fixed(ctx, nc, "qr_x1", [P, 2, D])
        st = fixed(ctx, nc, "qr_st", [P, 2, 6])
        agg = fixed(ctx, nc, "qr_agg", [P, 2, 2])
        pq = [psum(ctx, nc, f"qr_pq{i}") for i in range(2)]
        pf = psum(ctx, nc, "qr_pf")
        pn = psum(ctx, nc, "qr_pn")
        pd = [psum(ctx, nc, f"qr_pd{i}") for i in range(2)]
        pm = [psum(ctx, nc, f"qr_pm{i}") for i in range(2)]
        loaded, wloaded, set_up = sems(ctx, nc, "qr", "loaded wloaded setup")
        x_loaded = sems(ctx, nc, "qr", "x0 x1")
        r_loaded = sems(ctx, nc, "qr", "r0 r1")
        stored = sems(ctx, nc, "qr", "s0 s1")
        (projected, kept, featured, bounded, argued, mapped, summed, inverted, divided, mixed, used, dens, rdens,
         graphed, based, finished, rooted, counted, joined, passed, passed_v) = sems(
            ctx, nc, "qr", "projected kept featured bounded argued mapped summed inverted divided mixed used dens rdens "
                           "graphed based finished rooted counted joined passed passedv")
        block = ctx.enter_context(nc.Block())
        NC = 2 * KC
        rows = dram["x"].rearrange("(n p) d -> n p d", p=P)
        acc = dram["acc"][0:NP, :].rearrange("(n p) w -> n p w", p=P)
        x1_rows = dram["x1"].rearrange("(n p) d -> n p d", p=P)

        @block.sync
        def _(sp):
            sp.dma_start(wq[:, :, :], dram["Wq"].rearrange("(k p) n -> p k n", p=P)).then_inc(wloaded, 16)
            sp.wait_ge(set_up, 1)
            load_feature_maps(nc, sp, omega, dram["omega_q"], loaded)

            def macro(m, q, u):
                for j in range(TM):
                    n = m * TM + j
                    s = (q + j) % 2
                    sp.wait_ge(finished, n + 1)
                    hold(sp, passed)
                    sp.dma_start(xs[:, s, :], rows[n]).then_inc(r_loaded[s], 16)
                    sp.dma_start(ac[:, s, :], acc[n]).then_inc(r_loaded[s], 16)

            def transposed(m, q):
                sp.dma_start(xT[:, q, :, :], dram["xnT"][m]).then_inc(x_loaded[q], 16)
            transposed(0, 0)
            with sp.Fori(0, NM // 2) as i:
                transposed(i * 2 + 1, 1)
                macro(i * 2, 0, i)
                sp.wait_ge(projected, (i * 2 + 1) * NC + 2)
                hold(sp, passed)
                transposed(i * 2 + 2, 0)
                macro(i * 2 + 1, 1, i)
                sp.wait_ge(projected, (i * 2 + 2) * NC + 2)
                hold(sp, passed)
            macro(NM - 1, 0, NM // 2)

        @block.gpsimd
        def _(pool):
            def macro(m, q, u):
                for j in range(TM):
                    n = m * TM + j
                    s = (q + j) % 2
                    pool.wait_ge(finished, n + 1 + 2)
                    pool.dma_start(x1_rows[n], x1[:, s, :]).then_inc(stored[s], 16)
            over_macros(pool, macro)
            pool.wait_ge(stored[0], 16 * ((NT + 1) // 2))
            pool.wait_ge(stored[1], 16 * (NT // 2))

        @block.scalar
        def _(act):
            act.sem_inc(kept, 2)
            act.sem_inc(mapped, 2)

            def macro(m, q, u):
                for c in range(NC):
                    n = m * NC + c
                    act.wait_ge(projected, n + 1 + 2)
                    act.wait_ge(featured, n + 1)
                    nc.scalar.activation(qT[:, c % 2, :], pq[c % 2][:, 0:HW], ACT.Copy)
                    nc.scalar.activation(q2[:, c % 2, :], pq[c % 2][:, 0:HW], ACT.Square).then_inc(kept, 1)
                    act.wait_ge(argued, n + 1 + 2)
                    act.wait_ge(divided, n + 1)
                    nc.scalar.activation(phi[:, c % 2, :], nrm[:, c % 2, :], ACT.Exp).then_inc(mapped, 1)
            over_macros(act, macro)
            act.wait_ge(counted, 1)
            nc.scalar.activation(C["stats2"][:, :, 1], C["stats2"][:, :, 1], ACT.Sqrt).then_inc(rooted, 1)

        @block.vector
        def _(dve):
            nc.vector.memset(omega[:, :], 0.0).then_inc(set_up, 1)
            nc.vector.tensor_scalar(half[:, :], C["pair"][:, :], -0.5 / HF, None, ALU.mult).then_inc(set_up, 1)
            dve.sem_inc(argued, 2)
            dve.sem_inc(divided, 2)
            dve.sem_inc(finished, 2)
            dve.wait_ge(loaded, 32)
            nc.vector.tensor_scalar(omega[:, :], omega[:, :], HF ** -0.5, None, ALU.mult).then_inc(set_up, 1)

            def argue(m, c):
                n = m * NC + c
                dve.wait_ge(featured, n + 1 + 2)
                dve.wait_ge(mapped, n + 1)
                nc.vector.tensor_scalar(nrm[:, c % 2, :], pn[:, 0:HW], NORM_TOP, NORM_LOW, ALU.min, ALU.max).then_inc(bounded, 1)
                dve.wait_ge(bounded, n + 1)
                nc.vector.scalar_tensor_tensor(nrm[:, c % 2, :], pf[:, 0:HW], CLAMP, nrm[:, c % 2, :],
                                               ALU.min, ALU.add).then_inc(argued, 1)

            def divide(m, c):
                n = m * NC + c
                hf, k = divmod(c, KC)
                dve.wait_ge(summed, n + 1)
                nc.vector.reciprocal(rec[:, c % 2, :], pd[c % 2][:, 0:HW]).then_inc(inverted, 1)
                dve.wait_ge(inverted, n + 1)
                if c == 0:
                    dve.wait_ge(mixed, m * TM)
                nc.vector.tensor_tensor(phin[:, k, hf * HW:(hf + 1) * HW], phi[:, c % 2, :], rec[:, c % 2, :],
                                        ALU.mult).then_inc(divided, 1)

            def macro(m, q, u):
                for c in range(NC):
                    argue(m, c)
                    if c:
                        divide(m, c - 1)
                divide(m, NC - 1)
                for j in range(TM):
                    n = m * TM + j
                    s = (q + j) % 2
                    v = u * TM + (q * TM + j) // 2
                    dve.wait_ge(r_loaded[s], v * 32 + 32)
                    nc.vector.tensor_scalar(rden[:, s, 0, :], ac[:, s, D:D + H], DEN_LOW, None, ALU.max).then_inc(dens, 1)
                    dve.wait_ge(dens, n + 1)
                    nc.vector.reciprocal(rden[:, s, 1, :], rden[:, s, 0, :]).then_inc(rdens, 1)
                    dve.wait_ge(rdens, n + 1)
                    part = ac[:, s, 0:D].rearrange("p (h f) -> p h f", f=HF)
                    nc.vector.tensor_tensor(part, part, bc(rden[:, s, 1, :].unsqueeze(2), [P, H, HF]), ALU.mult).then_inc(graphed, 1)
                    dve.wait_ge(graphed, n + 1)
                    nc.vector.tensor_tensor(xs[:, s, :], xs[:, s, :], ac[:, s, 0:D], ALU.add).then_inc(based, 1)
                    dve.wait_ge(based, n + 1)
                    dve.wait_ge(mixed, n + 1)
                    dve.wait_ge(stored[s], v * 16)
                    nc.vector.tensor_tensor(x1[:, s, :], pm[s][:, :], xs[:, s, :], ALU.add).then_inc(finished, 1)
                    dve.wait_ge(finished, n + 1 + 2)
                    nc.vector.bn_stats(st[:, s, :], x1[:, s, :]).then_inc(used, 1)
                    dve.wait_ge(used, n + 1)
                    hold(dve, passed_v)
                    nc.vector.bn_aggr(agg[:, s, :], st[:, s, :]).then_inc(joined, 1)
                    dve.wait_ge(joined, n + 1)
                    nc.vector.tensor_copy(C["stats2"][:, n, :], agg[:, s, :])
            over_macros(dve, macro)
            dve.wait_ge(used, NT)
            nc.vector.memset(rden[:, 0, 0, :], 0.0).then_inc(dens, 1)
            dve.wait_ge(dens, NT + 1)
            nc.vector.tensor_scalar(C["stats2"][:, :, 1], C["stats2"][:, :, 1], LN_EPS, None, ALU.add).then_inc(counted, 1)
            dve.wait_ge(rooted, 1)
            nc.vector.reciprocal(C["stats2"][:, :, 1], C["stats2"][:, :, 1]).then_inc(counted, 1)
            dve.wait_ge(counted, 2)

        @block.tensor
        def _(pe):
            pe.wait_ge(wloaded, 16)
            pe.wait_ge(set_up, 3)
            pe.sem_inc(projected, 2)
            pe.sem_inc(featured, 2)

            def project(m, q, c):
                n = m * NC + c
                hf, kk = divmod(c, KC)
                pe.wait_ge(kept, n + 1)
                for k in range(KC):
                    last = nc.tensor.matmul(pq[c % 2][:, 0:HW], wq[:, k, kk * P:(kk + 1) * P],
                                            xT[:, q, k, hf * HW:(hf + 1) * HW], start=(k == 0), stop=(k == KC - 1))
                last.then_inc(projected, 1)

            def feature(m, c):
                n = m * NC + c
                pe.wait_ge(kept, n + 1 + 2)
                pe.wait_ge(argued, n + 2)
                nc.tensor.matmul(pf[:, 0:HW], omega[:, :], qT[:, c % 2, :], start=True, stop=True)
                nc.tensor.matmul(pn[:, 0:HW], half[:, :], q2[:, c % 2, :], start=True, stop=True).then_inc(featured, 1)

            def total(m, c):
                n = m * NC + c
                pe.wait_ge(mapped, n + 1 + 2)
                pe.wait_ge(divided, n + 1)
                nc.tensor.matmul(pd[c % 2][:, 0:HW], C["k1"][:, c % KC, :], phi[:, c % 2, :],
                                 start=True, stop=True).then_inc(summed, 1)

            def macro(m, q, u):
                pe.wait_ge(x_loaded[q], u * 16 + 16)
                project(m, q, 0)
                for c in range(NC):
                    if c + 1 < NC:
                        project(m, q, c + 1)
                    feature(m, c)
                    if c:
                        total(m, c - 1)
                total(m, NC - 1)
                pe.wait_ge(divided, m * NC + NC + 2)
                for j in range(TM):
                    n = m * TM + j
                    s = (q + j) % 2
                    pe.wait_ge(finished, n + 1)
                    for c in range(KC):
                        last = nc.tensor.matmul(pm[s][:, :], phin[:, c, j * P:(j + 1) * P], C["g"][:, c, :],
                                                start=(c == 0), stop=(c == KC - 1))
                    last.then_inc(mixed, 1)
            over_macros(pe, macro)


def route(nc, C, dram):
    with Stage(nc) as ctx:
        xs = fixed(ctx, nc, "rt_x", [P, 2, TM, D])
        xT = fixed(ctx, nc, "rt_xT", [P, 2, KC, P])
        wr = fixed(ctx, nc, "rt_wr", [P, KC, EX])
        lg = fixed(ctx, nc, "rt_lg", [P, 2, EX])
        best = fixed(ctx, nc, "rt_best", [P, 2, 8])
        which = fixed(ctx, nc, "rt_which", [P, 2, 8], U32)
        top = fixed(ctx, nc, "rt_top", [P, 2, NT])
        num = fixed(ctx, nc, "rt_num", [P, 2, NT])
        hit = fixed(ctx, nc, "rt_hit", [P, 2, NT, EX])
        both = fixed(ctx, nc, "rt_both", [P, NT, EX])
        tot = fixed(ctx, nc, "rt_tot", [P, NT, EX])
        cum = fixed(ctx, nc, "rt_cum", [P, NT, EX])
        nul = fixed(ctx, nc, "rt_nul", [P, NT])
        slot = fixed(ctx, nc, "rt_slot", [P, 2, NT])
        keep = fixed(ctx, nc, "rt_keep", [P, 2, NT])
        pos = fixed(ctx, nc, "rt_pos", [P, 2, NT])
        goal = fixed(ctx, nc, "rt_goal", [P, 2, NT])
        gap = fixed(ctx, nc, "rt_gap", [P, 2, NT])
        at = fixed(ctx, nc, "rt_at", [P, 2, TM, 2], I32)
        blank = fixed(ctx, nc, "rt_blank", [P, 4 * D])
        pT = [psum(ctx, nc, f"rt_pT{i}") for i in range(2)]
        pl = [psum(ctx, nc, f"rt_pl{i}") for i in range(2)]
        pp = psum(ctx, nc, "rt_pp")
        po = psum(ctx, nc, "rt_po")
        wloaded, blanks, blanked = sems(ctx, nc, "rt", "wloaded blanks blanked")
        loaded = sems(ctx, nc, "rt", " ".join(f"ld{i}" for i in range(2 * TM)))
        again = sems(ctx, nc, "rt", " ".join(f"again{i}" for i in range(2)))
        sent = sems(ctx, nc, "rt", "sent0 sent1")
        (normed, turned, kept, scored, logged, maxed, found, noted, v, s, counted, renormed, indexed, passed,
         passed_p, passed_v) = sems(ctx, nc, "rt", "normed turned kept scored logged maxed found noted v s counted renormed indexed "
                                         "passed passedp passedv")
        block = ctx.enter_context(nc.Block())
        rows = dram["x1"].rearrange("(n p) d -> n p d", p=P)
        macros = dram["x1"].rearrange("(m j p) d -> m p j d", j=TM, p=P)
        LAST = 14

        @block.sync
        def _(sp):
            sp.dma_start(wr[:, :, :], dram["router_w"].rearrange("(k p) e -> p k e", p=P)).then_inc(wloaded, 16)

            def macro(m, q, u):
                for j in range(TM):
                    sp.wait_ge(turned, m * TM + j + 1)
                    hold(sp, passed)
                    sp.dma_start(xs[:, q, j, :], rows[m * TM + j]).then_inc(loaded[q * TM + j], 16)
            over_macros(sp, macro)
            sp.wait_ge(blanks, 1)
            sp.dma_start(dram["xe"].rearrange("(p n) d -> p (n d)", p=P).rearrange("p (n w) -> p n w", w=4 * D),
                         bc(blank[:, :].unsqueeze(1), [P, EX * CAP // P // 4, 4 * D])).then_inc(blanked, 16)
            sp.wait_ge(turned, NT + 2 * TM)

            def send(m, q, u):
                sp.wait_ge(sent[q], u * (2 * TM * 16))
                hold(sp, passed)
                sp.dma_start(xs[:, q, :, :], macros[m]).then_inc(again[q], 16)
            over_macros(sp, send)

        @block.scalar
        def _(act):
            act.sem_inc(kept, 2)

            def macro(m, q, u):
                for j in range(TM):
                    n = m * TM + j
                    b = (q + j) % 2
                    act.wait_ge(turned, n + 1 + 2 * TM)
                    act.wait_ge(scored, n + 1)
                    nc.scalar.activation(xT[:, b, :, :].rearrange("p k t -> p (k t)"), pT[b][:, :], ACT.Copy).then_inc(kept, 1)
            over_macros(act, macro)
            act.wait_ge(v, 2)
            nc.scalar.activation(gap[:, 0, :], gap[:, 1, :], ACT.Exp).then_inc(s, 1)

        @block.vector
        def _(dve):
            nc.vector.memset(blank[:, :], 0.0).then_inc(blanks, 1)
            nc.vector.memset(nul[:, :], 0.0)

            def norm(n, q, j, done):
                nc.vector.tensor_scalar(xs[:, q, j, :], xs[:, q, j, :], C["stats2"][:, n, 0:1], C["stats2"][:, n, 1:2],
                                        ALU.subtract, ALU.mult).then_inc(done, 1)

            def macro(m, q, u):
                for j in range(TM + 1):
                    n = m * TM + j
                    if j < TM:
                        dve.wait_ge(loaded[q * TM + j], u * 16 + 16)
                        norm(n, q, j, normed)
                    if j:
                        pick(m, q, j - 1)

            def pick(m, q, j):
                n = m * TM + j
                b = (q + j) % 2
                dve.wait_ge(scored, n + 1 + 2)
                nc.vector.tensor_copy(lg[:, b, :], pl[b][:, 0:EX]).then_inc(logged, 1)
                dve.wait_ge(logged, n + 1)
                hold(dve, passed_v)
                nc.vector.max(best[:, b, :], lg[:, b, :]).then_inc(maxed, 1)
                dve.wait_ge(maxed, n + 1)
                hold(dve, passed_v)
                nc.vector.max_index(which[:, b, :], best[:, b, :], lg[:, b, :]).then_inc(found, 1)
                dve.wait_ge(found, n + 1)
                nc.vector.tensor_copy(top[:, :, bass.ds(n, 1)], best[:, b, 0:2].unsqueeze(2))
                nc.vector.tensor_copy(num[:, :, bass.ds(n, 1)], which[:, b, 0:2].unsqueeze(2)).then_inc(noted, 1)
            over_macros(dve, macro)
            dve.wait_ge(noted, NT)
            done = [0]

            def link(ins):
                done[0] += 1
                ins.then_inc(v, 1)
                dve.wait_ge(v, done[0])

            for kk in range(2):
                last = nc.vector.tensor_tensor(hit[:, kk, :, :], bc(num[:, kk, :].unsqueeze(2), [P, NT, EX]),
                                               bc(C["cols"][:, 0:EX].unsqueeze(1), [P, NT, EX]), ALU.is_equal)
            link(last)
            link(nc.vector.tensor_tensor(gap[:, 1, :], top[:, 1, :], top[:, 0, :], ALU.subtract))
            link(nc.vector.tensor_tensor(both[:, :, :], hit[:, 0, :, :], hit[:, 1, :, :], ALU.add))
            dve.wait_ge(s, 1)
            link(nc.vector.tensor_scalar(gap[:, 1, :], gap[:, 0, :], 1.0, None, ALU.add))
            link(nc.vector.reciprocal(C["weight"][:, 0, :], gap[:, 1, :]))
            nc.vector.tensor_tensor(C["weight"][:, 1, :], C["weight"][:, 0, :], gap[:, 0, :], ALU.mult)
            dve.wait_ge(counted, 1)
            link(nc.vector.tensor_copy(tot[:, :, :].rearrange("p n e -> p (n e)"), po[:, 0:NT * EX]))
            for x in range(EX):
                last = nc.vector.tensor_tensor_scan(cum[:, :, x], tot[:, :, x], nul[:, :], 0.0, ALU.add, ALU.add)
            link(last)
            link(nc.vector.tensor_tensor(cum[:, :, :], cum[:, :, :], tot[:, :, :], ALU.subtract))
            link(nc.vector.tensor_tensor(cum[:, :, :].rearrange("p n e -> p (n e)"), cum[:, :, :].rearrange("p n e -> p (n e)"),
                                         pp[:, 0:NT * EX], ALU.add))
            link(nc.vector.tensor_tensor(hit[:, :, :, :], hit[:, :, :, :], bc(cum[:, :, :].unsqueeze(1), [P, 2, NT, EX]),
                                         ALU.mult))
            nc.vector.tensor_scalar(pos[:, :, :], num[:, :, :], float(CAP), None, ALU.mult)
            link(nc.vector.tensor_reduce(slot[:, :, :], hit[:, :, :, :], AX.X, ALU.add))
            nc.vector.tensor_scalar(keep[:, :, :], slot[:, :, :], float(CAP), None, ALU.is_lt)
            nc.vector.tensor_tensor(goal[:, :, :], slot[:, :, :], pos[:, :, :], ALU.add)
            link(nc.vector.tensor_scalar(slot[:, :, :], slot[:, :, :], float(CAP - 1), None, ALU.min))
            nc.vector.tensor_tensor(C["weight"][:, :, :], C["weight"][:, :, :], keep[:, :, :], ALU.mult)
            nc.vector.tensor_tensor(slot[:, :, :], slot[:, :, :], pos[:, :, :], ALU.add)
            link(nc.vector.tensor_tensor(keep[:, :, :], keep[:, :, :], bc(C["valid"][:, :].unsqueeze(1), [P, 2, NT]), ALU.mult))
            nc.vector.tensor_copy(C["from"][:, :, :], slot[:, :, :].rearrange("p k n -> p n k"))
            link(nc.vector.tensor_scalar(keep[:, :, :], keep[:, :, :], -BIG, BIG, ALU.mult, ALU.add))
            assert done[0] == LAST
            nc.vector.tensor_tensor(goal[:, :, :], goal[:, :, :], keep[:, :, :], ALU.add).then_inc(indexed, 1)
            dve.wait_ge(indexed, 1)

            def send(m, q, u):
                dve.wait_ge(sent[q], u * (2 * TM * 16))
                nc.vector.tensor_copy(at[:, q, :, :], goal[:, :, bass.ds(m * TM, TM)].rearrange("p k j -> p j k")).then_inc(indexed, 1)
                dve.wait_ge(again[q], u * 16 + 16)
                for j in range(TM):
                    norm(m * TM + j, q, j, renormed)
            over_macros(dve, send)

        @block.gpsimd
        def _(pool):
            pool.wait_ge(blanked, 16)

            def send(m, q, u):
                pool.wait_ge(indexed, m + 2)
                for j in range(TM):
                    pool.wait_ge(renormed, m * TM + j + 1)
                    hold(pool, passed_p)
                    for kk in range(2):
                        pool.indirect_dma_start(out=dram["xe"], out_offset=bass.IndirectOffsetOnAxis(ap=at[:, q, j, kk:kk + 1], axis=0),
                                                in_=xs[:, q, j, :], in_offset=None, bounds_check=EX * CAP - 1,
                                                oob_is_err=False).then_inc(sent[q], 16)
            over_macros(pool, send)
            pool.wait_ge(sent[0], 2 * TM * 16 * ((NM + 1) // 2))
            pool.wait_ge(sent[1], 2 * TM * 16 * (NM // 2))

        @block.tensor
        def _(pe):
            pe.wait_ge(wloaded, 16)
            pe.sem_inc(turned, 2 * TM)
            pe.sem_inc(scored, 2)

            def turn(m, q, j):
                n = m * TM + j
                b = (q + j) % 2
                pe.wait_ge(normed, n + 1)
                pe.wait_ge(kept, n + 1)
                for k in range(KC):
                    last = nc.tensor.transpose(pT[b][:, k * P:(k + 1) * P], xs[:, q, j, k * P:(k + 1) * P], C["ident"][:, :])
                last.then_inc(turned, 1)

            def macro(m, q, u):
                turn(m, q, 0)
                for j in range(TM):
                    n = m * TM + j
                    b = (q + j) % 2
                    if j + 1 < TM:
                        turn(m, q, j + 1)
                    pe.wait_ge(kept, n + 1 + 2)
                    pe.wait_ge(logged, n)
                    for k in range(KC):
                        last = nc.tensor.matmul(pl[b][:, 0:EX], xT[:, b, k, :], wr[:, k, :], start=(k == 0), stop=(k == KC - 1))
                    last.then_inc(scored, 1)
            over_macros(pe, macro)
            pe.wait_ge(v, 3)
            flat = both[:, :, :].rearrange("p n e -> p (n e)")
            nc.tensor.matmul(pp[:, 0:NT * EX], C["before"][:, :], flat, start=True, stop=True)
            nc.tensor.matmul(po[:, 0:NT * EX], C["ones"][:, :], flat, start=True, stop=True).then_inc(counted, 1)


def experts(nc, C, dram):
    with Stage(nc) as ctx:
        w1 = fixed(ctx, nc, "ex_w1", [P, 2, KC, FF])
        w2 = fixed(ctx, nc, "ex_w2", [P, 2, FC, D])
        b1 = fixed(ctx, nc, "ex_b1", [P, 2, FC])
        b2 = fixed(ctx, nc, "ex_b2", [P, 2, D])
        xs = fixed(ctx, nc, "ex_x", [P, 2, ST, D])
        xT = fixed(ctx, nc, "ex_xT", [P, 2, KC, SW])
        hT = fixed(ctx, nc, "ex_hT", [P, 2, FC, SW])
        ys = fixed(ctx, nc, "ex_y", [P, 2, ST, D])
        pT = [psum(ctx, nc, f"ex_pT{i}") for i in range(2)]
        ph = [psum(ctx, nc, f"ex_ph{i}") for i in range(2)]
        py = [psum(ctx, nc, f"ex_py{i}") for i in range(2)]
        w_loaded = sems(ctx, nc, "ex", "w0 w1")
        x_loaded = sems(ctx, nc, "ex", "x0 x1")
        y_stored = sems(ctx, nc, "ex", "y0 y1")
        turned, kept_a, kept_v, expanded, bent, reduced, biased, used, passed = sems(
            ctx, nc, "ex", "turned kept_a kept_v expanded bent reduced biased used passed")
        block = ctx.enter_context(nc.Block())
        CH = CAP // SW
        xe = dram["xe"].rearrange("(c t p) d -> c p t d", t=ST, p=P)
        ye = dram["ye"].rearrange("(c t p) d -> c p t d", t=ST, p=P)

        def chunks(eng, body, open_expert=None):
            with eng.Fori(0, EX // 2) as i:
                for w in range(2):
                    if open_expert:
                        open_expert(i * 2 + w, w, i)
                    for c in range(CH):
                        body((i * 2 + w) * CH + c, c % 2, w, i * CH + (w * CH + c) // 2)

        @block.sync
        def _(sp):
            def open_expert(e, w, i):
                sp.wait_ge(used, e + 1)
                hold(sp, passed)
                sp.dma_start(w1[:, w, :, :], dram["w1"][e].rearrange("(k p) f -> p k f", p=P)).then_inc(w_loaded[w], 16)
                sp.dma_start(w2[:, w, :, :], dram["w2"][e].rearrange("(k p) d -> p k d", p=P)).then_inc(w_loaded[w], 16)
                sp.dma_start(b1[:, w, :], dram["b1"][e]).then_inc(w_loaded[w], 16)
                sp.dma_start(b2[:, w, :], dram["b2"][e].partition_broadcast(P)).then_inc(w_loaded[w], 16)

            def chunk(n, q, w, u):
                sp.wait_ge(turned, n * KC + KC)
                hold(sp, passed)
                sp.dma_start(xs[:, q, :, :], xe[n]).then_inc(x_loaded[q], 16)
            chunks(sp, chunk, open_expert)

        @block.gpsimd
        def _(pool):
            def chunk(n, q, w, u):
                pool.wait_ge(biased, n * ST + ST + 2)
                pool.dma_start(ye[n], ys[:, q, :, :]).then_inc(y_stored[q], 16)
            chunks(pool, chunk)
            for q in range(2):
                pool.wait_ge(y_stored[q], EX * CH // 2 * 16)

        @block.scalar
        def _(act):
            act.sem_inc(kept_a, 1)
            act.sem_inc(bent, 2)

            def chunk(n, q, w, u):
                for k in range(0, KC, 2):
                    act.wait_ge(turned, n * KC + k + 1 + 2 * KC)
                    act.wait_ge(expanded, n * FC + FC)
                    nc.scalar.activation(xT[:, q, k, :], pT[0][:, :], ACT.Copy).then_inc(kept_a, 1)
                for f in range(FC):
                    act.wait_ge(expanded, n * FC + f + 1 + 2 * FC)
                    act.wait_ge(reduced, n * ST + ST)
                    nc.scalar.activation(hT[:, q, f, :], ph[f][:, :], ACT.Gelu_apprx_tanh, bias=b1[:, w, f:f + 1]).then_inc(bent, 1)
            chunks(act, chunk)

        @block.vector
        def _(dve):
            dve.sem_inc(kept_v, 1)
            dve.sem_inc(biased, 2)

            def chunk(n, q, w, u):
                for k in range(1, KC, 2):
                    dve.wait_ge(turned, n * KC + k + 1 + 2 * KC)
                    dve.wait_ge(expanded, n * FC + FC)
                    nc.vector.tensor_copy(xT[:, q, k, :], pT[1][:, :]).then_inc(kept_v, 1)
                dve.wait_ge(y_stored[q], u * 16)
                for t in range(ST):
                    m = n * ST + t
                    dve.wait_ge(reduced, m + 1 + 2 * ST)
                    nc.vector.tensor_tensor(ys[:, q, t, :], py[t % 2][:, :], b2[:, w, :], ALU.add).then_inc(biased, 1)
            chunks(dve, chunk)

        @block.tensor
        def _(pe):
            pe.sem_inc(turned, 2 * KC)
            pe.sem_inc(expanded, 2 * FC)
            pe.sem_inc(reduced, 2 * ST)
            pe.sem_inc(used, 2)

            def open_expert(e, w, i):
                pe.wait_ge(w_loaded[w], i * 64 + 64)

            def chunk(n, q, w, u):
                pe.wait_ge(x_loaded[q], u * 16 + 16)
                for k in range(KC):
                    pe.wait_ge((kept_a, kept_v)[k % 2], n * (KC // 2) + k // 2 + 1)
                    for t in range(ST):
                        last = nc.tensor.transpose(pT[k % 2][:, t * P:(t + 1) * P], xs[:, q, t, k * P:(k + 1) * P], C["ident"][:, :])
                    last.then_inc(turned, 1)
                pe.wait_ge(kept_a, (n + 1) * (KC // 2) + 1)
                pe.wait_ge(kept_v, (n + 1) * (KC // 2) + 1)
                for f in range(FC):
                    pe.wait_ge(bent, n * FC + f + 1)
                    for k in range(KC):
                        last = nc.tensor.matmul(ph[f][:, :], w1[:, w, k, f * P:(f + 1) * P], xT[:, q, k, :],
                                                start=(k == 0), stop=(k == KC - 1))
                    last.then_inc(expanded, 1)
                pe.wait_ge(bent, n * FC + FC + 2)
                for t in range(ST):
                    m = n * ST + t
                    pe.wait_ge(biased, m + 1)
                    for f in range(FC):
                        last = nc.tensor.matmul(py[t % 2][:, :], hT[:, q, f, t * P:(t + 1) * P], w2[:, w, f, :],
                                                start=(f == 0), stop=(f == FC - 1))
                    last.then_inc(reduced, 1)
            with pe.Fori(0, EX // 2) as i:
                for w in range(2):
                    open_expert(i * 2 + w, w, i)
                    for c in range(CH):
                        chunk((i * 2 + w) * CH + c, c % 2, w, i * CH + (w * CH + c) // 2)
                    pe.wait_ge(biased, ((i * 2 + w + 1) * CH) * ST + 2)
                    hold(pe, used)


def combine(nc, C, dram):
    with Stage(nc) as ctx:
        xs = fixed(ctx, nc, "co_x", [P, TM, D])
        ya = fixed(ctx, nc, "co_ya", [P, 2, TM, D])
        at = fixed(ctx, nc, "co_at", [P, TM, 2], I32)
        os = fixed(ctx, nc, "co_o", [P, TM, D])
        loaded = sems(ctx, nc, "co", " ".join(f"ld{j}" for j in range(TM)))
        fetched = sems(ctx, nc, "co", " ".join(f"fe{j}" for j in range(TM)))
        stored = sems(ctx, nc, "co", " ".join(f"st{j}" for j in range(TM)))
        indexed, halved, summed, passed, passed_p = sems(ctx, nc, "co", "indexed halved summed passed passedp")
        block = ctx.enter_context(nc.Block())
        rows = dram["x1"].rearrange("(n p) d -> n p d", p=P)
        out = dram["out"].rearrange("(n p) d -> n p d", p=P)

        @block.sync
        def _(sp):
            def load(n, j):
                sp.dma_start(xs[:, j, :], rows[n]).then_inc(loaded[j], 16)

            def store(n, j):
                sp.wait_ge(summed, n + 1)
                hold(sp, passed)
                sp.dma_start(out[n], os[:, j, :]).then_inc(stored[j], 16)
            for j in range(TM):
                load(j, j)
            with sp.Fori(0, NM - 1) as m:
                for j in range(TM):
                    store(m * TM + j, j)
                    load(m * TM + j + TM, j)
            for j in range(TM):
                store((NM - 1) * TM + j, j)
            for j in range(TM):
                sp.wait_ge(stored[j], 16 * NM)

        @block.gpsimd
        def _(pool):
            with pool.Fori(0, NM) as m:
                pool.wait_ge(indexed, m + 1)
                for j in range(TM):
                    pool.wait_ge(summed, m * TM)
                    hold(pool, passed_p)
                    for kk in range(2):
                        pool.indirect_dma_start(out=ya[:, kk, j, :], out_offset=None, in_=dram["ye"],
                                                in_offset=bass.IndirectOffsetOnAxis(ap=at[:, j, kk:kk + 1], axis=0)).then_inc(fetched[j], 16)

        @block.vector
        def _(dve):
            with dve.Fori(0, NM) as m:
                for j in range(TM):
                    dve.wait_ge(fetched[j], m * 32)
                nc.vector.tensor_copy(at[:, :, :], C["from"][:, bass.ds(m * TM, TM), :]).then_inc(indexed, 1)
                for j in range(TM):
                    n = m * TM + j
                    dve.wait_ge(loaded[j], m * 16 + 16)
                    dve.wait_ge(fetched[j], m * 32 + 32)
                    nc.vector.scalar_tensor_tensor(xs[:, j, :], ya[:, 0, j, :], C["weight"][:, 0, bass.ds(n, 1)], xs[:, j, :],
                                                   ALU.mult, ALU.add).then_inc(halved, 1)
                    dve.wait_ge(halved, n + 1)
                    dve.wait_ge(stored[j], m * 16)
                    nc.vector.scalar_tensor_tensor(os[:, j, :], ya[:, 1, j, :], C["weight"][:, 1, bass.ds(n, 1)], xs[:, j, :],
                                                   ALU.mult, ALU.add).then_inc(summed, 1)


_INS = {"x": (NP, D), "src_em": (ET // BT, P, BT), "dst_em": (ET // BT, P, BT), "dst": (EP,), "dst_before": (EP,),
        "W_src": (D, D), "b_src": (D,), "W_dst": (D, D), "b_dst": (D,), "W_val": (D, D), "b_val": (D,),
        "attn_l": (D,), "attn_r": (D,),
        "Wq": (D, D), "Wk": (D, D), "Wv": (D, D), "Wo": (D, D), "omega_q": (HF, HF), "omega_k": (HF, HF),
        "router_w": (D, EX), "w1": (EX, D, FF), "b1": (EX, P, FC), "w2": (EX, FF, D), "b2": (EX, D)}


def build(nc, dram, upto=99):
    with ExitStack() as ctx:
        C = {
            "ident": fixed(ctx, nc, "c_ident", [P, P]),
            "before": fixed(ctx, nc, "c_before", [P, P]),
            "ones": fixed(ctx, nc, "c_ones", [P, P]),
            "cols": fixed(ctx, nc, "c_cols", [P, P]),
            "pair": fixed(ctx, nc, "c_pair", [P, P]),
            "after": fixed(ctx, nc, "c_after", [P, P]),
            "valid": fixed(ctx, nc, "c_valid", [P, NT]),
            "stats1": fixed(ctx, nc, "c_stats1", [P, NT, 2]),
            "stats2": fixed(ctx, nc, "c_stats2", [P, NT, 2]),
        }
        with ExitStack() as inner:
            C["wval"] = fixed(inner, nc, "c_wval", [P, KC, D + 2 * H])
            C["vbias"] = fixed(inner, nc, "c_vbias", [P, D + 2 * H])
            prep_weights(nc, C, dram)
            norm_stats(nc, C, dram, dram["x"], C["stats1"], "s1")
            project_nodes(nc, C, dram)
        if upto >= 2:
            with ExitStack() as inner:
                C["rank"] = fixed(inner, nc, "c_rank", [P, ET])
                C["target"] = fixed(inner, nc, "c_target", [P, ET])
                C["first"] = fixed(inner, nc, "c_first", [P, ET])
                C["own"] = fixed(inner, nc, "c_own", [GH, 2])
                prep_edges(nc, C, dram)
                edge_attention(nc, C, dram)
                merge_groups(nc, C, dram)
        if upto >= 3:
            with ExitStack() as inner:
                C["g"] = fixed(inner, nc, "c_g", [P, KC, D])
                C["k1"] = fixed(inner, nc, "c_k1", [P, KC, P])
                with ExitStack() as keys:
                    C["wo"] = fixed(keys, nc, "c_wo", [P, KC, D])
                    key_sums(nc, C, dram)
                query_rows(nc, C, dram)
        if upto >= 4:
            C["weight"] = fixed(ctx, nc, "c_weight", [P, 2, NT])
            C["from"] = fixed(ctx, nc, "c_from", [P, NT, 2], I32)
            route(nc, C, dram)
            experts(nc, C, dram)
            combine(nc, C, dram)


def scratch(nc, dram):
    dram["xnT"] = nc.dram_tensor("xnT", (NM, P, KC, MW), F32).ap()
    dram["vtab"] = nc.dram_tensor("vtab", (NP, VW), F32).ap()
    dram["ertab"] = nc.dram_tensor("ertab", (NP, H), F32).ap()
    dram["acc"] = nc.dram_tensor("acc", (NP + NG, AW), F32).ap()
    dram["pen"] = nc.dram_tensor("pen", (NG, GE + 1), F32).ap()
    dram["x1"] = nc.dram_tensor("x1", (NP, D), F32).ap()
    dram["xe"] = nc.dram_tensor("xe", (EX * CAP, D), F32).ap()
    dram["ye"] = nc.dram_tensor("ye", (EX * CAP, D), F32).ap()
    dram["out"] = nc.dram_tensor("out_0_dram", (NP, D), F32, kind="ExternalOutput").ap()


def kernel(**inputs):
    import numpy as np
    import concourse.bacc as bacc
    from concourse.bass_utils import run_bass_kernel_spmd as run

    def given(name):
        return np.ascontiguousarray(inputs[name])

    def batches(edges):
        return np.ascontiguousarray(edges.reshape(ET // BT, BT, P).transpose(0, 2, 1))

    dst = np.pad(given("dst").astype(np.int32), (0, EP - E), constant_values=N)
    src = np.pad(given("src").astype(np.int32), (0, EP - E))
    arrays = {
        "x": np.pad(given("x"), ((0, NP - N), (0, 0))),
        "src_em": batches(src), "dst_em": batches(dst),
        "dst": dst, "dst_before": np.concatenate([np.full(1, -1, np.int32), dst[:-1]]),
        "b1": np.ascontiguousarray(given("L0_ffn_b1").reshape(EX, FC, P).transpose(0, 2, 1)),
    }
    for part in ("gnn", "mix", "ffn"):
        for name in inputs:
            short = name.removeprefix(f"L0_{part}_")
            if short != name and short in _INS and short not in arrays:
                arrays[short] = given(name).reshape(_INS[short])
    nc = bacc.Bacc("TRN2", target_bir_lowering=False, num_devices=1)
    dram = {name: nc.dram_tensor(f"in_{name}", a.shape, mybir.dt.from_np(a.dtype), kind="ExternalInput").ap()
            for name, a in arrays.items()}
    scratch(nc, dram)
    build(nc, dram)
    result = run(nc, [{f"in_{name}": a for name, a in arrays.items()}], core_ids=[0])
    return result.results[0]["out_0_dram"][:N]
```

```python
import math
from contextlib import ExitStack

import concourse.bass as bass
from concourse import mybir

F32 = mybir.dt.float32
I32 = mybir.dt.int32
U32 = mybir.dt.uint32
ALU = mybir.AluOpType
ACT = mybir.ActivationFunctionType
AX = mybir.AxisListType

N, D, H, HF = 6250, 512, 8, 64
P = 128
KC = D // P
TM = 7
NT = -(-N // P)
NM = NT // TM
NP = NT * P
MW = TM * P
HW = MW // 2
assert NM * TM == NT and NM % 2
E = 100000
GT = 4
GE = GT * P
BT = 16
BG = BT // GT
NG = -(-E // (2 * BT * P)) * 2 * BG
ET = NG * GT
EP = ET * P
GH = NG // 2
assert GH <= P
VW = D + H
AW = D + 2 * H
XW = 2 * H + 1
RS = 3
SG = 8
BIG = float(1 << 20)
LOW = -1.0e30
EB = 640
assert NG % SG == 0 and EP * H // P % EB == 0 and BG * GE == BT * P
LN_EPS = 1e-5
SLOPE = 0.2
CLAMP = 50.0
FLOOR = 1e-8
NORM_TOP, NORM_LOW = -0.5 * FLOOR ** 2, math.log(FLOOR)
DEN_LOW = 1e-16
EX, FF = 8, 256
FC = FF // P
CAP = min(N, P * math.ceil(math.ceil(0.3125 * N) / P))
SW = 512
ST = SW // P
assert CAP % (2 * SW) == 0 and NT * EX <= 512


def fixed(ctx, nc, name, shape, dt=F32):
    return ctx.enter_context(nc.sbuf_tensor(name, list(shape), dt))


def psum(ctx, nc, name, cols=512):
    return ctx.enter_context(nc.psum_tensor(name, [P, cols], F32))


def sems(ctx, nc, prefix, names):
    taken = [nc.alloc_semaphore(f"{prefix}_{n}") for n in names.split()]
    ctx.taken += taken
    return taken


class Stage(ExitStack):

    def __init__(self, nc):
        super().__init__()
        self.taken = []

        def give_back():
            nc.clear_and_free_semaphores(self.taken)
            nc.all_engine_barrier()
        self.callback(give_back)


def bc(ap, shape):
    return ap.to_broadcast(list(shape))


def hold(eng, passed):
    eng.sem_inc(passed, 1)


def later(n):
    return not isinstance(n, int) or n > 0


def over_macros(eng, body):
    body(0, 0, 0)
    body(1, 1, 0)
    with eng.Fori(1, NM // 2) as i:
        body(i * 2, 0, i)
        body(i * 2 + 1, 1, i)
    body(NM - 1, 0, NM // 2)


def prep_weights(nc, C, dram):
    with Stage(nc) as ctx:
        wsrc = fixed(ctx, nc, "pw_wsrc", [P, KC, D])
        wdst = fixed(ctx, nc, "pw_wdst", [P, KC, D])
        rows = fixed(ctx, nc, "pw_rows", [P, 4, D])
        prod = fixed(ctx, nc, "pw_prod", [P, 2, D])
        loaded, wv_loaded, zeroed, const, mult, folded, paired = sems(
            ctx, nc, "pw", "loaded wv zeroed const mult folded paired")
        block = ctx.enter_context(nc.Block())

        @block.sync
        def _(sp):
            sp.dma_start(wsrc[:, :, :], dram["W_src"].rearrange("(k p) n -> p k n", p=P)).then_inc(loaded, 16)
            sp.dma_start(wdst[:, :, :], dram["W_dst"].rearrange("(k p) n -> p k n", p=P)).then_inc(loaded, 16)
            for r, name in enumerate(("attn_l", "attn_r", "b_src", "b_dst")):
                sp.dma_start(rows[:, r, :], dram[name].partition_broadcast(P)).then_inc(loaded, 16)
            for k in range(KC):
                sp.dma_start(C["wval"][:, k, 0:D], dram["W_val"][k * P:(k + 1) * P, :]).then_inc(wv_loaded, 16)
            sp.dma_start(C["vbias"][:, 0:D], dram["b_val"].partition_broadcast(P)).then_inc(wv_loaded, 16)
            sp.wait_ge(wv_loaded, 16 * (KC + 1))

        @block.gpsimd
        def _(pool):
            pool.memset(C["ident"][:, :], 0.0).then_inc(zeroed, 1)
            pool.memset(C["before"][:, :], 1.0).then_inc(zeroed, 1)
            pool.memset(C["ones"][:, :], 1.0)
            pool.iota(C["cols"][:, :], [[1, P]], base=0, channel_multiplier=0,
                      allow_small_or_imprecise_dtypes=True).then_inc(const, 1)
            pool.memset(C["after"][:, :], 1.0).then_inc(zeroed, 1)
            pool.wait_ge(zeroed, 3)
            pool.affine_select(out=C["ident"][:, :], in_=C["ident"][:, :], compare_op=ALU.not_equal, fill=1.0,
                               base=0, pattern=[[-1, P]], channel_multiplier=1).then_inc(const, 1)
            pool.affine_select(out=C["before"][:, :], in_=C["before"][:, :], compare_op=ALU.is_gt, fill=0.0,
                               base=0, pattern=[[1, P]], channel_multiplier=-1).then_inc(const, 1)
            pool.affine_select(out=C["after"][:, :], in_=C["after"][:, :], compare_op=ALU.is_gt, fill=0.0,
                               base=0, pattern=[[-1, P]], channel_multiplier=1).then_inc(const, 1)
            pool.memset(C["valid"][:, :], 1.0).then_inc(zeroed, 1)
            pool.wait_ge(zeroed, 4)
            pool.affine_select(out=C["valid"][:, :], in_=C["valid"][:, :], compare_op=ALU.is_gt, fill=0.0,
                               base=N, pattern=[[-P, NT]], channel_multiplier=-1).then_inc(const, 1)
            pool.wait_ge(const, 5)

        @block.vector
        def _(dve):
            nc.vector.memset(C["pair"][:, :], 0.0).then_inc(paired, 1)
            dve.wait_ge(paired, 1)
            nc.vector.memset(C["pair"][0:HF, 0:HF], 1.0)
            nc.vector.memset(C["pair"][HF:P, HF:P], 1.0).then_inc(paired, 1)
            dve.wait_ge(loaded, 6 * 16)
            done = 0
            for k in range(KC):
                for s, w in enumerate((wsrc, wdst)):
                    if done >= 2:
                        dve.wait_ge(folded, done - 1)
                    nc.vector.tensor_tensor(prod[:, s, :], w[:, k, :], rows[:, s, :], ALU.mult).then_inc(mult, 1)
                    dve.wait_ge(mult, done + 1)
                    nc.vector.tensor_reduce(C["wval"][:, k, D + s * H:D + (s + 1) * H],
                                            prod[:, s, :].rearrange("p (h f) -> p h f", f=HF), AX.X, ALU.add).then_inc(folded, 1)
                    done += 1
            for s in range(2):
                dve.wait_ge(folded, done - 1)
                nc.vector.tensor_tensor(prod[:, s, :], rows[:, 2 + s, :], rows[:, s, :], ALU.mult).then_inc(mult, 1)
                dve.wait_ge(mult, done + 1)
                nc.vector.tensor_reduce(C["vbias"][:, D + s * H:D + (s + 1) * H],
                                        prod[:, s, :].rearrange("p (h f) -> p h f", f=HF), AX.X, ALU.add).then_inc(folded, 1)
                done += 1
            dve.wait_ge(folded, done)
            dve.wait_ge(paired, 2)


def norm_stats(nc, C, dram, source, out_stats, prefix):
    with Stage(nc) as ctx:
        xs = fixed(ctx, nc, prefix + "_x", [P, TM, D])
        st = fixed(ctx, nc, prefix + "_st", [P, NT, 6])
        loaded = sems(ctx, nc, prefix, " ".join(f"ld{j}" for j in range(TM)))
        read, stats, aggr = sems(ctx, nc, prefix, "read stats aggr")
        block = ctx.enter_context(nc.Block())
        rows = source.rearrange("(n p) d -> n p d", p=P)

        @block.sync
        def _(sp):
            with sp.Fori(0, NM) as m:
                for j in range(TM):
                    sp.wait_ge(read, m * TM + j + 1)
                    sp.dma_start(xs[:, j, :], rows[m * TM + j]).then_inc(loaded[j], 16)

        @block.vector
        def _(dve):
            dve.sem_inc(read, TM)
            with dve.Fori(0, NM) as m:
                for j in range(TM):
                    dve.wait_ge(loaded[j], m * 16 + 16)
                    nc.vector.bn_stats(st[:, m * TM + j, :], xs[:, j, :]).then_inc(read, 1)
            dve.wait_ge(read, NT + TM)
            for n in range(NT):
                ins = nc.vector.bn_aggr(out_stats[:, n, :], st[:, n, :])
            ins.then_inc(stats, 1)
            dve.wait_ge(stats, 1)
            nc.vector.tensor_scalar(out_stats[:, :, 1], out_stats[:, :, 1], LN_EPS, None, ALU.add).then_inc(aggr, 1)
            dve.wait_ge(aggr, 2)
            nc.vector.reciprocal(out_stats[:, :, 1], out_stats[:, :, 1]).then_inc(aggr, 1)
            dve.wait_ge(aggr, 3)

        @block.scalar
        def _(act):
            act.wait_ge(aggr, 1)
            nc.scalar.activation(out_stats[:, :, 1], out_stats[:, :, 1], ACT.Sqrt).then_inc(aggr, 1)



def project_nodes(nc, C, dram):
    with Stage(nc) as ctx:
        xs = fixed(ctx, nc, "pn_x", [P, TM, D])
        xT = fixed(ctx, nc, "pn_xT", [P, TM, KC, P])
        vr = fixed(ctx, nc, "pn_v", [P, TM, D + 2 * H])
        at = fixed(ctx, nc, "pn_at", [P, TM], I32)
        pT = [psum(ctx, nc, f"pn_pT{i}") for i in range(2)]
        pV = [psum(ctx, nc, f"pn_pV{i}") for i in range(2)]
        pE = [psum(ctx, nc, f"pn_pE{i}") for i in range(2)]
        x_loaded = sems(ctx, nc, "pn", " ".join(f"ld{j}" for j in range(TM)))
        t_stored = sems(ctx, nc, "pn", " ".join(f"ts{j}" for j in range(TM)))
        v_stored = sems(ctx, nc, "pn", " ".join(f"vs{j}" for j in range(TM)))
        normed, turned, kept, projected, biased, passed = sems(ctx, nc, "pn", "normed turned kept projected biased passed")
        block = ctx.enter_context(nc.Block())
        rows = dram["x"].rearrange("(n p) d -> n p d", p=P)
        v_rows = dram["vtab"].rearrange("(n p) w -> n p w", p=P)
        er_rows = dram["ertab"].rearrange("(n p) w -> n p w", p=P)

        @block.sync
        def _(sp):
            def macro(m, q, u):
                for j in range(TM):
                    n = m * TM + j
                    sp.wait_ge(turned, n + 1)
                    sp.dma_start(xs[:, j, :], rows[n]).then_inc(x_loaded[j], 16)
            over_macros(sp, macro)

        @block.gpsimd
        def _(pool):
            def macro(m, q, u):
                for j in range(TM):
                    n = m * TM + j
                    pool.wait_ge(kept, n + 1 + 2)
                    pool.dma_start(dram["xnT"][m, :, :, j * P:(j + 1) * P], xT[:, j, :, :]).then_inc(t_stored[j], 16)
                    pool.wait_ge(biased, n + 1 + 2)
                    hold(pool, passed)
                    pool.dma_start(v_rows[n], vr[:, j, 0:VW]).then_inc(v_stored[j], 16)
                    pool.dma_start(er_rows[n], vr[:, j, VW:VW + H]).then_inc(v_stored[j], 16)
                    pool.indirect_dma_start(out=dram["er_edge"], out_offset=bass.IndirectOffsetOnAxis(ap=at[:, j:j + 1], axis=0),
                                            in_=vr[:, j, VW:VW + H], in_offset=None, bounds_check=EP - 1,
                                            oob_is_err=False).then_inc(v_stored[j], 16)
            over_macros(pool, macro)
            for j in range(TM):
                pool.wait_ge(t_stored[j], 16 * NM)
                pool.wait_ge(v_stored[j], 48 * NM)

        @block.scalar
        def _(act):
            act.sem_inc(kept, 2)

            def macro(m, q, u):
                for j in range(TM):
                    n = m * TM + j
                    act.wait_ge(turned, n + 1 + TM)
                    act.wait_ge(projected, n + 1)
                    if later(m):
                        act.wait_ge(t_stored[j], m * 16)
                    nc.scalar.activation(xT[:, j, :, :].rearrange("p k t -> p (k t)"),
                                         pT[(q + j) % 2][:, :], ACT.Copy).then_inc(kept, 1)
            over_macros(act, macro)

        @block.vector
        def _(dve):
            dve.sem_inc(biased, 2)

            def norm(m, j):
                n = m * TM + j
                dve.wait_ge(x_loaded[j], m * 16 + 16)
                nc.vector.tensor_scalar(xs[:, j, :], xs[:, j, :], C["stats1"][:, n, 0:1], C["stats1"][:, n, 1:2],
                                        ALU.subtract, ALU.mult).then_inc(normed, 1)

            def macro(m, q, u):
                norm(m, 0)
                for j in range(TM):
                    n = m * TM + j
                    if j + 1 < TM:
                        norm(m, j + 1)
                    s = (q + j) % 2
                    dve.wait_ge(projected, n + 1 + TM)
                    if later(m):
                        dve.wait_ge(v_stored[j], m * 48)
                    nc.vector.tensor_copy(at[:, j:j + 1], C["start"][:, bass.ds(n, 1)])
                    nc.vector.tensor_tensor(vr[:, j, 0:D], pV[s][:, :], C["vbias"][:, 0:D], ALU.add)
                    nc.vector.tensor_tensor(vr[:, j, D:D + 2 * H], pE[s][:, 0:2 * H], C["vbias"][:, D:D + 2 * H],
                                            ALU.add).then_inc(biased, 1)
            over_macros(dve, macro)

        @block.tensor
        def _(pe):
            pe.sem_inc(turned, TM)
            pe.sem_inc(projected, TM)

            def turn(m, q, j):
                n = m * TM + j
                pe.wait_ge(normed, n + 1)
                pe.wait_ge(kept, n + 1)
                for k in range(KC):
                    last = nc.tensor.transpose(pT[(q + j) % 2][:, k * P:(k + 1) * P], xs[:, j, k * P:(k + 1) * P],
                                               C["ident"][:, :])
                last.then_inc(turned, 1)

            def macro(m, q, u):
                turn(m, q, 0)
                for j in range(TM):
                    n = m * TM + j
                    if j + 1 < TM:
                        turn(m, q, j + 1)
                    s = (q + j) % 2
                    pe.wait_ge(kept, n + 1 + 2)
                    pe.wait_ge(biased, n + 1)
                    for k in range(KC):
                        nc.tensor.matmul(pV[s][:, :], xT[:, j, k, :], C["wval"][:, k, 0:D],
                                         start=(k == 0), stop=(k == KC - 1))
                    for k in range(KC):
                        last = nc.tensor.matmul(pE[s][:, 0:2 * H], xT[:, j, k, :], C["wval"][:, k, D:D + 2 * H],
                                                start=(k == 0), stop=(k == KC - 1))
                    last.then_inc(projected, 1)
            over_macros(pe, macro)


def prep_edges(nc, C, dram):
    with Stage(nc) as ctx:
        ints = fixed(ctx, nc, "pe_ints", [GH, 2, 2, GE], I32)
        dst = fixed(ctx, nc, "pe_dst", [GH, 2, GE])
        bef = fixed(ctx, nc, "pe_bef", [GH, 2, GE])
        first = fixed(ctx, nc, "pe_first", [GH, 2, GE + 1])
        pen = fixed(ctx, nc, "pe_pen", [GH, 2, GE + 1])
        rank = fixed(ctx, nc, "pe_rank", [GH, 2, GE])
        zero = fixed(ctx, nc, "pe_zero", [GH, GE])
        tgt = fixed(ctx, nc, "pe_tgt", [GH, 2, GE])
        cont = fixed(ctx, nc, "pe_cont", [GH, 2, 3])
        row = fixed(ctx, nc, "pe_row", [GH, 2])
        blank = fixed(ctx, nc, "pe_blank", [P, AW])
        nil = fixed(ctx, nc, "pe_nil", [P, EB])
        wide = fixed(ctx, nc, "pe_wide", [GH, 2, P])
        pw = psum(ctx, nc, "pe_pw")
        pt = [psum(ctx, nc, f"pe_pt{i}") for i in range(2)]
        loaded, rows_made, step, turned, kept, pen_stored, blanks, blanked, widened, spread = sems(
            ctx, nc, "pe", "loaded rows step turned kept pens blanks blanked widened spread")
        block = ctx.enter_context(nc.Block())
        NS = NP + NG
        whole = NS // P * P

        @block.sync
        def _(sp):
            for a, name in enumerate(("dst", "dst_before")):
                for hf in range(2):
                    sp.dma_start(ints[:, a, hf, :], dram[name].rearrange("(c p e) -> c p e", c=2, p=GH)[hf]).then_inc(loaded, 16)
            sp.wait_ge(blanks, 3)
            sp.dma_start(dram["acc"][0:whole, :].rearrange("(n p) w -> p n w", p=P),
                         bc(blank[:, :].unsqueeze(1), [P, whole // P, AW])).then_inc(blanked, 16)
            sp.dma_start(dram["acc"][whole:NS, :], blank[0:NS - whole, :]).then_inc(blanked, 16)
            sp.dma_start(dram["er_edge"].rearrange("(p b) h -> p (b h)", p=P).rearrange("p (n w) -> p n w", w=EB),
                         bc(nil[:, :].unsqueeze(1), [P, EP * H // P // EB, EB])).then_inc(blanked, 16)
            sp.wait_ge(step, 1)
            sp.dma_start(dram["dst_f"].rearrange("(c p) e -> p c e", p=GH), dst[:, :, :]).then_inc(pen_stored, 16)
            sp.wait_ge(step, 6)
            sp.dma_start(dram["pen"].rearrange("(c p) e -> p c e", p=GH), pen[:, :, :]).then_inc(pen_stored, 16)
            sp.wait_ge(pen_stored, 32)
            sp.wait_ge(blanked, 48)

        @block.gpsimd
        def _(pool):
            pool.iota(row[:, :], [[GH, 2]], base=NP, channel_multiplier=1,
                      allow_small_or_imprecise_dtypes=True).then_inc(rows_made, 1)

        @block.vector
        def _(dve):
            nc.vector.memset(blank[:, 0:D + H], 0.0).then_inc(blanks, 1)
            nc.vector.memset(blank[:, D + H:AW], LOW).then_inc(blanks, 1)
            nc.vector.memset(nil[:, :], 0.0).then_inc(blanks, 1)
            nc.vector.memset(zero[:, :], 0.0)
            dve.wait_ge(loaded, 64)
            nc.vector.tensor_copy(dst[:, :, :], ints[:, 0, :, :])
            nc.vector.tensor_copy(bef[:, :, :], ints[:, 1, :, :]).then_inc(step, 1)
            dve.wait_ge(step, 1)
            nc.vector.tensor_tensor(first[:, :, 0:GE], dst[:, :, :], bef[:, :, :], ALU.not_equal)
            nc.vector.tensor_tensor(cont[:, :, 0], dst[:, :, 0], bef[:, :, 0], ALU.is_equal).then_inc(step, 1)
            dve.wait_ge(step, 2)
            dve.wait_ge(rows_made, 1)
            nc.vector.tensor_copy(wide[:, :, :], bc(dst[:, :, 0:1], [GH, 2, P])).then_inc(widened, 1)
            nc.vector.memset(first[:, :, 0:1], 1.0)
            nc.vector.memset(first[:, :, GE:GE + 1], 1.0)
            nc.vector.tensor_tensor(cont[:, :, 1], row[:, :], dst[:, :, 0], ALU.subtract).then_inc(step, 1)
            dve.wait_ge(step, 3)
            for hf in range(2):
                nc.vector.tensor_tensor_scan(rank[:, hf, :], first[:, hf, 0:GE], zero[:, :], -1.0, ALU.add, ALU.max)
            nc.vector.tensor_tensor(cont[:, :, 1], cont[:, :, 1], cont[:, :, 0], ALU.mult).then_inc(step, 1)
            dve.wait_ge(step, 4)
            nc.vector.tensor_scalar(tgt[:, :, :], dst[:, :, :], -BIG, None, ALU.add).then_inc(step, 1)
            dve.wait_ge(step, 5)
            nc.vector.tensor_scalar(pen[:, :, :], first[:, :, :], LOW, None, ALU.mult).then_inc(step, 1)
            nc.vector.tensor_tensor(cont[:, :, 2], tgt[:, :, 0], cont[:, :, 0], ALU.mult).then_inc(step, 1)
            dve.wait_ge(step, 7)
            nc.vector.tensor_scalar(C["own"][:, :], cont[:, :, 2], BIG, None, ALU.add).then_inc(step, 1)
            nc.vector.tensor_tensor(tgt[:, :, 0], tgt[:, :, 0], cont[:, :, 1], ALU.add).then_inc(step, 1)
            dve.wait_ge(step, 9)
            nc.vector.tensor_tensor(tgt[:, :, :], tgt[:, :, :], first[:, :, 0:GE], ALU.mult).then_inc(step, 1)
            dve.wait_ge(spread, 1)
            nc.vector.tensor_copy(C["begin"][:, :], pw[:, 0:NG])
            for t in range(4):
                hf, a = divmod(t, 2)
                dve.wait_ge(turned, t + 1)
                out = (C["rank"], C["target"])[a]
                nc.vector.tensor_copy(out[:, hf * GH * GT:(hf + 1) * GH * GT].rearrange("q (p s) -> q s p", s=GT),
                                      pt[t % 2][:, 0:GT * GH].rearrange("q (s p) -> q s p", s=GT)).then_inc(kept, 1)
            dve.wait_ge(kept, 4)
            nc.vector.tensor_scalar(C["first"][:, :], C["target"][:, :], 0.0, None, ALU.not_equal).then_inc(step, 1)
            dve.wait_ge(step, 11)

        @block.tensor
        def _(pe):
            pe.wait_ge(widened, 1)
            for hf in range(2):
                last = nc.tensor.transpose(pw[:, hf * GH:(hf + 1) * GH], wide[:, hf, :], C["ident"][0:GH, 0:GH])
            last.then_inc(spread, 1)
            pe.wait_ge(step, 10)
            for t in range(4):
                hf, a = divmod(t, 2)
                if t >= 2:
                    pe.wait_ge(kept, t - 1)
                for s in range(GT):
                    last = nc.tensor.transpose(pt[t % 2][:, s * GH:(s + 1) * GH], (rank, tgt)[a][:, hf, s * P:(s + 1) * P],
                                               C["ident"][0:GH, 0:GH])
                last.then_inc(turned, 1)


def find_starts(nc, C, dram):
    with Stage(nc) as ctx:
        ids = fixed(ctx, nc, "fs_ids", [P, NT])
        junk = fixed(ctx, nc, "fs_junk", [P, 2, GE])
        row = fixed(ctx, nc, "fs_row", [P, 2, GE])
        below = fixed(ctx, nc, "fs_below", [P, NT])
        start = fixed(ctx, nc, "fs_start", [P, NT])
        equal = fixed(ctx, nc, "fs_equal", [P, NT])
        group = fixed(ctx, nc, "fs_group", [P, NT])
        count = fixed(ctx, nc, "fs_count", [P, NT, 2])
        some = fixed(ctx, nc, "fs_some", [P, NT])
        ai = fixed(ctx, nc, "fs_ai", [P, 5, NT], I32)
        gi = fixed(ctx, nc, "fs_gi", [P, NT], I32)
        numbered, v, counted, passed = sems(ctx, nc, "fs", "numbered v counted passed")
        fetched = sems(ctx, nc, "fs", "f0 f1")
        block = ctx.enter_context(nc.Block())
        chain = [0]

        @block.gpsimd
        def _(pool):
            pool.iota(ids[:, :], [[P, NT]], base=0, channel_multiplier=1,
                      allow_small_or_imprecise_dtypes=True).then_inc(numbered, 1)
            pool.wait_ge(v, 2 * NT + 2)
            for n in range(NT):
                if n >= 2:
                    pool.wait_ge(counted, 2 * (n - 1))
                pool.indirect_dma_start(out=row[:, n % 2, :], out_offset=None, in_=dram["dst_f"],
                                        in_offset=bass.IndirectOffsetOnAxis(ap=gi[:, n:n + 1], axis=0)).then_inc(fetched[n % 2], 16)

        @block.vector
        def _(dve):
            def link(ins):
                chain[0] += 1
                ins.then_inc(v, 1)
                dve.wait_ge(v, chain[0])

            dve.wait_ge(numbered, 1)
            for n in range(NT):
                for a, (op, out) in enumerate(((ALU.is_lt, below), (ALU.is_equal, equal))):
                    if n:
                        dve.wait_ge(v, 2 * n - 1 + a)
                    nc.vector.tensor_scalar(junk[:, a, 0:NG], C["begin"][:, :], ids[:, n:n + 1], None, op, ALU.add,
                                            accum_out=out[:, n:n + 1]).then_inc(v, 1)
            chain[0] = 2 * NT
            dve.wait_ge(v, 2 * NT)
            link(nc.vector.tensor_scalar(group[:, :], below[:, :], -1.0, 0.0, ALU.add, ALU.max))
            link(nc.vector.tensor_copy(gi[:, :], group[:, :]))
            for n in range(NT):
                dve.wait_ge(fetched[n % 2], 16 * (n // 2) + 16)
                for a, op in enumerate((ALU.is_lt, ALU.is_equal)):
                    if n:
                        dve.wait_ge(counted, 2 * n - 1 + a)
                    nc.vector.tensor_scalar(junk[:, a, :], row[:, n % 2, :], ids[:, n:n + 1], None, op, ALU.add,
                                            accum_out=count[:, n, a:a + 1]).then_inc(counted, 1)
            dve.wait_ge(counted, 2 * NT)
            link(nc.vector.scalar_tensor_tensor(start[:, :], group[:, :], float(GE), count[:, :, 0], ALU.mult, ALU.add))
            link(nc.vector.tensor_tensor(some[:, :], count[:, :, 1], equal[:, :], ALU.add))
            link(nc.vector.tensor_scalar(some[:, :], some[:, :], 0.0, BIG, ALU.is_equal, ALU.mult))
            link(nc.vector.tensor_tensor(start[:, :], start[:, :], some[:, :], ALU.add))
            place_edges(nc, link, start[:, :], ai, C["start"][:, :])


def place_edges(nc, link, edge, ai, out):
    eb, tb, gb = (x.bit_length() - 1 for x in (P, GT, SG))
    link(nc.vector.tensor_copy(ai[:, 0, :], edge))
    nc.vector.tensor_scalar(ai[:, 1, :], ai[:, 0, :], P - 1, tb + gb, ALU.bitwise_and, ALU.logical_shift_left)
    nc.vector.tensor_scalar(ai[:, 3, :], ai[:, 0, :], eb + tb, SG - 1, ALU.logical_shift_right, ALU.bitwise_and)
    link(nc.vector.tensor_scalar(ai[:, 2, :], ai[:, 0, :], eb, GT - 1, ALU.logical_shift_right, ALU.bitwise_and))
    nc.vector.tensor_tensor(ai[:, 1, :], ai[:, 1, :], ai[:, 3, :], ALU.bitwise_or)
    link(nc.vector.tensor_scalar(ai[:, 4, :], ai[:, 2, :], gb, None, ALU.logical_shift_left))
    link(nc.vector.tensor_scalar(ai[:, 0, :], ai[:, 0, :], -SG * GE, None, ALU.bitwise_and))
    link(nc.vector.tensor_tensor(ai[:, 2, :], ai[:, 1, :], ai[:, 4, :], ALU.bitwise_or))
    link(nc.vector.tensor_tensor(out, ai[:, 0, :], ai[:, 2, :], ALU.bitwise_or))


def spread_er(nc, C, dram):
    with Stage(nc) as ctx:
        SE = SG * GT * H
        SR = SG * H
        NS = NG // SG
        EACH = (1 + SG) * 16
        dst = fixed(ctx, nc, "se_dst", [GH, 2], I32)
        num = fixed(ctx, nc, "se_num", [GH, 2])
        ai = fixed(ctx, nc, "se_ai", [GH, 5, 2], I32)
        at = fixed(ctx, nc, "se_at", [GH, 2], I32)
        lead = fixed(ctx, nc, "se_lead", [GH, 2, H])
        raw = fixed(ctx, nc, "se_raw", [P, 2, SE])
        pen = fixed(ctx, nc, "se_pen", [SR, 2, GE])
        go = fixed(ctx, nc, "se_go", [SR, 2, GE])
        er = fixed(ctx, nc, "se_er", [SR, 2, GE])
        pt = [psum(ctx, nc, f"se_pt{i}") for i in range(2)]
        pb = [psum(ctx, nc, f"se_pb{i}") for i in range(2)]
        first, made, v, fetched, led = sems(ctx, nc, "se", "first made v fetched led")
        loaded = sems(ctx, nc, "se", "l0 l1")
        turned, going, spread, back, kept, passed, passed_pe, passed_v = sems(
            ctx, nc, "se", "turned going spread back kept passed passedpe passedv")
        block = ctx.enter_context(nc.Block())

        def steps(eng, body):
            body(0, 0, 0)
            body(1, 1, 0)
            with eng.Fori(1, NS // 2) as i:
                body(i * 2, 0, i)
                body(i * 2 + 1, 1, i)
            if NS % 2:
                body(NS - 1, 0, NS // 2)

        @block.sync
        def _(sp):
            for hf in range(2):
                sp.dma_start(dst[:, hf:hf + 1], dram["dst"].rearrange("(c p e) -> c p e", c=2, p=GH)[hf, :, 0:1],
                             allow_slow_non_contiguous=True).then_inc(first, 16)
            sp.wait_ge(led, 32)

            def step(k, q, u):
                sp.wait_ge(spread, k + 1)
                hold(sp, passed)
                sp.dma_start(raw[:, q, :], er_steps[k]).then_inc(loaded[q], 16)
                for g in range(SG):
                    sp.dma_start(pen[g * H:(g + 1) * H, q, :],
                                 dram["pen"][k * SG + g, 0:GE].partition_broadcast(H)).then_inc(loaded[q], 16)
            er_steps = dram["er_edge"].rearrange("(k p t) h -> k p (t h)", p=P, t=SG * GT)
            steps(sp, step)

        @block.gpsimd
        def _(pool):
            pool.iota(num[:, :], [[GH, 2]], base=0, channel_multiplier=1,
                      allow_small_or_imprecise_dtypes=True).then_inc(made, 1)
            pool.wait_ge(first, 32)
            pool.wait_ge(v, 7)
            for hf in range(2):
                pool.indirect_dma_start(out=lead[:, hf, :], out_offset=None, in_=dram["ertab"],
                                        in_offset=bass.IndirectOffsetOnAxis(ap=dst[:, hf:hf + 1], axis=0)).then_inc(fetched, 16)
            pool.wait_ge(fetched, 32)
            for hf in range(2):
                pool.indirect_dma_start(out=dram["er_edge"], out_offset=bass.IndirectOffsetOnAxis(ap=at[:, hf:hf + 1], axis=0),
                                        in_=lead[:, hf, :], in_offset=None).then_inc(led, 16)

        @block.vector
        def _(dve):
            done = [0]

            def link(ins):
                done[0] += 1
                ins.then_inc(v, 1)
                dve.wait_ge(v, done[0])
            dve.wait_ge(made, 1)
            link(nc.vector.tensor_scalar(num[:, :], num[:, :], float(GE), None, ALU.mult))
            place_edges(nc, link, num[:, :], ai, at[:, :])
            assert done[0] == 7
            dve.sem_inc(spread, 2)

            def step(k, q, u):
                dve.wait_ge(loaded[q], u * EACH + EACH)
                if later(k):
                    dve.wait_ge(back, k)
                nc.vector.tensor_scalar(go[:, q, :], pen[:, q, :], 0.0, None, ALU.is_equal).then_inc(going, 1)
                dve.wait_ge(going, k + 1)
                dve.wait_ge(turned, k + 1)
                nc.vector.tensor_tensor_scan(er[:, q, :], go[:, q, :], pt[q][0:SR, :], 0.0, ALU.mult, ALU.add).then_inc(spread, 1)
            steps(dve, step)

        @block.scalar
        def _(act):
            def step(k, q, u):
                act.wait_ge(back, k + 1 + 1)
                nc.scalar.activation(C["er"][:, bass.ds(k * SG * GT * H, SG * GT * H)].rearrange("p (g s h) -> p s g h", s=GT, h=H),
                                     pb[q][:, 0:SE].rearrange("p (s g h) -> p s g h", s=GT, h=H), ACT.Copy).then_inc(kept, 1)
            act.sem_inc(kept, 2)
            steps(act, step)

        @block.tensor
        def _(pe):
            pe.sem_inc(back, 1)

            def forth(k, q, u):
                pe.wait_ge(loaded[q], u * EACH + EACH)
                pe.wait_ge(spread, k + 1)
                hold(pe, passed_pe)
                for s in range(GT):
                    last = nc.tensor.transpose(pt[q][0:SR, s * P:(s + 1) * P],
                                               raw[:, q, s * SR:(s + 1) * SR], C["ident"][:, :])
                last.then_inc(turned, 1)

            def returned(k, q, u):
                pe.wait_ge(spread, k + 1 + 2)
                pe.wait_ge(kept, k + 1)
                hold(pe, passed_pe)
                for s in range(GT):
                    last = nc.tensor.transpose(pb[q][:, s * SR:(s + 1) * SR], er[:, q, s * P:(s + 1) * P], C["ident"][0:SR, 0:SR])
                last.then_inc(back, 1)

            def step(k, q, u):
                forth(k, q, u)
                returned(k, q, u)
            steps(pe, step)


def edge_attention(nc, C, dram):
    with Stage(nc) as ctx:
        GC = BG * H
        ix = fixed(ctx, nc, "ea_ix", [P, RS, BT], I32)
        rows = fixed(ctx, nc, "ea_rows", [P, RS, BT, VW])
        z = fixed(ctx, nc, "ea_z", [P, BT * H])
        e = fixed(ctx, nc, "ea_e", [P, BT * H])
        pen = fixed(ctx, nc, "ea_pen", [GC, RS, GE + 1])
        run = fixed(ctx, nc, "ea_run", [GC, GE])
        top = fixed(ctx, nc, "ea_top", [GC, GE])
        wt = fixed(ctx, nc, "ea_wt", [GC, GE])
        ext = fixed(ctx, nc, "ea_ext", [P, RS, BT, XW])
        hot = fixed(ctx, nc, "ea_hot", [P, 2, GT, P])
        sums = fixed(ctx, nc, "ea_sums", [P, BG, AW])
        at = fixed(ctx, nc, "ea_at", [P, BG, 1], I32)
        pz = psum(ctx, nc, "ea_pz")
        pb = psum(ctx, nc, "ea_pb")
        pn = [psum(ctx, nc, f"ea_pn{i}") for i in range(2)]
        px = [psum(ctx, nc, f"ea_px{i}") for i in range(2)]
        ix_loaded = sems(ctx, nc, "ea", " ".join(f"ix{q}" for q in range(RS)))
        gathered = sems(ctx, nc, "ea", " ".join(f"ga{q}" for q in range(RS)))
        scattered = sems(ctx, nc, "ea", " ".join(f"sc{g}" for g in range(BG)))
        (raw, scored, turned, ran, topped, scanned, weighted, back, extras, scaled, hotted, grouped,
         evacuated) = sems(ctx, nc, "ea", "raw scored turned ran topped scanned weighted back extras scaled hotted "
                                          "grouped evacuated")
        pool_passed, sp_passed, pe_passed = sems(ctx, nc, "ea", "pool_passed sp_passed pe_passed")
        block = ctx.enter_context(nc.Block())
        NB = -(-E // (BT * P))
        LOOPS = NB // RS
        assert NB == LOOPS * RS + 1
        GS = BT * 16

        def pipelined(eng, head, step):
            head(0, 0, 0)
            for q in range(RS):
                step(q, q, 0, True)
            with eng.Fori(1, LOOPS) as i:
                for q in range(RS):
                    step(i * RS + q, q, i, True)
            step(NB - 1, 0, LOOPS, False)

        def after(q, u):
            return (q + 1, u) if q + 1 < RS else (0, u + 1)

        @block.sync
        def _(sp):
            def batch(b, q, u):
                if later(u):
                    sp.wait_ge(gathered[q], u * GS)
                hold(sp, sp_passed)
                sp.wait_ge(scanned, b + 1)
                hold(sp, sp_passed)
                sp.dma_start(ix[:, q, :], dram["src_em"][b]).then_inc(ix_loaded[q], 16)
                for g in range(BG):
                    sp.dma_start(pen[g * H:(g + 1) * H, q, :],
                                 dram["pen"][b * BG + g, :].partition_broadcast(H)).then_inc(ix_loaded[q], 16)
            for q in range(RS):
                batch(q, q, 0)
            with sp.Fori(1, LOOPS) as i:
                for q in range(RS):
                    batch(i * RS + q, q, i)
            batch(NB - 1, 0, LOOPS)

        @block.gpsimd
        def _(pool):
            def gather(b, q, u, full, old):
                pool.wait_ge(ix_loaded[q], u * 80 + 80)
                hold(pool, pool_passed)
                for t in range(BT):
                    if full and t % GT == 0:
                        pool.wait_ge(grouped, (b - RS) * BG + t // GT + 1 + 2)
                        hold(pool, pool_passed)
                    pool.indirect_dma_start(out=rows[:, q, t, :], out_offset=None, in_=dram["vtab"],
                                            in_offset=bass.IndirectOffsetOnAxis(ap=ix[:, q, t:t + 1], axis=0)).then_inc(gathered[q], 16)
                    if old and t % GT == GT - 1 and t >= GT:
                        scatter(b - 2, t // GT - 1)
                if old:
                    scatter(b - 2, BG - 1)

            def scatter(b, g):
                pool.wait_ge(evacuated, b * BG + g + 1 + 2)
                hold(pool, pool_passed)
                pool.indirect_dma_start(out=dram["acc"], out_offset=bass.IndirectOffsetOnAxis(ap=at[:, g, 0:1], axis=0),
                                        in_=sums[:, g, :], in_offset=None, bounds_check=NP + NG - 1,
                                        oob_is_err=False).then_inc(scattered[g], 16)
            for q in range(RS):
                gather(q, q, 0, False, q >= 2)
            with pool.Fori(1, LOOPS) as i:
                for q in range(RS):
                    gather(i * RS + q, q, i, True, True)
            gather(NB - 1, 0, LOOPS, True, True)
            for b in (NB - 2, NB - 1):
                for g in range(BG):
                    scatter(b, g)
            for g in range(BG):
                pool.wait_ge(scattered[g], NB * 16)

        @block.vector
        def _(dve):
            dve.sem_inc(scanned, RS)

            def score(b, q, u):
                dve.wait_ge(gathered[q], u * GS + GS)
                nc.vector.tensor_tensor(z[:, :].rearrange("p (s g h) -> p s g h", s=GT, g=BG),
                                        rows[:, q, :, D:VW].rearrange("p (g s) h -> p s g h", s=GT),
                                        C["er"][:, bass.ds(b * (BT * H), BT * H)].rearrange("p (g s h) -> p s g h", s=GT, h=H), ALU.add).then_inc(raw, 1)
                dve.wait_ge(raw, b + 1)
                nc.vector.scalar_tensor_tensor(e[:, :], z[:, :], SLOPE, z[:, :], ALU.mult, ALU.max).then_inc(scored, 1)

            def scan(b, q, u):
                dve.wait_ge(turned, b + 1)
                dve.wait_ge(ix_loaded[q], u * 80 + 80)
                nc.vector.tensor_tensor_scan(run[:, :], pen[:, q, 0:GE], pz[0:GC, :], LOW, ALU.add, ALU.max).then_inc(ran, 1)
                dve.wait_ge(ran, b + 1)
                nc.vector.tensor_tensor_scan(top[:, ::-1], pen[:, q, GE:0:-1], run[:, ::-1], LOW,
                                             ALU.add, ALU.max).then_inc(topped, 1)
                dve.wait_ge(topped, b + 1)
                nc.vector.tensor_tensor(wt[:, :], pz[0:GC, :], top[:, :], ALU.subtract).then_inc(scanned, 1)

            def extend(b, q):
                dve.wait_ge(back, b + 1)
                nc.vector.tensor_copy(ext[:, q, :, 0:H].rearrange("p (g s) h -> p s g h", s=GT),
                                      pb[:, 0:BT * H].rearrange("p (s g h) -> p s g h", s=GT, g=BG))
                nc.vector.tensor_tensor(ext[:, q, :, H:2 * H].rearrange("p (g s) h -> p s g h", s=GT),
                                        pb[:, BT * H:2 * BT * H].rearrange("p (s g h) -> p s g h", s=GT, g=BG),
                                        bc(C["first"][:, bass.ds(b * BT, BT)].rearrange("p (g s) -> p s g", s=GT).unsqueeze(3),
                                           [P, GT, BG, H]), ALU.mult)
                nc.vector.tensor_copy(ext[:, q, :, 2 * H], C["target"][:, bass.ds(b * BT, BT)]).then_inc(extras, 1)

            def scale(b, q, g):
                n = b * BG + g
                part = rows[:, q, g * GT:(g + 1) * GT, 0:D].rearrange("p s (h f) -> p s h f", f=HF)
                nc.vector.tensor_tensor(part, part, bc(ext[:, q, g * GT:(g + 1) * GT, 0:H].unsqueeze(3), [P, GT, H, HF]),
                                        ALU.mult).then_inc(scaled, 1)
                dve.wait_ge(grouped, n + 1)
                nc.vector.tensor_tensor(hot[:, g % 2, :, :], bc(C["cols"][:, :].unsqueeze(1), [P, GT, P]),
                                        bc(C["rank"][:, bass.ds(n * GT, GT)].unsqueeze(2), [P, GT, P]),
                                        ALU.is_equal).then_inc(hotted, 1)

            def head(b, q, u):
                score(b, q, u)
                scan(b, q, u)
                extend(b, q)

            def step(b, q, u, more):
                nq, nu = after(q, u)
                dve.wait_ge(extras, b + 1)
                scale(b, q, 0)
                if more:
                    score(b + 1, nq, nu)
                scale(b, q, 1)
                if more:
                    scan(b + 1, nq, nu)
                scale(b, q, 2)
                scale(b, q, 3)
                if more:
                    extend(b + 1, nq)
            pipelined(dve, head, step)

        @block.scalar
        def _(act):
            act.sem_inc(evacuated, 2)

            def head(b, q, u):
                act.wait_ge(scanned, b + 1 + RS)
                nc.scalar.activation(wt[:, :], wt[:, :], ACT.Exp).then_inc(weighted, 1)

            def step(b, q, u, more):
                nq, nu = after(q, u)
                for g in range(BG):
                    n = b * BG + g
                    act.wait_ge(grouped, n + 1 + 2)
                    if later(b):
                        act.wait_ge(scattered[g], b * 16)
                    nc.scalar.activation(sums[:, g, 0:D], pn[g % 2][:, :], ACT.Copy)
                    nc.scalar.activation(sums[:, g, D:AW], px[g % 2][:, 0:2 * H], ACT.Copy)
                    nc.scalar.activation(at[:, g, :], px[g % 2][:, 2 * H:XW], ACT.Copy, bias=BIG).then_inc(evacuated, 1)
                    if g == 0 and more:
                        head(b + 1, nq, nu)
            pipelined(act, head, step)

        @block.tensor
        def _(pe):
            pe.sem_inc(grouped, 2)

            def forth(b, q):
                pe.wait_ge(scored, b + 1)
                pe.wait_ge(scanned, b + RS)
                for s in range(GT):
                    last = nc.tensor.transpose(pz[0:GC, s * P:(s + 1) * P], e[:, s * GC:(s + 1) * GC], C["ident"][:, :])
                last.then_inc(turned, 1)

            def returned(b, q):
                pe.wait_ge(weighted, b + 1)
                if later(b):
                    pe.wait_ge(extras, b)
                hold(pe, pe_passed)
                for a, src in enumerate((wt, top)):
                    for s in range(GT):
                        last = nc.tensor.transpose(pb[:, a * BT * H + s * GC:a * BT * H + (s + 1) * GC],
                                                   src[:, s * P:(s + 1) * P], C["ident"][0:GC, 0:GC])
                last.then_inc(back, 1)

            def head(b, q, u):
                forth(b, q)
                returned(b, q)

            def step(b, q, u, more):
                nq, nu = after(q, u)
                for g in range(BG):
                    n = b * BG + g
                    pe.wait_ge(scaled, n + 1)
                    pe.wait_ge(hotted, n + 1)
                    pe.wait_ge(evacuated, n + 1)
                    for s in range(GT):
                        t = g * GT + s
                        nc.tensor.matmul(pn[g % 2][:, :], hot[:, g % 2, s, :], rows[:, q, t, 0:D], start=(s == 0), stop=(s == GT - 1))
                        last = nc.tensor.matmul(px[g % 2][:, 0:XW], hot[:, g % 2, s, :], ext[:, q, t, :],
                                                start=(s == 0), stop=(s == GT - 1))
                    last.then_inc(grouped, 1)
                    if g == 0 and more:
                        forth(b + 1, nq)
                    if g == 2 and more:
                        returned(b + 1, nq)
            pipelined(pe, head, step)


def merge_groups(nc, C, dram):
    with Stage(nc) as ctx:
        part = fixed(ctx, nc, "mg_part", [GH, AW])
        own = fixed(ctx, nc, "mg_own", [GH, AW])
        wide = fixed(ctx, nc, "mg_wide", [GH, H + 1, GH])
        same = fixed(ctx, nc, "mg_same", [GH, GH])
        off = fixed(ctx, nc, "mg_off", [GH, GH])
        work = fixed(ctx, nc, "mg_work", [GH, H, GH])
        peak = fixed(ctx, nc, "mg_peak", [GH, 4, H])
        lead = fixed(ctx, nc, "mg_lead", [GH, 4])
        ids = fixed(ctx, nc, "mg_ids", [GH, 2, 1], I32)
        out = fixed(ctx, nc, "mg_out", [GH, AW])
        pt = [psum(ctx, nc, f"mg_pt{i}") for i in range(3)]
        pn = psum(ctx, nc, "mg_pn")
        px = psum(ctx, nc, "mg_px")
        loaded, fetched, stored, v, t, s, m = sems(ctx, nc, "mg", "loaded fetched stored v t s m")
        block = ctx.enter_context(nc.Block())

        V = 13

        @block.sync
        def _(sp):
            for hf in range(2):
                if hf:
                    sp.wait_ge(v, V)
                sp.dma_start(part[:, :], dram["acc"][NP + hf * GH:NP + (hf + 1) * GH, :]).then_inc(loaded, 16)

        @block.gpsimd
        def _(pool):
            for hf in range(2):
                pool.wait_ge(v, V * hf + 1)
                pool.indirect_dma_start(out=own[:, :], out_offset=None, in_=dram["acc"],
                                        in_offset=bass.IndirectOffsetOnAxis(ap=ids[:, 0, :], axis=0),
                                        bounds_check=NP - 1, oob_is_err=False).then_inc(fetched, 16)
                pool.wait_ge(v, V * (hf + 1))
                pool.indirect_dma_start(out=dram["acc"], out_offset=bass.IndirectOffsetOnAxis(ap=ids[:, 1, :], axis=0),
                                        in_=out[:, :], in_offset=None, bounds_check=NP - 1,
                                        oob_is_err=False).then_inc(stored, 16)
                pool.wait_ge(stored, 16 * (hf + 1))

        @block.scalar
        def _(act):
            for hf in range(2):
                act.wait_ge(v, V * hf + 9)
                nc.scalar.activation(peak[:, 2:4, :], peak[:, 2:4, :], ACT.Exp).then_inc(s, 1)

        @block.vector
        def _(dve):
            done = [0]

            def link(ins):
                done[0] += 1
                ins.then_inc(v, 1)
                dve.wait_ge(v, done[0])

            for hf in range(2):
                if hf:
                    dve.wait_ge(stored, 16)
                nc.vector.tensor_copy(ids[:, 0, :], C["own"][:, hf:hf + 1])
                link(nc.vector.memset(own[:, :], 0.0))
                dve.wait_ge(loaded, 16 * (hf + 1))
                nc.vector.tensor_copy(wide[:, 0:H, :], bc(part[:, D + H:AW].unsqueeze(2), [GH, H, GH]))
                link(nc.vector.tensor_copy(wide[:, H, :], bc(C["own"][:, hf:hf + 1], [GH, GH])))
                dve.wait_ge(t, hf + 1)
                link(nc.vector.tensor_scalar(same[:, :], pt[2][0:GH, 0:GH], C["own"][:, hf:hf + 1], None, ALU.is_equal))
                nc.vector.tensor_scalar(off[:, :], same[:, :], -1.0, -LOW, ALU.add, ALU.mult)
                for b in range(2):
                    last = nc.vector.tensor_tensor(work[:, 4 * b:4 * b + 4, :], pt[b][0:GH, 0:4 * GH].rearrange("p (h c) -> p h c", h=4),
                                                   bc(same[:, :].unsqueeze(1), [GH, 4, GH]), ALU.mult)
                link(last)
                link(nc.vector.tensor_tensor(work[:, :, :], work[:, :, :], bc(off[:, :].unsqueeze(1), [GH, H, GH]), ALU.add))
                link(nc.vector.tensor_reduce(peak[:, 0, :], work[:, :, :], AX.X, ALU.max))
                dve.wait_ge(fetched, 16 * (hf + 1))
                link(nc.vector.tensor_tensor(peak[:, 1, :], peak[:, 0, :], own[:, D + H:AW], ALU.max))
                nc.vector.tensor_tensor(peak[:, 2, :], part[:, D + H:AW], peak[:, 1, :], ALU.subtract)
                nc.vector.tensor_tensor(off[:, :], same[:, :], C["after"][0:GH, 0:GH], ALU.mult)
                link(nc.vector.tensor_copy(out[:, D + H:AW], peak[:, 1, :]))
                nc.vector.tensor_reduce(lead[:, 0:1], off[:, :], AX.X, ALU.add)
                link(nc.vector.tensor_tensor(peak[:, 3, :], own[:, D + H:AW], peak[:, 1, :], ALU.subtract))
                dve.wait_ge(s, hf + 1)
                nc.vector.tensor_tensor(part[:, D:D + H], part[:, D:D + H], peak[:, 2, :], ALU.mult)
                nc.vector.tensor_scalar(lead[:, 1:2], lead[:, 0:1], BIG, None, ALU.mult)
                nc.vector.tensor_tensor(own[:, D:D + H], own[:, D:D + H], peak[:, 3, :], ALU.mult)
                nc.vector.tensor_tensor(own[:, 0:D].rearrange("p (h f) -> p h f", f=HF), own[:, 0:D].rearrange("p (h f) -> p h f", f=HF),
                                        bc(peak[:, 3, :].unsqueeze(2), [GH, H, HF]), ALU.mult)
                link(nc.vector.tensor_tensor(part[:, 0:D].rearrange("p (h f) -> p h f", f=HF), part[:, 0:D].rearrange("p (h f) -> p h f", f=HF),
                                             bc(peak[:, 2, :].unsqueeze(2), [GH, H, HF]), ALU.mult))
                link(nc.vector.tensor_tensor(lead[:, 2:3], lead[:, 1:2], C["own"][:, hf:hf + 1], ALU.add))
                dve.wait_ge(m, hf + 1)
                nc.vector.tensor_copy(ids[:, 1, :], lead[:, 2:3])
                nc.vector.tensor_tensor(out[:, D:D + H], px[0:GH, 0:H], own[:, D:D + H], ALU.add)
                link(nc.vector.tensor_tensor(out[:, 0:D], pn[0:GH, :], own[:, 0:D], ALU.add))
                link(nc.vector.memset(lead[:, 3:4], 0.0))
            assert done[0] == 2 * V

        @block.tensor
        def _(pe):
            for hf in range(2):
                pe.wait_ge(v, V * hf + 2)
                for h in range(H + 1):
                    last = nc.tensor.transpose(pt[h // 4][0:GH, (h % 4) * GH:(h % 4 + 1) * GH], wide[:, h, :], C["ident"][0:GH, 0:GH])
                last.then_inc(t, 1)
                pe.wait_ge(v, V * hf + 10)
                nc.tensor.matmul(pn[0:GH, :], same[:, :], part[:, 0:D], start=True, stop=True)
                nc.tensor.matmul(px[0:GH, 0:H], same[:, :], part[:, D:D + H], start=True, stop=True).then_inc(m, 1)


def load_feature_maps(nc, sp, tile, omega, loaded):
    sp.dma_start(tile[0:HF, 0:HF], omega).then_inc(loaded, 16)
    sp.dma_start(tile[HF:P, HF:P], omega).then_inc(loaded, 16)


def key_sums(nc, C, dram):
    with Stage(nc) as ctx:
        xT = fixed(ctx, nc, "ks_xT", [P, 2, KC, MW])
        wk = fixed(ctx, nc, "ks_wk", [P, KC, D])
        wv = fixed(ctx, nc, "ks_wv", [P, KC, D])
        omega = fixed(ctx, nc, "ks_omega", [P, P])
        half = fixed(ctx, nc, "ks_half", [P, 2])
        kT = fixed(ctx, nc, "ks_kT", [P, KC, MW])
        k2 = fixed(ctx, nc, "ks_k2", [P, KC, MW])
        nrm = fixed(ctx, nc, "ks_nrm", [P, 2, H])
        feat = fixed(ctx, nc, "ks_feat", [P, 2, D])
        phi = fixed(ctx, nc, "ks_phi", [P, 2, D])
        vm = fixed(ctx, nc, "ks_vm", [P, 2, D])
        kv = fixed(ctx, nc, "ks_kv", [P, KC, P])
        k1 = fixed(ctx, nc, "ks_k1", [P, KC])
        pk = [psum(ctx, nc, f"ks_pk{i}") for i in range(2)]
        pf = psum(ctx, nc, "ks_pf")
        pq = psum(ctx, nc, "ks_pq")
        pv = [psum(ctx, nc, f"ks_pv{i}") for i in range(2)]
        pkv = psum(ctx, nc, "ks_pkv")
        pk1 = psum(ctx, nc, "ks_pone")
        loaded, wloaded, set_up = sems(ctx, nc, "ks", "loaded wloaded setup")
        x_loaded = sems(ctx, nc, "ks", "x0 x1")
        (projected, kept, featured, normed, bounded, valued, cleared, mapped, copied, added, drained, masked, multiplied,
         moved, passed) = sems(ctx, nc, "ks", "projected kept featured normed bounded valued cleared mapped copied added "
                                              "drained masked multiplied moved passed")
        block = ctx.enter_context(nc.Block())
        NC = 2 * KC

        @block.sync
        def _(sp):
            for w, name in ((wk, "Wk"), (wv, "Wv"), (C["wo"], "Wo")):
                sp.dma_start(w[:, :, :], dram[name].rearrange("(k p) n -> p k n", p=P)).then_inc(wloaded, 16)
            sp.wait_ge(set_up, 1)
            load_feature_maps(nc, sp, omega, dram["omega_k"], loaded)

            sp.dma_start(xT[:, 0, :, :], dram["xnT"][0]).then_inc(x_loaded[0], 16)
            sp.dma_start(xT[:, 1, :, :], dram["xnT"][1]).then_inc(x_loaded[1], 16)
            with sp.Fori(0, (NM - 3) // 2) as i:
                for q in range(2):
                    sp.wait_ge(valued, (i * 2 + q + 1) * TM)
                    hold(sp, passed)
                    sp.dma_start(xT[:, q, :, :], dram["xnT"][i * 2 + q + 2]).then_inc(x_loaded[q], 16)
            sp.wait_ge(valued, (NM - 2) * TM)
            sp.dma_start(xT[:, 0, :, :], dram["xnT"][NM - 1]).then_inc(x_loaded[0], 16)

        @block.scalar
        def _(act):
            act.sem_inc(copied, 1)
            act.sem_inc(mapped, 1)

            def macro(m, q, u):
                if later(m):
                    act.wait_ge(normed, m * TM)
                for c in range(NC):
                    n = m * NC + c
                    hf, k = divmod(c, KC)
                    act.wait_ge(projected, n + 1)
                    nc.scalar.activation(kT[:, k, hf * HW:(hf + 1) * HW], pk[c % 2][:, 0:HW], ACT.Copy)
                    nc.scalar.activation(k2[:, k, hf * HW:(hf + 1) * HW], pk[c % 2][:, 0:HW], ACT.Square).then_inc(kept, 1)
                for j in range(TM):
                    n = m * TM + j
                    s = (q + j) % 2
                    act.wait_ge(valued, n + 1)
                    if later(n):
                        act.wait_ge(added, n)
                    nc.scalar.activation(vm[:, s, :], pv[s][:, :], ACT.Copy).then_inc(copied, 1)
                    act.wait_ge(featured, n + 1)
                    nc.scalar.activation(phi[:, s, :], feat[:, s, :], ACT.Exp).then_inc(mapped, 1)
            over_macros(act, macro)

        @block.vector
        def _(dve):
            nc.vector.memset(omega[:, :], 0.0).then_inc(set_up, 1)
            nc.vector.memset(half[:, :], 0.0).then_inc(moved, 1)
            nc.vector.memset(kv[:, :, :], 0.0)
            nc.vector.memset(k1[:, :], 0.0).then_inc(moved, 1)
            dve.wait_ge(moved, 2)
            nc.vector.memset(half[0:HF, 0:1], -0.5 / HF)
            nc.vector.memset(half[HF:P, 1:2], -0.5 / HF).then_inc(moved, 1)
            dve.wait_ge(loaded, 32)
            nc.vector.tensor_scalar(omega[:, :], omega[:, :], HF ** -0.5, None, ALU.mult).then_inc(set_up, 1)

            def macro(m, q, u):
                for j in range(TM):
                    n = m * TM + j
                    s = (q + j) % 2
                    dve.wait_ge(normed, n + 1)
                    nc.vector.tensor_scalar(nrm[:, s, :], pq[:, 0:H], NORM_TOP, NORM_LOW, ALU.min, ALU.max).then_inc(bounded, 1)
                    dve.wait_ge(bounded, n + 1)
                    if later(n):
                        dve.wait_ge(mapped, n)
                    nc.vector.scalar_tensor_tensor(feat[:, s, :].rearrange("p (h f) -> p h f", f=HF),
                                                   pf[:, :].rearrange("p (h f) -> p h f", f=HF), CLAMP,
                                                   bc(nrm[:, s, :].unsqueeze(2), [P, H, HF]), ALU.min, ALU.add).then_inc(featured, 1)
                dve.wait_ge(added, m * TM + TM + 1)
                nc.vector.tensor_tensor(kv[:, :, :].rearrange("p k c -> p (k c)"), kv[:, :, :].rearrange("p k c -> p (k c)"),
                                        pkv[:, :], ALU.add)
                nc.vector.tensor_tensor(k1[:, :], k1[:, :], pk1[:, 0:KC], ALU.add).then_inc(drained, 1)
            over_macros(dve, macro)
            dve.wait_ge(drained, NM)
            nc.vector.tensor_tensor(kv[:, :, :], kv[:, :, :], bc(C["pair"][:, :].unsqueeze(1), [P, KC, P]), ALU.mult)
            nc.vector.tensor_tensor(C["k1"][:, :, :], bc(k1[:, :].unsqueeze(2), [P, KC, P]),
                                    bc(C["pair"][:, :].unsqueeze(1), [P, KC, P]), ALU.mult).then_inc(masked, 1)
            for c in range(KC):
                dve.wait_ge(multiplied, c + 1)
                nc.vector.tensor_copy(C["g"][:, c, :], pk[c % 2][:, :]).then_inc(cleared, 1)
            dve.wait_ge(cleared, KC)

        @block.tensor
        def _(pe):
            pe.sem_inc(added, 1)
            pe.wait_ge(wloaded, 48)
            pe.wait_ge(set_up, 2)
            pe.wait_ge(moved, 3)

            def add(m, q, j):
                n = m * TM + j
                s = (q + j) % 2
                pe.wait_ge(copied, n + 1 + 1)
                pe.wait_ge(mapped, n + 1 + 1)
                if j == 0:
                    if later(m):
                        pe.wait_ge(drained, m)
                for c in range(KC):
                    nc.tensor.matmul(pkv[:, c * P:(c + 1) * P], vm[:, s, c * P:(c + 1) * P], phi[:, s, c * P:(c + 1) * P],
                                     start=(j == 0 and c == 0), stop=(j == TM - 1), skip_group_check=True)
                for c in range(KC):
                    last = nc.tensor.matmul(pk1[:, c:c + 1], phi[:, s, c * P:(c + 1) * P], C["valid"][:, bass.ds(n, 1)],
                                            start=(j == 0 and c == 0), stop=(j == TM - 1), skip_group_check=True)
                last.then_inc(added, 1)

            def macro(m, q, u):
                pe.wait_ge(x_loaded[q], u * 16 + 16)
                for c in range(NC):
                    n = m * NC + c
                    hf, kk = divmod(c, KC)
                    if c >= 2:
                        pe.wait_ge(kept, n - 1)
                    else:
                        if later(m):
                            pe.wait_ge(kept, m * NC)
                    for k in range(KC):
                        last = nc.tensor.matmul(pk[c % 2][:, 0:HW], wk[:, k, kk * P:(kk + 1) * P],
                                                xT[:, q, k, hf * HW:(hf + 1) * HW], start=(k == 0), stop=(k == KC - 1))
                    last.then_inc(projected, 1)
                for j in range(TM):
                    n = m * TM + j
                    s = (q + j) % 2
                    t = slice(j * P, (j + 1) * P)
                    if later(n):
                        pe.wait_ge(copied, n)
                    for k in range(KC):
                        last = nc.tensor.matmul(pv[s][:, :], xT[:, q, k, t], wv[:, k, :], start=(k == 0), stop=(k == KC - 1))
                    last.then_inc(valued, 1)
                    pe.wait_ge(kept, m * NC + NC)
                    if later(n):
                        pe.wait_ge(featured, n)
                    for c in range(KC):
                        nc.tensor.matmul(pf[:, c * P:(c + 1) * P], kT[:, c, t], omega[:, :], start=True, stop=True)
                    for c in range(KC):
                        last = nc.tensor.matmul(pq[:, 2 * c:2 * c + 2], k2[:, c, t], half[:, :], start=True, stop=True)
                    last.then_inc(normed, 1)
                    if j:
                        add(m, q, j - 1)
                add(m, q, TM - 1)
            over_macros(pe, macro)
            pe.wait_ge(masked, 1)
            for c in range(KC):
                if c >= 2:
                    pe.wait_ge(cleared, c - 1)
                nc.tensor.matmul(pk[c % 2][:, :], kv[:, c, :], C["wo"][:, c, :], start=True, stop=True).then_inc(multiplied, 1)


def query_rows(nc, C, dram):
    with Stage(nc) as ctx:
        xT = fixed(ctx, nc, "qr_xT", [P, 2, KC, MW])
        wq = fixed(ctx, nc, "qr_wq", [P, KC, D])
        omega = fixed(ctx, nc, "qr_omega", [P, P])
        half = fixed(ctx, nc, "qr_half", [P, P])
        qT = fixed(ctx, nc, "qr_qT", [P, 2, HW])
        q2 = fixed(ctx, nc, "qr_q2", [P, 2, HW])
        nrm = fixed(ctx, nc, "qr_nrm", [P, 2, HW])
        phi = fixed(ctx, nc, "qr_phi", [P, 2, HW])
        rec = fixed(ctx, nc, "qr_rec", [P, 2, HW])
        phin = fixed(ctx, nc, "qr_phin", [P, KC, MW])
        xs = fixed(ctx, nc, "qr_x", [P, 2, D])
        ac = fixed(ctx, nc, "qr_ac", [P, 2, AW])
        rden = fixed(ctx, nc, "qr_rden", [P, 2, 2, H])
        x1 = fixed(ctx, nc, "qr_x1", [P, 2, D])
        st = fixed(ctx, nc, "qr_st", [P, 2, 6])
        agg = fixed(ctx, nc, "qr_agg", [P, 2, 2])
        pq = [psum(ctx, nc, f"qr_pq{i}") for i in range(2)]
        pf = psum(ctx, nc, "qr_pf")
        pn = psum(ctx, nc, "qr_pn")
        pd = [psum(ctx, nc, f"qr_pd{i}") for i in range(2)]
        pm = [psum(ctx, nc, f"qr_pm{i}") for i in range(2)]
        loaded, wloaded, set_up = sems(ctx, nc, "qr", "loaded wloaded setup")
        x_loaded = sems(ctx, nc, "qr", "x0 x1")
        r_loaded = sems(ctx, nc, "qr", "r0 r1")
        stored = sems(ctx, nc, "qr", "s0 s1")
        (projected, kept, featured, bounded, argued, mapped, summed, inverted, divided, mixed, used, dens, rdens,
         graphed, based, finished, rooted, counted, joined, passed, passed_v) = sems(
            ctx, nc, "qr", "projected kept featured bounded argued mapped summed inverted divided mixed used dens rdens "
                           "graphed based finished rooted counted joined passed passedv")
        block = ctx.enter_context(nc.Block())
        NC = 2 * KC
        rows = dram["x"].rearrange("(n p) d -> n p d", p=P)
        acc = dram["acc"][0:NP, :].rearrange("(n p) w -> n p w", p=P)
        x1_rows = dram["x1"].rearrange("(n p) d -> n p d", p=P)

        @block.sync
        def _(sp):
            sp.dma_start(wq[:, :, :], dram["Wq"].rearrange("(k p) n -> p k n", p=P)).then_inc(wloaded, 16)
            sp.wait_ge(set_up, 1)
            load_feature_maps(nc, sp, omega, dram["omega_q"], loaded)

            def macro(m, q, u):
                for j in range(TM):
                    n = m * TM + j
                    s = (q + j) % 2
                    sp.wait_ge(finished, n + 1)
                    hold(sp, passed)
                    sp.dma_start(xs[:, s, :], rows[n]).then_inc(r_loaded[s], 16)
                    sp.dma_start(ac[:, s, :], acc[n]).then_inc(r_loaded[s], 16)

            def transposed(m, q):
                sp.dma_start(xT[:, q, :, :], dram["xnT"][m]).then_inc(x_loaded[q], 16)
            transposed(0, 0)

            def pair(i):
                transposed(i * 2 + 1, 1)
                macro(i * 2, 0, i)
                sp.wait_ge(projected, (i * 2 + 1) * NC + 2)
                hold(sp, passed)
                transposed(i * 2 + 2, 0)
                macro(i * 2 + 1, 1, i)
                sp.wait_ge(projected, (i * 2 + 2) * NC + 2)
                hold(sp, passed)
            pair(0)
            with sp.Fori(1, NM // 2) as i:
                pair(i)
            macro(NM - 1, 0, NM // 2)

        @block.gpsimd
        def _(pool):
            def macro(m, q, u):
                for j in range(TM):
                    n = m * TM + j
                    s = (q + j) % 2
                    pool.wait_ge(finished, n + 1 + 2)
                    pool.dma_start(x1_rows[n], x1[:, s, :]).then_inc(stored[s], 16)
            over_macros(pool, macro)
            pool.wait_ge(stored[0], 16 * ((NT + 1) // 2))
            pool.wait_ge(stored[1], 16 * (NT // 2))

        @block.scalar
        def _(act):
            act.sem_inc(kept, 2)
            act.sem_inc(mapped, 2)

            def macro(m, q, u):
                for c in range(NC):
                    n = m * NC + c
                    act.wait_ge(projected, n + 1 + 2)
                    act.wait_ge(featured, n + 1)
                    nc.scalar.activation(qT[:, c % 2, :], pq[c % 2][:, 0:HW], ACT.Copy)
                    nc.scalar.activation(q2[:, c % 2, :], pq[c % 2][:, 0:HW], ACT.Square).then_inc(kept, 1)
                    act.wait_ge(argued, n + 1 + 2)
                    act.wait_ge(divided, n + 1)
                    nc.scalar.activation(phi[:, c % 2, :], nrm[:, c % 2, :], ACT.Exp).then_inc(mapped, 1)
            over_macros(act, macro)
            act.wait_ge(counted, 1)
            nc.scalar.activation(C["stats2"][:, :, 1], C["stats2"][:, :, 1], ACT.Sqrt).then_inc(rooted, 1)

        @block.vector
        def _(dve):
            nc.vector.memset(omega[:, :], 0.0).then_inc(set_up, 1)
            nc.vector.tensor_scalar(half[:, :], C["pair"][:, :], -0.5 / HF, None, ALU.mult).then_inc(set_up, 1)
            dve.sem_inc(argued, 2)
            dve.sem_inc(divided, 2)
            dve.sem_inc(finished, 2)
            dve.wait_ge(loaded, 32)
            nc.vector.tensor_scalar(omega[:, :], omega[:, :], HF ** -0.5, None, ALU.mult).then_inc(set_up, 1)

            def argue(m, c):
                n = m * NC + c
                dve.wait_ge(featured, n + 1 + 2)
                dve.wait_ge(mapped, n + 1)
                nc.vector.tensor_scalar(nrm[:, c % 2, :], pn[:, 0:HW], NORM_TOP, NORM_LOW, ALU.min, ALU.max).then_inc(bounded, 1)
                dve.wait_ge(bounded, n + 1)
                nc.vector.scalar_tensor_tensor(nrm[:, c % 2, :], pf[:, 0:HW], CLAMP, nrm[:, c % 2, :],
                                               ALU.min, ALU.add).then_inc(argued, 1)

            def divide(m, c):
                n = m * NC + c
                hf, k = divmod(c, KC)
                dve.wait_ge(summed, n + 1)
                nc.vector.reciprocal(rec[:, c % 2, :], pd[c % 2][:, 0:HW]).then_inc(inverted, 1)
                dve.wait_ge(inverted, n + 1)
                if c == 0:
                    if later(m):
                        dve.wait_ge(mixed, m * TM)
                nc.vector.tensor_tensor(phin[:, k, hf * HW:(hf + 1) * HW], phi[:, c % 2, :], rec[:, c % 2, :],
                                        ALU.mult).then_inc(divided, 1)

            def macro(m, q, u):
                for c in range(NC):
                    argue(m, c)
                    if c:
                        divide(m, c - 1)
                divide(m, NC - 1)
                for j in range(TM):
                    n = m * TM + j
                    s = (q + j) % 2
                    v = u * TM + (q * TM + j) // 2
                    dve.wait_ge(r_loaded[s], v * 32 + 32)
                    nc.vector.tensor_scalar(rden[:, s, 0, :], ac[:, s, D:D + H], DEN_LOW, None, ALU.max).then_inc(dens, 1)
                    dve.wait_ge(dens, n + 1)
                    nc.vector.reciprocal(rden[:, s, 1, :], rden[:, s, 0, :]).then_inc(rdens, 1)
                    dve.wait_ge(rdens, n + 1)
                    part = ac[:, s, 0:D].rearrange("p (h f) -> p h f", f=HF)
                    nc.vector.tensor_tensor(part, part, bc(rden[:, s, 1, :].unsqueeze(2), [P, H, HF]), ALU.mult).then_inc(graphed, 1)
                    dve.wait_ge(graphed, n + 1)
                    nc.vector.tensor_tensor(xs[:, s, :], xs[:, s, :], ac[:, s, 0:D], ALU.add).then_inc(based, 1)
                    dve.wait_ge(based, n + 1)
                    dve.wait_ge(mixed, n + 1)
                    if later(v):
                        dve.wait_ge(stored[s], v * 16)
                    nc.vector.tensor_tensor(x1[:, s, :], pm[s][:, :], xs[:, s, :], ALU.add).then_inc(finished, 1)
                    dve.wait_ge(finished, n + 1 + 2)
                    nc.vector.bn_stats(st[:, s, :], x1[:, s, :]).then_inc(used, 1)
                    dve.wait_ge(used, n + 1)
                    hold(dve, passed_v)
                    nc.vector.bn_aggr(agg[:, s, :], st[:, s, :]).then_inc(joined, 1)
                    dve.wait_ge(joined, n + 1)
                    nc.vector.tensor_copy(C["stats2"][:, n, :], agg[:, s, :])
            over_macros(dve, macro)
            dve.wait_ge(used, NT)
            nc.vector.memset(rden[:, 0, 0, :], 0.0).then_inc(dens, 1)
            dve.wait_ge(dens, NT + 1)
            nc.vector.tensor_scalar(C["stats2"][:, :, 1], C["stats2"][:, :, 1], LN_EPS, None, ALU.add).then_inc(counted, 1)
            dve.wait_ge(rooted, 1)
            nc.vector.reciprocal(C["stats2"][:, :, 1], C["stats2"][:, :, 1]).then_inc(counted, 1)
            dve.wait_ge(counted, 2)

        @block.tensor
        def _(pe):
            pe.wait_ge(wloaded, 16)
            pe.wait_ge(set_up, 3)
            pe.sem_inc(projected, 2)
            pe.sem_inc(featured, 2)

            def project(m, q, c):
                n = m * NC + c
                hf, kk = divmod(c, KC)
                pe.wait_ge(kept, n + 1)
                for k in range(KC):
                    last = nc.tensor.matmul(pq[c % 2][:, 0:HW], wq[:, k, kk * P:(kk + 1) * P],
                                            xT[:, q, k, hf * HW:(hf + 1) * HW], start=(k == 0), stop=(k == KC - 1))
                last.then_inc(projected, 1)

            def feature(m, c):
                n = m * NC + c
                pe.wait_ge(kept, n + 1 + 2)
                pe.wait_ge(argued, n + 2)
                nc.tensor.matmul(pf[:, 0:HW], omega[:, :], qT[:, c % 2, :], start=True, stop=True)
                nc.tensor.matmul(pn[:, 0:HW], half[:, :], q2[:, c % 2, :], start=True, stop=True).then_inc(featured, 1)

            def total(m, c):
                n = m * NC + c
                pe.wait_ge(mapped, n + 1 + 2)
                pe.wait_ge(divided, n + 1)
                nc.tensor.matmul(pd[c % 2][:, 0:HW], C["k1"][:, c % KC, :], phi[:, c % 2, :],
                                 start=True, stop=True).then_inc(summed, 1)

            def macro(m, q, u):
                pe.wait_ge(x_loaded[q], u * 16 + 16)
                project(m, q, 0)
                for c in range(NC):
                    if c + 1 < NC:
                        project(m, q, c + 1)
                    feature(m, c)
                    if c:
                        total(m, c - 1)
                total(m, NC - 1)
                pe.wait_ge(divided, m * NC + NC + 2)
                for j in range(TM):
                    n = m * TM + j
                    s = (q + j) % 2
                    pe.wait_ge(finished, n + 1)
                    for c in range(KC):
                        last = nc.tensor.matmul(pm[s][:, :], phin[:, c, j * P:(j + 1) * P], C["g"][:, c, :],
                                                start=(c == 0), stop=(c == KC - 1))
                    last.then_inc(mixed, 1)
            over_macros(pe, macro)


def route(nc, C, dram):
    with Stage(nc) as ctx:
        xs = fixed(ctx, nc, "rt_x", [P, 2, TM, D])
        xT = fixed(ctx, nc, "rt_xT", [P, 2, KC, P])
        wr = fixed(ctx, nc, "rt_wr", [P, KC, EX])
        lg = fixed(ctx, nc, "rt_lg", [P, 2, EX])
        best = fixed(ctx, nc, "rt_best", [P, 2, 8])
        which = fixed(ctx, nc, "rt_which", [P, 2, 8], U32)
        top = fixed(ctx, nc, "rt_top", [P, 2, NT])
        num = fixed(ctx, nc, "rt_num", [P, 2, NT])
        hit = fixed(ctx, nc, "rt_hit", [P, 2, NT, EX])
        both = fixed(ctx, nc, "rt_both", [P, NT, EX])
        tot = fixed(ctx, nc, "rt_tot", [P, NT, EX])
        cum = fixed(ctx, nc, "rt_cum", [P, NT, EX])
        nul = fixed(ctx, nc, "rt_nul", [P, NT])
        slot = fixed(ctx, nc, "rt_slot", [P, 2, NT])
        keep = fixed(ctx, nc, "rt_keep", [P, 2, NT])
        pos = fixed(ctx, nc, "rt_pos", [P, 2, NT])
        goal = fixed(ctx, nc, "rt_goal", [P, 2, NT])
        gap = fixed(ctx, nc, "rt_gap", [P, 2, NT])
        at = fixed(ctx, nc, "rt_at", [P, 2, TM, 2], I32)
        blank = fixed(ctx, nc, "rt_blank", [P, 4 * D])
        pT = [psum(ctx, nc, f"rt_pT{i}") for i in range(2)]
        pl = [psum(ctx, nc, f"rt_pl{i}") for i in range(2)]
        pp = psum(ctx, nc, "rt_pp")
        po = psum(ctx, nc, "rt_po")
        wloaded, blanks, blanked = sems(ctx, nc, "rt", "wloaded blanks blanked")
        loaded = sems(ctx, nc, "rt", " ".join(f"ld{i}" for i in range(2 * TM)))
        again = sems(ctx, nc, "rt", " ".join(f"again{i}" for i in range(2)))
        sent = sems(ctx, nc, "rt", "sent0 sent1")
        (normed, turned, kept, scored, logged, maxed, found, noted, v, s, counted, renormed, indexed, passed,
         passed_p, passed_v) = sems(ctx, nc, "rt", "normed turned kept scored logged maxed found noted v s counted renormed indexed "
                                         "passed passedp passedv")
        block = ctx.enter_context(nc.Block())
        rows = dram["x1"].rearrange("(n p) d -> n p d", p=P)
        macros = dram["x1"].rearrange("(m j p) d -> m p j d", j=TM, p=P)
        LAST = 14

        @block.sync
        def _(sp):
            sp.dma_start(wr[:, :, :], dram["router_w"].rearrange("(k p) e -> p k e", p=P)).then_inc(wloaded, 16)

            def macro(m, q, u):
                for j in range(TM):
                    sp.wait_ge(turned, m * TM + j + 1)
                    hold(sp, passed)
                    sp.dma_start(xs[:, q, j, :], rows[m * TM + j]).then_inc(loaded[q * TM + j], 16)
            over_macros(sp, macro)
            sp.wait_ge(blanks, 1)
            sp.dma_start(dram["xe"].rearrange("(p n) d -> p (n d)", p=P).rearrange("p (n w) -> p n w", w=4 * D),
                         bc(blank[:, :].unsqueeze(1), [P, EX * CAP // P // 4, 4 * D])).then_inc(blanked, 16)
            sp.wait_ge(turned, NT + 2 * TM)

            def send(m, q, u):
                if later(u):
                    sp.wait_ge(sent[q], u * (2 * TM * 16))
                hold(sp, passed)
                sp.dma_start(xs[:, q, :, :], macros[m]).then_inc(again[q], 16)
            over_macros(sp, send)

        @block.scalar
        def _(act):
            act.sem_inc(kept, 2)

            def macro(m, q, u):
                for j in range(TM):
                    n = m * TM + j
                    b = (q + j) % 2
                    act.wait_ge(turned, n + 1 + 2 * TM)
                    act.wait_ge(scored, n + 1)
                    nc.scalar.activation(xT[:, b, :, :].rearrange("p k t -> p (k t)"), pT[b][:, :], ACT.Copy).then_inc(kept, 1)
            over_macros(act, macro)
            act.wait_ge(v, 2)
            nc.scalar.activation(gap[:, 0, :], gap[:, 1, :], ACT.Exp).then_inc(s, 1)

        @block.vector
        def _(dve):
            nc.vector.memset(blank[:, :], 0.0).then_inc(blanks, 1)
            nc.vector.memset(nul[:, :], 0.0)

            def norm(n, q, j, done):
                nc.vector.tensor_scalar(xs[:, q, j, :], xs[:, q, j, :], C["stats2"][:, n, 0:1], C["stats2"][:, n, 1:2],
                                        ALU.subtract, ALU.mult).then_inc(done, 1)

            def macro(m, q, u):
                for j in range(TM + 1):
                    n = m * TM + j
                    if j < TM:
                        dve.wait_ge(loaded[q * TM + j], u * 16 + 16)
                        norm(n, q, j, normed)
                    if j:
                        pick(m, q, j - 1)

            def pick(m, q, j):
                n = m * TM + j
                b = (q + j) % 2
                dve.wait_ge(scored, n + 1 + 2)
                nc.vector.tensor_copy(lg[:, b, :], pl[b][:, 0:EX]).then_inc(logged, 1)
                dve.wait_ge(logged, n + 1)
                hold(dve, passed_v)
                nc.vector.max(best[:, b, :], lg[:, b, :]).then_inc(maxed, 1)
                dve.wait_ge(maxed, n + 1)
                hold(dve, passed_v)
                nc.vector.max_index(which[:, b, :], best[:, b, :], lg[:, b, :]).then_inc(found, 1)
                dve.wait_ge(found, n + 1)
                nc.vector.tensor_copy(top[:, :, bass.ds(n, 1)], best[:, b, 0:2].unsqueeze(2))
                nc.vector.tensor_copy(num[:, :, bass.ds(n, 1)], which[:, b, 0:2].unsqueeze(2)).then_inc(noted, 1)
            over_macros(dve, macro)
            dve.wait_ge(noted, NT)
            done = [0]

            def link(ins):
                done[0] += 1
                ins.then_inc(v, 1)
                dve.wait_ge(v, done[0])

            for kk in range(2):
                last = nc.vector.tensor_tensor(hit[:, kk, :, :], bc(num[:, kk, :].unsqueeze(2), [P, NT, EX]),
                                               bc(C["cols"][:, 0:EX].unsqueeze(1), [P, NT, EX]), ALU.is_equal)
            link(last)
            link(nc.vector.tensor_tensor(gap[:, 1, :], top[:, 1, :], top[:, 0, :], ALU.subtract))
            link(nc.vector.tensor_tensor(both[:, :, :], hit[:, 0, :, :], hit[:, 1, :, :], ALU.add))
            dve.wait_ge(s, 1)
            link(nc.vector.tensor_scalar(gap[:, 1, :], gap[:, 0, :], 1.0, None, ALU.add))
            link(nc.vector.reciprocal(C["weight"][:, 0, :], gap[:, 1, :]))
            nc.vector.tensor_tensor(C["weight"][:, 1, :], C["weight"][:, 0, :], gap[:, 0, :], ALU.mult)
            dve.wait_ge(counted, 1)
            link(nc.vector.tensor_copy(tot[:, :, :].rearrange("p n e -> p (n e)"), po[:, 0:NT * EX]))
            for x in range(EX):
                last = nc.vector.tensor_tensor_scan(cum[:, :, x], tot[:, :, x], nul[:, :], 0.0, ALU.add, ALU.add)
            link(last)
            link(nc.vector.tensor_tensor(cum[:, :, :], cum[:, :, :], tot[:, :, :], ALU.subtract))
            link(nc.vector.tensor_tensor(cum[:, :, :].rearrange("p n e -> p (n e)"), cum[:, :, :].rearrange("p n e -> p (n e)"),
                                         pp[:, 0:NT * EX], ALU.add))
            link(nc.vector.tensor_tensor(hit[:, :, :, :], hit[:, :, :, :], bc(cum[:, :, :].unsqueeze(1), [P, 2, NT, EX]),
                                         ALU.mult))
            nc.vector.tensor_scalar(pos[:, :, :], num[:, :, :], float(CAP), None, ALU.mult)
            link(nc.vector.tensor_reduce(slot[:, :, :], hit[:, :, :, :], AX.X, ALU.add))
            nc.vector.tensor_scalar(keep[:, :, :], slot[:, :, :], float(CAP), None, ALU.is_lt)
            nc.vector.tensor_tensor(goal[:, :, :], slot[:, :, :], pos[:, :, :], ALU.add)
            link(nc.vector.tensor_scalar(slot[:, :, :], slot[:, :, :], float(CAP - 1), None, ALU.min))
            nc.vector.tensor_tensor(C["weight"][:, :, :], C["weight"][:, :, :], keep[:, :, :], ALU.mult)
            nc.vector.tensor_tensor(slot[:, :, :], slot[:, :, :], pos[:, :, :], ALU.add)
            link(nc.vector.tensor_tensor(keep[:, :, :], keep[:, :, :], bc(C["valid"][:, :].unsqueeze(1), [P, 2, NT]), ALU.mult))
            nc.vector.tensor_copy(C["from"][:, :, :], slot[:, :, :].rearrange("p k n -> p n k"))
            link(nc.vector.tensor_scalar(keep[:, :, :], keep[:, :, :], -BIG, BIG, ALU.mult, ALU.add))
            assert done[0] == LAST
            nc.vector.tensor_tensor(goal[:, :, :], goal[:, :, :], keep[:, :, :], ALU.add).then_inc(indexed, 1)
            dve.wait_ge(indexed, 1)

            def send(m, q, u):
                if later(u):
                    dve.wait_ge(sent[q], u * (2 * TM * 16))
                nc.vector.tensor_copy(at[:, q, :, :], goal[:, :, bass.ds(m * TM, TM)].rearrange("p k j -> p j k")).then_inc(indexed, 1)
                dve.wait_ge(again[q], u * 16 + 16)
                for j in range(TM):
                    norm(m * TM + j, q, j, renormed)
            over_macros(dve, send)

        @block.gpsimd
        def _(pool):
            pool.wait_ge(blanked, 16)

            def send(m, q, u):
                pool.wait_ge(indexed, m + 2)
                for j in range(TM):
                    pool.wait_ge(renormed, m * TM + j + 1)
                    hold(pool, passed_p)
                    for kk in range(2):
                        pool.indirect_dma_start(out=dram["xe"], out_offset=bass.IndirectOffsetOnAxis(ap=at[:, q, j, kk:kk + 1], axis=0),
                                                in_=xs[:, q, j, :], in_offset=None, bounds_check=EX * CAP - 1,
                                                oob_is_err=False).then_inc(sent[q], 16)
            over_macros(pool, send)
            pool.wait_ge(sent[0], 2 * TM * 16 * ((NM + 1) // 2))
            pool.wait_ge(sent[1], 2 * TM * 16 * (NM // 2))

        @block.tensor
        def _(pe):
            pe.wait_ge(wloaded, 16)
            pe.sem_inc(turned, 2 * TM)
            pe.sem_inc(scored, 2)

            def turn(m, q, j):
                n = m * TM + j
                b = (q + j) % 2
                pe.wait_ge(normed, n + 1)
                pe.wait_ge(kept, n + 1)
                for k in range(KC):
                    last = nc.tensor.transpose(pT[b][:, k * P:(k + 1) * P], xs[:, q, j, k * P:(k + 1) * P], C["ident"][:, :])
                last.then_inc(turned, 1)

            def macro(m, q, u):
                turn(m, q, 0)
                for j in range(TM):
                    n = m * TM + j
                    b = (q + j) % 2
                    if j + 1 < TM:
                        turn(m, q, j + 1)
                    pe.wait_ge(kept, n + 1 + 2)
                    if later(n):
                        pe.wait_ge(logged, n)
                    for k in range(KC):
                        last = nc.tensor.matmul(pl[b][:, 0:EX], xT[:, b, k, :], wr[:, k, :], start=(k == 0), stop=(k == KC - 1))
                    last.then_inc(scored, 1)
            over_macros(pe, macro)
            pe.wait_ge(v, 3)
            flat = both[:, :, :].rearrange("p n e -> p (n e)")
            nc.tensor.matmul(pp[:, 0:NT * EX], C["before"][:, :], flat, start=True, stop=True)
            nc.tensor.matmul(po[:, 0:NT * EX], C["ones"][:, :], flat, start=True, stop=True).then_inc(counted, 1)


def experts(nc, C, dram):
    with Stage(nc) as ctx:
        w1 = fixed(ctx, nc, "ex_w1", [P, 2, KC, FF])
        w2 = fixed(ctx, nc, "ex_w2", [P, 2, FC, D])
        b1 = fixed(ctx, nc, "ex_b1", [P, 2, FC])
        b2 = fixed(ctx, nc, "ex_b2", [P, 2, D])
        xs = fixed(ctx, nc, "ex_x", [P, 2, ST, D])
        xT = fixed(ctx, nc, "ex_xT", [P, 2, KC, SW])
        hT = fixed(ctx, nc, "ex_hT", [P, 2, FC, SW])
        ys = fixed(ctx, nc, "ex_y", [P, 2, ST, D])
        pT = [psum(ctx, nc, f"ex_pT{i}") for i in range(2)]
        ph = [psum(ctx, nc, f"ex_ph{i}") for i in range(2)]
        py = [psum(ctx, nc, f"ex_py{i}") for i in range(2)]
        w_loaded = sems(ctx, nc, "ex", "w0 w1")
        x_loaded = sems(ctx, nc, "ex", "x0 x1")
        y_stored = sems(ctx, nc, "ex", "y0 y1")
        turned, kept_a, kept_v, expanded, bent, reduced, biased, used, passed = sems(
            ctx, nc, "ex", "turned kept_a kept_v expanded bent reduced biased used passed")
        block = ctx.enter_context(nc.Block())
        CH = CAP // SW
        xe = dram["xe"].rearrange("(c t p) d -> c p t d", t=ST, p=P)
        ye = dram["ye"].rearrange("(c t p) d -> c p t d", t=ST, p=P)

        def chunks(eng, body, open_expert=None, close_expert=None):
            def pair(i):
                for w in range(2):
                    if open_expert:
                        open_expert(i * 2 + w, w, i)
                    for c in range(CH):
                        body((i * 2 + w) * CH + c, c % 2, w, i * CH + (w * CH + c) // 2)
                    if close_expert:
                        close_expert(i * 2 + w)
            pair(0)
            with eng.Fori(1, EX // 2) as i:
                pair(i)

        @block.sync
        def _(sp):
            def open_expert(e, w, i):
                sp.wait_ge(used, e + 1)
                hold(sp, passed)
                sp.dma_start(w1[:, w, :, :], dram["w1"][e].rearrange("(k p) f -> p k f", p=P)).then_inc(w_loaded[w], 16)
                sp.dma_start(w2[:, w, :, :], dram["w2"][e].rearrange("(k p) d -> p k d", p=P)).then_inc(w_loaded[w], 16)
                sp.dma_start(b1[:, w, :], dram["b1"][e]).then_inc(w_loaded[w], 16)
                sp.dma_start(b2[:, w, :], dram["b2"][e].partition_broadcast(P)).then_inc(w_loaded[w], 16)

            def chunk(n, q, w, u):
                sp.wait_ge(turned, n * KC + KC)
                hold(sp, passed)
                sp.dma_start(xs[:, q, :, :], xe[n]).then_inc(x_loaded[q], 16)
            chunks(sp, chunk, open_expert)

        @block.gpsimd
        def _(pool):
            def chunk(n, q, w, u):
                pool.wait_ge(biased, n * ST + ST + 2)
                pool.dma_start(ye[n], ys[:, q, :, :]).then_inc(y_stored[q], 16)
            chunks(pool, chunk)
            for q in range(2):
                pool.wait_ge(y_stored[q], EX * CH // 2 * 16)

        @block.scalar
        def _(act):
            act.sem_inc(kept_a, 1)
            act.sem_inc(bent, 2)

            def chunk(n, q, w, u):
                for k in range(0, KC, 2):
                    act.wait_ge(turned, n * KC + k + 1 + 2 * KC)
                    act.wait_ge(expanded, n * FC + FC)
                    nc.scalar.activation(xT[:, q, k, :], pT[0][:, :], ACT.Copy).then_inc(kept_a, 1)
                for f in range(FC):
                    act.wait_ge(expanded, n * FC + f + 1 + 2 * FC)
                    act.wait_ge(reduced, n * ST + ST)
                    nc.scalar.activation(hT[:, q, f, :], ph[f][:, :], ACT.Gelu_apprx_tanh, bias=b1[:, w, f:f + 1]).then_inc(bent, 1)
            chunks(act, chunk)

        @block.vector
        def _(dve):
            dve.sem_inc(kept_v, 1)
            dve.sem_inc(biased, 2)

            def chunk(n, q, w, u):
                for k in range(1, KC, 2):
                    dve.wait_ge(turned, n * KC + k + 1 + 2 * KC)
                    dve.wait_ge(expanded, n * FC + FC)
                    nc.vector.tensor_copy(xT[:, q, k, :], pT[1][:, :]).then_inc(kept_v, 1)
                if later(u):
                    dve.wait_ge(y_stored[q], u * 16)
                for t in range(ST):
                    m = n * ST + t
                    dve.wait_ge(reduced, m + 1 + 2 * ST)
                    nc.vector.tensor_tensor(ys[:, q, t, :], py[t % 2][:, :], b2[:, w, :], ALU.add).then_inc(biased, 1)
            chunks(dve, chunk)

        @block.tensor
        def _(pe):
            pe.sem_inc(turned, 2 * KC)
            pe.sem_inc(expanded, 2 * FC)
            pe.sem_inc(reduced, 2 * ST)
            pe.sem_inc(used, 2)

            def open_expert(e, w, i):
                pe.wait_ge(w_loaded[w], i * 64 + 64)

            def chunk(n, q, w, u):
                pe.wait_ge(x_loaded[q], u * 16 + 16)
                for k in range(KC):
                    pe.wait_ge((kept_a, kept_v)[k % 2], n * (KC // 2) + k // 2 + 1)
                    for t in range(ST):
                        last = nc.tensor.transpose(pT[k % 2][:, t * P:(t + 1) * P], xs[:, q, t, k * P:(k + 1) * P], C["ident"][:, :])
                    last.then_inc(turned, 1)
                pe.wait_ge(kept_a, (n + 1) * (KC // 2) + 1)
                pe.wait_ge(kept_v, (n + 1) * (KC // 2) + 1)
                for f in range(FC):
                    pe.wait_ge(bent, n * FC + f + 1)
                    for k in range(KC):
                        last = nc.tensor.matmul(ph[f][:, :], w1[:, w, k, f * P:(f + 1) * P], xT[:, q, k, :],
                                                start=(k == 0), stop=(k == KC - 1))
                    last.then_inc(expanded, 1)
                pe.wait_ge(bent, n * FC + FC + 2)
                for t in range(ST):
                    m = n * ST + t
                    pe.wait_ge(biased, m + 1)
                    for f in range(FC):
                        last = nc.tensor.matmul(py[t % 2][:, :], hT[:, q, f, t * P:(t + 1) * P], w2[:, w, f, :],
                                                start=(f == 0), stop=(f == FC - 1))
                    last.then_inc(reduced, 1)

            def close_expert(e):
                pe.wait_ge(biased, ((e + 1) * CH) * ST + 2)
                hold(pe, used)
            chunks(pe, chunk, open_expert, close_expert)


def combine(nc, C, dram):
    with Stage(nc) as ctx:
        xs = fixed(ctx, nc, "co_x", [P, TM, D])
        ya = fixed(ctx, nc, "co_ya", [P, 2, TM, D])
        at = fixed(ctx, nc, "co_at", [P, TM, 2], I32)
        os = fixed(ctx, nc, "co_o", [P, TM, D])
        loaded = sems(ctx, nc, "co", " ".join(f"ld{j}" for j in range(TM)))
        fetched = sems(ctx, nc, "co", " ".join(f"fe{j}" for j in range(TM)))
        stored = sems(ctx, nc, "co", " ".join(f"st{j}" for j in range(TM)))
        indexed, halved, summed, passed, passed_p = sems(ctx, nc, "co", "indexed halved summed passed passedp")
        block = ctx.enter_context(nc.Block())
        rows = dram["x1"].rearrange("(n p) d -> n p d", p=P)
        out = dram["out"].rearrange("(n p) d -> n p d", p=P)

        @block.sync
        def _(sp):
            def load(n, j):
                sp.dma_start(xs[:, j, :], rows[n]).then_inc(loaded[j], 16)

            def store(n, j):
                sp.wait_ge(summed, n + 1)
                hold(sp, passed)
                sp.dma_start(out[n], os[:, j, :]).then_inc(stored[j], 16)
            for j in range(TM):
                load(j, j)
            with sp.Fori(0, NM - 1) as m:
                for j in range(TM):
                    store(m * TM + j, j)
                    load(m * TM + j + TM, j)
            for j in range(TM):
                store((NM - 1) * TM + j, j)
            for j in range(TM):
                sp.wait_ge(stored[j], 16 * NM)

        @block.gpsimd
        def _(pool):
            def macro(m):
                pool.wait_ge(indexed, m + 1)
                for j in range(TM):
                    if later(m):
                        pool.wait_ge(summed, m * TM)
                    hold(pool, passed_p)
                    for kk in range(2):
                        pool.indirect_dma_start(out=ya[:, kk, j, :], out_offset=None, in_=dram["ye"],
                                                in_offset=bass.IndirectOffsetOnAxis(ap=at[:, j, kk:kk + 1], axis=0)).then_inc(fetched[j], 16)
            macro(0)
            with pool.Fori(1, NM) as m:
                macro(m)

        @block.vector
        def _(dve):
            def macro(m):
                for j in range(TM):
                    if later(m):
                        dve.wait_ge(fetched[j], m * 32)
                nc.vector.tensor_copy(at[:, :, :], C["from"][:, bass.ds(m * TM, TM), :]).then_inc(indexed, 1)
                for j in range(TM):
                    n = m * TM + j
                    dve.wait_ge(loaded[j], m * 16 + 16)
                    dve.wait_ge(fetched[j], m * 32 + 32)
                    nc.vector.scalar_tensor_tensor(xs[:, j, :], ya[:, 0, j, :], C["weight"][:, 0, bass.ds(n, 1)], xs[:, j, :],
                                                   ALU.mult, ALU.add).then_inc(halved, 1)
                    dve.wait_ge(halved, n + 1)
                    if later(m):
                        dve.wait_ge(stored[j], m * 16)
                    nc.vector.scalar_tensor_tensor(os[:, j, :], ya[:, 1, j, :], C["weight"][:, 1, bass.ds(n, 1)], xs[:, j, :],
                                                   ALU.mult, ALU.add).then_inc(summed, 1)
            macro(0)
            with dve.Fori(1, NM) as m:
                macro(m)


_INS = {"x": (NP, D), "src_em": (ET // BT, P, BT), "dst": (EP,), "dst_before": (EP,),
        "W_src": (D, D), "b_src": (D,), "W_dst": (D, D), "b_dst": (D,), "W_val": (D, D), "b_val": (D,),
        "attn_l": (D,), "attn_r": (D,),
        "Wq": (D, D), "Wk": (D, D), "Wv": (D, D), "Wo": (D, D), "omega_q": (HF, HF), "omega_k": (HF, HF),
        "router_w": (D, EX), "w1": (EX, D, FF), "b1": (EX, P, FC), "w2": (EX, FF, D), "b2": (EX, D)}


def build(nc, dram, upto=99):
    with ExitStack() as ctx:
        C = {
            "ident": fixed(ctx, nc, "c_ident", [P, P]),
            "before": fixed(ctx, nc, "c_before", [P, P]),
            "ones": fixed(ctx, nc, "c_ones", [P, P]),
            "cols": fixed(ctx, nc, "c_cols", [P, P]),
            "pair": fixed(ctx, nc, "c_pair", [P, P]),
            "after": fixed(ctx, nc, "c_after", [P, P]),
            "valid": fixed(ctx, nc, "c_valid", [P, NT]),
            "stats1": fixed(ctx, nc, "c_stats1", [P, NT, 2]),
            "stats2": fixed(ctx, nc, "c_stats2", [P, NT, 2]),
        }
        with ExitStack() as edges:
            C["rank"] = fixed(edges, nc, "c_rank", [P, ET])
            C["target"] = fixed(edges, nc, "c_target", [P, ET])
            C["first"] = fixed(edges, nc, "c_first", [P, ET])
            C["own"] = fixed(edges, nc, "c_own", [GH, 2])
            with ExitStack() as nodes:
                C["wval"] = fixed(nodes, nc, "c_wval", [P, KC, D + 2 * H])
                C["vbias"] = fixed(nodes, nc, "c_vbias", [P, D + 2 * H])
                C["begin"] = fixed(nodes, nc, "c_begin", [P, NG])
                C["start"] = fixed(nodes, nc, "c_start", [P, NT], I32)
                prep_weights(nc, C, dram)
                prep_edges(nc, C, dram)
                find_starts(nc, C, dram)
                norm_stats(nc, C, dram, dram["x"], C["stats1"], "s1")
                project_nodes(nc, C, dram)
            C["er"] = fixed(edges, nc, "c_er", [P, ET * H])
            if upto >= 2:
                spread_er(nc, C, dram)
                edge_attention(nc, C, dram)
                merge_groups(nc, C, dram)
        if upto >= 3:
            with ExitStack() as inner:
                C["g"] = fixed(inner, nc, "c_g", [P, KC, D])
                C["k1"] = fixed(inner, nc, "c_k1", [P, KC, P])
                with ExitStack() as keys:
                    C["wo"] = fixed(keys, nc, "c_wo", [P, KC, D])
                    key_sums(nc, C, dram)
                query_rows(nc, C, dram)
        if upto >= 4:
            C["weight"] = fixed(ctx, nc, "c_weight", [P, 2, NT])
            C["from"] = fixed(ctx, nc, "c_from", [P, NT, 2], I32)
            route(nc, C, dram)
            experts(nc, C, dram)
            combine(nc, C, dram)


def scratch(nc, dram):
    dram["xnT"] = nc.dram_tensor("xnT", (NM, P, KC, MW), F32).ap()
    dram["vtab"] = nc.dram_tensor("vtab", (NP, VW), F32).ap()
    dram["ertab"] = nc.dram_tensor("ertab", (NP, H), F32).ap()
    dram["dst_f"] = nc.dram_tensor("dst_f", (NG, GE), F32).ap()
    dram["er_edge"] = nc.dram_tensor("er_edge", (EP, H), F32).ap()
    dram["acc"] = nc.dram_tensor("acc", (NP + NG, AW), F32).ap()
    dram["pen"] = nc.dram_tensor("pen", (NG, GE + 1), F32).ap()
    dram["x1"] = nc.dram_tensor("x1", (NP, D), F32).ap()
    dram["xe"] = nc.dram_tensor("xe", (EX * CAP, D), F32).ap()
    dram["ye"] = nc.dram_tensor("ye", (EX * CAP, D), F32).ap()
    dram["out"] = nc.dram_tensor("out_0_dram", (NP, D), F32, kind="ExternalOutput").ap()


def kernel(**inputs):
    import numpy as np
    import concourse.bacc as bacc
    from concourse.bass_utils import run_bass_kernel_spmd as run

    def given(name):
        return np.ascontiguousarray(inputs[name])

    def batches(edges):
        return np.ascontiguousarray(edges.reshape(ET // BT, BT, P).transpose(0, 2, 1))

    dst = np.pad(given("dst").astype(np.int32), (0, EP - E), constant_values=N)
    src = np.pad(given("src").astype(np.int32), (0, EP - E))
    arrays = {
        "x": np.pad(given("x"), ((0, NP - N), (0, 0))),
        "src_em": batches(src),
        "dst": dst, "dst_before": np.concatenate([np.full(1, -1, np.int32), dst[:-1]]),
        "b1": np.ascontiguousarray(given("L0_ffn_b1").reshape(EX, FC, P).transpose(0, 2, 1)),
    }
    for part in ("gnn", "mix", "ffn"):
        for name in inputs:
            short = name.removeprefix(f"L0_{part}_")
            if short != name and short in _INS and short not in arrays:
                arrays[short] = given(name).reshape(_INS[short])
    nc = bacc.Bacc("TRN2", target_bir_lowering=False, num_devices=1)
    dram = {name: nc.dram_tensor(f"in_{name}", a.shape, mybir.dt.from_np(a.dtype), kind="ExternalInput").ap()
            for name, a in arrays.items()}
    scratch(nc, dram)
    build(nc, dram)
    result = run(nc, [{f"in_{name}": a for name, a in arrays.items()}], core_ids=[0])
    return result.results[0]["out_0_dram"][:N]
```

```python
import math
from contextlib import ExitStack

import concourse.bass as bass
from concourse import mybir

F32 = mybir.dt.float32
F32R = mybir.dt.float32r
I32 = mybir.dt.int32
ALU = mybir.AluOpType
ACT = mybir.ActivationFunctionType
AX = mybir.AxisListType

N, D, H, HF = 6250, 512, 8, 64
P = 128
KC = D // P
TM = 7
NT = -(-N // P)
NM = NT // TM
NP = NT * P
MW = TM * P
HW = MW // 2
assert NM * TM == NT and NM % 2
E = 100000
GT = 4
GE = GT * P
BT = 16
BG = BT // GT
NG = -(-E // (2 * BT * P)) * 2 * BG
ET = NG * GT
EP = ET * P
GH = NG // 2
assert GH <= P
VW = D + H
VH = (D + 2 * H) // 2
AW = D + 2 * H
XW = 2 * H + 1
RS = 3
SG = 8
BIG = float(1 << 20)
LOW = -1.0e30
PARTS = ((0, 0), (1, 0), (0, 1))
EB = 640
assert RS == 3 and NG % SG == 0 and EP * H // P % EB == 0 and BG * GE == BT * P
LN_EPS = 1e-5
SLOPE = 0.2
CLAMP = 50.0
FLOOR = 1e-8
NORM_TOP, NORM_LOW = -0.5 * FLOOR ** 2, math.log(FLOOR)
DEN_LOW = 1e-16
EX, FF = 8, 256
FC = FF // P
CAP = min(N, P * math.ceil(math.ceil(0.3125 * N) / P))
SW = 512
ST = SW // P
assert CAP % (2 * SW) == 0 and NT * EX <= 512


def fixed(ctx, nc, name, shape, dt=F32):
    return ctx.enter_context(nc.sbuf_tensor(name, list(shape), dt))


def psum(ctx, nc, name, cols=512):
    return ctx.enter_context(nc.psum_tensor(name, [P, cols], F32))


def sems(ctx, nc, prefix, names):
    taken = [nc.alloc_semaphore(f"{prefix}_{n}") for n in names.split()]
    ctx.taken += taken
    return taken


class Stage(ExitStack):

    def __init__(self, nc):
        super().__init__()
        self.taken = []

        def give_back():
            nc.clear_and_free_semaphores(self.taken)
            nc.all_engine_barrier()
        self.callback(give_back)


def bc(ap, shape):
    return ap.to_broadcast(list(shape))


def hold(eng, passed):
    eng.sem_inc(passed, 1)


def later(n):
    return not isinstance(n, int) or n > 0


def over_macros(eng, body, **last):
    body(0, 0, 0)
    body(1, 1, 0)
    with eng.Fori(1, NM // 2) as i:
        body(i * 2, 0, i)
        body(i * 2 + 1, 1, i)
    body(NM - 1, 0, NM // 2, **last)


def prep_weights(nc, C, dram):
    with Stage(nc) as ctx:
        wsrc = fixed(ctx, nc, "pw_wsrc", [P, KC, D])
        wdst = fixed(ctx, nc, "pw_wdst", [P, KC, D])
        rows = fixed(ctx, nc, "pw_rows", [P, 4, D])
        prod = fixed(ctx, nc, "pw_prod", [P, 2, D])
        loaded, wv_loaded, zeroed, const, mult, folded, paired = sems(
            ctx, nc, "pw", "loaded wv zeroed const mult folded paired")
        block = ctx.enter_context(nc.Block())

        @block.sync
        def _(sp):
            sp.dma_start(wsrc[:, :, :], dram["W_src"].rearrange("(k p) n -> p k n", p=P)).then_inc(loaded, 16)
            sp.dma_start(wdst[:, :, :], dram["W_dst"].rearrange("(k p) n -> p k n", p=P)).then_inc(loaded, 16)
            for r, name in enumerate(("attn_l", "attn_r", "b_src", "b_dst")):
                sp.dma_start(rows[:, r, :], dram[name].partition_broadcast(P)).then_inc(loaded, 16)
            for k in range(KC):
                sp.dma_start(C["wval"][:, k, 0:D], dram["W_val"][k * P:(k + 1) * P, :]).then_inc(wv_loaded, 16)
            sp.dma_start(C["vbias"][:, 0:D], dram["b_val"].partition_broadcast(P)).then_inc(wv_loaded, 16)
            sp.wait_ge(wv_loaded, 16 * (KC + 1))

        @block.gpsimd
        def _(pool):
            pool.memset(C["ident"][:, :], 0.0).then_inc(zeroed, 1)
            pool.memset(C["before"][:, :], 1.0).then_inc(zeroed, 1)
            pool.memset(C["ones"][:, :], 1.0)
            pool.iota(C["cols"][:, :], [[1, P]], base=0, channel_multiplier=0,
                      allow_small_or_imprecise_dtypes=True).then_inc(const, 1)
            pool.memset(C["after"][:, :], 1.0).then_inc(zeroed, 1)
            pool.wait_ge(zeroed, 3)
            pool.affine_select(out=C["ident"][:, :], in_=C["ident"][:, :], compare_op=ALU.not_equal, fill=1.0,
                               base=0, pattern=[[-1, P]], channel_multiplier=1).then_inc(const, 1)
            pool.affine_select(out=C["before"][:, :], in_=C["before"][:, :], compare_op=ALU.is_gt, fill=0.0,
                               base=0, pattern=[[1, P]], channel_multiplier=-1).then_inc(const, 1)
            pool.affine_select(out=C["after"][:, :], in_=C["after"][:, :], compare_op=ALU.is_gt, fill=0.0,
                               base=0, pattern=[[-1, P]], channel_multiplier=1).then_inc(const, 1)
            pool.memset(C["valid"][:, :], 1.0).then_inc(zeroed, 1)
            pool.wait_ge(zeroed, 4)
            pool.affine_select(out=C["valid"][:, :], in_=C["valid"][:, :], compare_op=ALU.is_gt, fill=0.0,
                               base=N, pattern=[[-P, NT]], channel_multiplier=-1).then_inc(const, 1)
            pool.wait_ge(const, 5)

        @block.vector
        def _(dve):
            nc.vector.memset(C["pair"][:, :], 0.0).then_inc(paired, 1)
            dve.wait_ge(paired, 1)
            nc.vector.memset(C["pair"][0:HF, 0:HF], 1.0)
            nc.vector.memset(C["pair"][HF:P, HF:P], 1.0).then_inc(paired, 1)
            dve.wait_ge(loaded, 6 * 16)
            done = 0
            for k in range(KC):
                for s, w in enumerate((wsrc, wdst)):
                    if done >= 2:
                        dve.wait_ge(folded, done - 1)
                    nc.vector.tensor_tensor(prod[:, s, :], w[:, k, :], rows[:, s, :], ALU.mult).then_inc(mult, 1)
                    dve.wait_ge(mult, done + 1)
                    nc.vector.tensor_reduce(C["wval"][:, k, D + s * H:D + (s + 1) * H],
                                            prod[:, s, :].rearrange("p (h f) -> p h f", f=HF), AX.X, ALU.add).then_inc(folded, 1)
                    done += 1
            for s in range(2):
                dve.wait_ge(folded, done - 1)
                nc.vector.tensor_tensor(prod[:, s, :], rows[:, 2 + s, :], rows[:, s, :], ALU.mult).then_inc(mult, 1)
                dve.wait_ge(mult, done + 1)
                nc.vector.tensor_reduce(C["vbias"][:, D + s * H:D + (s + 1) * H],
                                        prod[:, s, :].rearrange("p (h f) -> p h f", f=HF), AX.X, ALU.add).then_inc(folded, 1)
                done += 1
            dve.wait_ge(folded, done)
            dve.wait_ge(paired, 2)


def project_nodes(nc, C, dram):
    with Stage(nc) as ctx:
        xs = fixed(ctx, nc, "pn_x", [P, 2, TM, D])
        st = fixed(ctx, nc, "pn_st", [P, TM, 6])
        mom = fixed(ctx, nc, "pn_mom", [P, 2, TM, 2])
        xT = fixed(ctx, nc, "pn_xT", [P, TM, KC, P])
        vr = fixed(ctx, nc, "pn_v", [P, TM, 2, VH])
        ids = fixed(ctx, nc, "pn_ids", [P, NT])
        junk = fixed(ctx, nc, "pn_junk", [P, 2 * TM, NG])
        seen = fixed(ctx, nc, "pn_seen", [P, 2, GE])
        row = fixed(ctx, nc, "pn_row", [P, TM, GE])
        gi = fixed(ctx, nc, "pn_gi", [P, TM], I32)
        below = fixed(ctx, nc, "pn_below", [P, 2, TM])
        group = fixed(ctx, nc, "pn_group", [P, TM])
        count = fixed(ctx, nc, "pn_count", [P, 2, TM])
        start = fixed(ctx, nc, "pn_start", [P, TM])
        some = fixed(ctx, nc, "pn_some", [P, TM])
        ai = fixed(ctx, nc, "pn_ai", [P, 5, TM], I32)
        at = fixed(ctx, nc, "pn_at", [P, 2, TM], I32)
        blank = fixed(ctx, nc, "pn_blank", [P, AW])
        pT = [psum(ctx, nc, f"pn_pT{i}") for i in range(2)]
        pV = [[psum(ctx, nc, f"pn_pV{i}{half}") for half in range(2)] for i in range(2)]
        x_loaded = [sems(ctx, nc, "pn", " ".join(f"ld{q}{j}" for j in range(TM))) for q in range(2)]
        t_stored = sems(ctx, nc, "pn", " ".join(f"ts{j}" for j in range(TM)))
        v_stored = sems(ctx, nc, "pn", " ".join(f"vs{j}" for j in range(TM)))
        e_stored = sems(ctx, nc, "pn", " ".join(f"es{j}" for j in range(TM)))
        fetched = sems(ctx, nc, "pn", " ".join(f"fe{j}" for j in range(TM)))
        (blanks, blanked, numbered, searched, measured, v, rooted, counted, normed, turned, kept, projected, biased, passed, passed_p,
         passed_v) = sems(ctx, nc, "pn", "blanks blanked numbered searched measured v rooted counted normed turned kept projected biased "
                                         "passed passedp passedv")
        block = ctx.enter_context(nc.Block())
        rows = dram["x"].rearrange("(n p) d -> n p d", p=P)
        v_rows = dram["vtab"].rearrange("(n p) w -> n p w", p=P)
        er_rows = dram["ertab"].rearrange("(n p) w -> n p w", p=P)
        GROUPED, NORMED, PLACED = 2, 5, 16

        def next_of(m, q, u):
            return m + 1, 1 - q, u + q

        @block.sync
        def _(sp):
            def load(m, q, u):
                for j in range(TM):
                    sp.wait_ge(turned, m * TM + j + 1)
                    hold(sp, passed)
                    sp.dma_start(xs[:, q, j, :], rows[m * TM + j]).then_inc(x_loaded[q][j], 16)

            def macro(m, q, u, more=True):
                if more:
                    load(*next_of(m, q, u))
                sp.dma_start(acc_macros[m], bc(blank[:, :].unsqueeze(1), [P, TM, AW])).then_inc(blanked, 16)
                for j in range(TM):
                    n = m * TM + j
                    sp.wait_ge(kept, n + 1 + 2)
                    hold(sp, passed)
                    sp.dma_start(dram["xnT"][m, :, :, j * P:(j + 1) * P], xT[:, j, :, :]).then_inc(t_stored[j], 16)
                    sp.wait_ge(biased, n + 1 + 2)
                    hold(sp, passed)
                    sp.dma_start(v_rows[n], vr[:, j, :, :].rearrange("p a w -> p (a w)")[:, 0:VW]).then_inc(v_stored[j], 16)
                    sp.dma_start(er_rows[n], vr[:, j, 1, VH - H:VH]).then_inc(v_stored[j], 16)
            acc_macros = dram["acc"][0:NP, :].rearrange("(m j p) w -> m p j w", j=TM, p=P)
            load(0, 0, 0)
            sp.wait_ge(blanks, 2)
            sp.dma_start(dram["acc"][NP:NP + GH, :], blank[0:GH, :]).then_inc(blanked, 16)
            sp.dma_start(dram["acc"][NP + GH:NP + NG, :], blank[0:GH, :]).then_inc(blanked, 16)
            over_macros(sp, macro, more=False)
            sp.wait_ge(blanked, 16 * (NM + 2))
            for j in range(TM):
                sp.wait_ge(t_stored[j], 16 * NM)
                sp.wait_ge(v_stored[j], 32 * NM)

        @block.gpsimd
        def _(pool):
            def look(m):
                pool.wait_ge(v, m * PLACED + GROUPED)
                hold(pool, passed_p)
                for j in range(TM):
                    pool.indirect_dma_start(out=row[:, j, :], out_offset=None, in_=dram["dst_f"],
                                            in_offset=bass.IndirectOffsetOnAxis(ap=gi[:, j:j + 1], axis=0)).then_inc(fetched[j], 16)

            def macro(m, q, u, more=True):
                if more:
                    look(m + 1)
                pool.wait_ge(v, m * PLACED + PLACED)
                hold(pool, passed_p)
                for j in range(TM):
                    pool.wait_ge(biased, m * TM + j + 1 + 2)
                    hold(pool, passed_p)
                    pool.indirect_dma_start(out=dram["er_edge"], out_offset=bass.IndirectOffsetOnAxis(ap=at[:, q, j:j + 1], axis=0),
                                            in_=vr[:, j, 1, VH - H:VH], in_offset=None, bounds_check=EP - 1,
                                            oob_is_err=False).then_inc(e_stored[j], 16)
            pool.iota(ids[:, :], [[P, NT]], base=0, channel_multiplier=1,
                      allow_small_or_imprecise_dtypes=True).then_inc(numbered, 1)
            look(0)
            over_macros(pool, macro, more=False)
            for j in range(TM):
                pool.wait_ge(e_stored[j], 16 * NM)

        @block.scalar
        def _(act):
            act.sem_inc(kept, 2)

            def root(m, q):
                act.wait_ge(v, m * PLACED + NORMED - 1)
                nc.scalar.activation(mom[:, q, :, 1], mom[:, q, :, 1], ACT.Sqrt).then_inc(rooted, 1)

            def macro(m, q, u, more=True):
                for j in range(TM):
                    n = m * TM + j
                    act.wait_ge(turned, n + 1 + 2 * TM)
                    act.wait_ge(projected, n + 1)
                    if later(m):
                        act.wait_ge(t_stored[j], m * 16)
                    nc.scalar.activation(xT[:, j, :, :].rearrange("p k t -> p (k t)"),
                                         pT[(q + j) % 2][:, :], ACT.Copy).then_inc(kept, 1)
                if more:
                    root(m + 1, 1 - q)
            root(0, 0)
            over_macros(act, macro, more=False)

        @block.vector
        def _(dve):
            nc.vector.memset(blank[:, 0:D + H], 0.0).then_inc(blanks, 1)
            nc.vector.memset(blank[:, D + H:AW], LOW).then_inc(blanks, 1)
            dve.sem_inc(biased, 2)

            def chain(m, done):
                def link(ins):
                    done[0] += 1
                    ins.then_inc(v, 1)
                    dve.wait_ge(v, m * PLACED + done[0])
                return link

            def search(m):
                for j in range(TM):
                    for a, op in enumerate((ALU.is_lt, ALU.is_equal)):
                        nc.vector.tensor_scalar(junk[:, 2 * j + a, :], C["begin"][:, :], ids[:, bass.ds(m * TM + j, 1)], None, op,
                                                ALU.add, accum_out=below[:, a, j:j + 1]).then_inc(searched, 1)
                dve.wait_ge(searched, m * (2 * TM) + 2 * TM)
                done = [0]
                link = chain(m, done)
                link(nc.vector.tensor_scalar(group[:, :], below[:, 0, :], -1.0, 0.0, ALU.add, ALU.max))
                link(nc.vector.tensor_copy(gi[:, :], group[:, :]))
                assert done[0] == GROUPED

            def measure(m, q, u, j):
                dve.wait_ge(x_loaded[q][j], u * 16 + 16)
                nc.vector.bn_stats(st[:, j, :], xs[:, q, j, :]).then_inc(measured, 1)

            def count_edges(m, j):
                n = m * TM + j
                dve.wait_ge(fetched[j], m * 16 + 16)
                for a, op in enumerate((ALU.is_lt, ALU.is_equal)):
                    if later(n):
                        dve.wait_ge(counted, 2 * n - 1 + a)
                    nc.vector.tensor_scalar(seen[:, a, :], row[:, j, :], ids[:, bass.ds(n, 1)], None, op, ALU.add,
                                            accum_out=count[:, a, j:j + 1]).then_inc(counted, 1)
            def factors(m, q):
                dve.wait_ge(measured, m * TM + TM)
                hold(dve, passed_v)
                done = [GROUPED]
                link = chain(m, done)
                for j in range(TM):
                    last = nc.vector.bn_aggr(mom[:, q, j, :], st[:, j, :])
                link(last)
                link(nc.vector.tensor_scalar(mom[:, q, :, 1], mom[:, q, :, 1], LN_EPS, None, ALU.add))
                assert done[0] == NORMED - 1
                dve.wait_ge(rooted, m + 1)
                link(nc.vector.reciprocal(mom[:, q, :, 1], mom[:, q, :, 1]))

            def place(m, q):
                dve.wait_ge(counted, m * (2 * TM) + 2 * TM)
                done = [NORMED]
                link = chain(m, done)
                link(nc.vector.scalar_tensor_tensor(start[:, :], group[:, :], float(GE), count[:, 0, :], ALU.mult, ALU.add))
                link(nc.vector.tensor_tensor(some[:, :], count[:, 1, :], below[:, 1, :], ALU.add))
                link(nc.vector.tensor_scalar(some[:, :], some[:, :], 0.0, BIG, ALU.is_equal, ALU.mult))
                link(nc.vector.tensor_tensor(start[:, :], start[:, :], some[:, :], ALU.add))
                link(nc.vector.scalar_tensor_tensor(start[:, :], bc(C["orderly"][:, 1:2], [P, TM]), BIG, start[:, :], ALU.mult, ALU.add))
                place_edges(nc, link, start[:, :], ai, at[:, q, :])
                assert done[0] == PLACED

            def norm(m, q, j):
                nc.vector.tensor_scalar(xs[:, q, j, :], xs[:, q, j, :], mom[:, q, j, 0:1], mom[:, q, j, 1:2],
                                        ALU.subtract, ALU.mult).then_inc(normed, 1)

            def macro(m, q, u, more=True):
                for j in range(TM):
                    n = m * TM + j
                    if j + 2 < TM:
                        norm(m, q, j + 2)
                    elif more:
                        norm(m + 1, 1 - q, j + 2 - TM)
                    if more and j == 0:
                        search(m + 1)
                    if more and 1 <= j < TM - 3:
                        for i in range((j - 1) * TM // (TM - 4), j * TM // (TM - 4)):
                            measure(*next_of(m, q, u), i)
                            count_edges(m + 1, i)
                    if more and j == TM - 3:
                        factors(m + 1, 1 - q)
                        place(m + 1, 1 - q)
                    s = (q + j) % 2
                    dve.wait_ge(projected, n + 1 + TM)
                    if later(m):
                        dve.wait_ge(v_stored[j], m * 32)
                        dve.wait_ge(e_stored[j], m * 16)
                    nc.vector.tensor_tensor(vr[:, j, 0, :], pV[s][0][:, 0:VH], C["vbias"][:, 0:VH], ALU.add)
                    nc.vector.tensor_tensor(vr[:, j, 1, :], pV[s][1][:, 0:VH], C["vbias"][:, VH:2 * VH], ALU.add).then_inc(biased, 1)
            dve.wait_ge(numbered, 1)
            search(0)
            for j in range(TM):
                measure(0, 0, 0, j)
            factors(0, 0)
            norm(0, 0, 0)
            norm(0, 0, 1)
            for j in range(TM):
                count_edges(0, j)
            place(0, 0)
            over_macros(dve, macro, more=False)

        @block.tensor
        def _(pe):
            pe.sem_inc(turned, 2 * TM)
            pe.sem_inc(projected, TM)

            def turn(m, q, j):
                n = m * TM + j
                pe.wait_ge(normed, n + 1)
                pe.wait_ge(kept, n + 1)
                for k in range(KC):
                    last = nc.tensor.transpose(pT[(q + j) % 2][:, k * P:(k + 1) * P], xs[:, q, j, k * P:(k + 1) * P],
                                               C["ident"][:, :])
                last.then_inc(turned, 1)

            def macro(m, q, u, more=True):
                for j in range(TM):
                    n = m * TM + j
                    if j + 1 < TM:
                        turn(m, q, j + 1)
                    elif more:
                        turn(m + 1, 1 - q, 0)
                    s = (q + j) % 2
                    pe.wait_ge(kept, n + 1 + 2)
                    pe.wait_ge(biased, n + 1)
                    for half in range(2):
                        for k in range(KC):
                            last = nc.tensor.matmul(pV[s][half][:, 0:VH], xT[:, j, k, :], C["wval"][:, k, half * VH:(half + 1) * VH],
                                                    start=(k == 0), stop=(k == KC - 1))
                    last.then_inc(projected, 1)
            turn(0, 0, 0)
            over_macros(pe, macro, more=False)


def prep_edges(nc, C, dram):
    with Stage(nc) as ctx:
        ints = fixed(ctx, nc, "pe_ints", [GH, 2, 2, GE], I32)
        dst = fixed(ctx, nc, "pe_dst", [GH, 2, GE])
        bef = fixed(ctx, nc, "pe_bef", [GH, 2, GE])
        first = fixed(ctx, nc, "pe_first", [GH, 2, GE + 1])
        pen = fixed(ctx, nc, "pe_pen", [GH, 2, GE + 1])
        rank = fixed(ctx, nc, "pe_rank", [GH, 2, GE])
        zero = fixed(ctx, nc, "pe_zero", [GH, GE])
        tgt = fixed(ctx, nc, "pe_tgt", [GH, 2, GE])
        cont = fixed(ctx, nc, "pe_cont", [GH, 2, 3])
        row = fixed(ctx, nc, "pe_row", [GH, 2])
        bad = fixed(ctx, nc, "pe_bad", [GH, 6])
        
        nil = fixed(ctx, nc, "pe_nil", [P, EB])
        wide = fixed(ctx, nc, "pe_wide", [GH, 2, P])
        pw = psum(ctx, nc, "pe_pw")
        pc = psum(ctx, nc, "pe_pc")
        pt = [psum(ctx, nc, f"pe_pt{i}") for i in range(2)]
        loaded, rows_made, step, turned, kept, pen_stored, blanks, blanked, widened, spread, judged, counted = sems(
            ctx, nc, "pe", "loaded rows step turned kept pens blanks blanked widened spread judged counted")
        block = ctx.enter_context(nc.Block())

        @block.sync
        def _(sp):
            for a, name in enumerate(("dst", "dst_before")):
                for hf in range(2):
                    sp.dma_start(ints[:, a, hf, :], dram[name].rearrange("(c p e) -> c p e", c=2, p=GH)[hf]).then_inc(loaded, 16)
            sp.wait_ge(blanks, 1)
            sp.dma_start(dram["er_edge"].rearrange("(p b) h -> p (b h)", p=P).rearrange("p (n w) -> p n w", w=EB),
                         bc(nil[:, :].unsqueeze(1), [P, EP * H // P // EB, EB])).then_inc(blanked, 16)
            sp.wait_ge(step, 1)
            sp.dma_start(dram["dst_f"].rearrange("(c p) e -> p c e", p=GH), dst[:, :, :]).then_inc(pen_stored, 16)
            sp.wait_ge(step, 6)
            sp.dma_start(dram["pen"].rearrange("(c p) e -> p c e", p=GH), pen[:, :, :]).then_inc(pen_stored, 16)
            sp.wait_ge(pen_stored, 32)
            sp.wait_ge(blanked, 16)

        @block.gpsimd
        def _(pool):
            pool.iota(row[:, :], [[GH, 2]], base=NP, channel_multiplier=1,
                      allow_small_or_imprecise_dtypes=True).then_inc(rows_made, 1)

        @block.vector
        def _(dve):
            nc.vector.memset(nil[:, :], 0.0).then_inc(blanks, 1)
            nc.vector.memset(zero[:, :], 0.0)
            dve.wait_ge(loaded, 64)
            nc.vector.tensor_copy(dst[:, :, :], ints[:, 0, :, :])
            nc.vector.tensor_copy(bef[:, :, :], ints[:, 1, :, :]).then_inc(step, 1)
            dve.wait_ge(step, 1)
            nc.vector.tensor_tensor(first[:, :, 0:GE], dst[:, :, :], bef[:, :, :], ALU.not_equal)
            nc.vector.tensor_tensor(cont[:, :, 0], dst[:, :, 0], bef[:, :, 0], ALU.is_equal).then_inc(step, 1)
            dve.wait_ge(step, 2)
            dve.wait_ge(rows_made, 1)
            nc.vector.tensor_copy(wide[:, :, :], bc(dst[:, :, 0:1], [GH, 2, P])).then_inc(widened, 1)
            nc.vector.tensor_tensor(tgt[:, :, :], dst[:, :, :], bef[:, :, :], ALU.is_lt).then_inc(judged, 1)
            dve.wait_ge(judged, 1)
            nc.vector.tensor_reduce(bad[:, 0:2], tgt[:, :, :], AX.X, ALU.max).then_inc(judged, 1)
            dve.wait_ge(judged, 2)
            nc.vector.memset(first[:, :, 0:1], 1.0)
            nc.vector.memset(first[:, :, GE:GE + 1], 1.0)
            nc.vector.tensor_tensor(cont[:, :, 1], row[:, :], dst[:, :, 0], ALU.subtract).then_inc(step, 1)
            dve.wait_ge(step, 3)
            for hf in range(2):
                nc.vector.tensor_tensor_scan(rank[:, hf, :], first[:, hf, 0:GE], zero[:, :], -1.0, ALU.add, ALU.max)
            nc.vector.tensor_tensor(cont[:, :, 1], cont[:, :, 1], cont[:, :, 0], ALU.mult).then_inc(step, 1)
            dve.wait_ge(step, 4)
            nc.vector.tensor_scalar(bad[:, 2:4], rank[:, :, GE - 1], float(P - 1), None, ALU.is_gt).then_inc(judged, 1)
            dve.wait_ge(judged, 3)
            nc.vector.tensor_reduce(bad[:, 4:5], bad[:, 0:4], AX.X, ALU.max).then_inc(judged, 1)
            nc.vector.tensor_scalar(tgt[:, :, :], dst[:, :, :], -BIG, None, ALU.add).then_inc(step, 1)
            dve.wait_ge(step, 5)
            nc.vector.tensor_scalar(pen[:, :, :], first[:, :, :], LOW, None, ALU.mult).then_inc(step, 1)
            dve.wait_ge(counted, 1)
            nc.vector.tensor_scalar(C["orderly"][:, 0:1], pc[:, 0:1], 0.0, None, ALU.is_equal)
            nc.vector.tensor_scalar(C["orderly"][:, 1:2], pc[:, 0:1], 0.0, None, ALU.is_gt).then_inc(judged, 1)
            dve.wait_ge(judged, 5)
            nc.vector.tensor_copy(C["general"][:, :], C["orderly"][0:1, 1:2])
            nc.vector.tensor_tensor(cont[:, :, 2], tgt[:, :, 0], cont[:, :, 0], ALU.mult).then_inc(step, 1)
            dve.wait_ge(step, 7)
            nc.vector.tensor_scalar(C["own"][:, :], cont[:, :, 2], C["orderly"][0:GH, 0:1], BIG, ALU.mult, ALU.add).then_inc(step, 1)
            nc.vector.tensor_tensor(tgt[:, :, 0], tgt[:, :, 0], cont[:, :, 1], ALU.add).then_inc(step, 1)
            dve.wait_ge(step, 9)
            nc.vector.tensor_tensor(tgt[:, :, :], tgt[:, :, :], first[:, :, 0:GE], ALU.mult).then_inc(step, 1)
            dve.wait_ge(spread, 1)
            nc.vector.tensor_copy(C["begin"][:, :], pw[:, 0:NG])
            for t in range(4):
                hf, a = divmod(t, 2)
                dve.wait_ge(turned, t + 1)
                out = (C["rank"], C["target"])[a]
                nc.vector.tensor_scalar(out[:, hf * GH * GT:(hf + 1) * GH * GT].rearrange("q (p s) -> q s p", s=GT),
                                        pt[t % 2][:, 0:GT * GH].rearrange("q (s p) -> q s p", s=GT),
                                        C["orderly"][:, 0:1], None, ALU.mult).then_inc(kept, 1)
            dve.wait_ge(kept, 4)
            nc.vector.tensor_scalar(C["first"][:, :], C["target"][:, :], 0.0, None, ALU.not_equal).then_inc(step, 1)
            dve.wait_ge(step, 11)

        @block.tensor
        def _(pe):
            pe.wait_ge(widened, 1)
            for hf in range(2):
                last = nc.tensor.transpose(pw[:, hf * GH:(hf + 1) * GH], wide[:, hf, :], C["ident"][0:GH, 0:GH])
            last.then_inc(spread, 1)
            pe.wait_ge(judged, 4)
            nc.tensor.matmul(pc[:, 0:1], C["ones"][0:GH, :], bad[:, 4:5], start=True, stop=True).then_inc(counted, 1)
            pe.wait_ge(step, 10)
            for t in range(4):
                hf, a = divmod(t, 2)
                if t >= 2:
                    pe.wait_ge(kept, t - 1)
                for s in range(GT):
                    last = nc.tensor.transpose(pt[t % 2][:, s * GH:(s + 1) * GH], (rank, tgt)[a][:, hf, s * P:(s + 1) * P],
                                               C["ident"][0:GH, 0:GH])
                last.then_inc(turned, 1)


def place_edges(nc, link, edge, ai, out):
    eb, tb, gb = (x.bit_length() - 1 for x in (P, GT, SG))
    link(nc.vector.tensor_copy(ai[:, 0, :], edge))
    nc.vector.tensor_scalar(ai[:, 1, :], ai[:, 0, :], P - 1, tb + gb, ALU.bitwise_and, ALU.logical_shift_left)
    nc.vector.tensor_scalar(ai[:, 3, :], ai[:, 0, :], eb + tb, SG - 1, ALU.logical_shift_right, ALU.bitwise_and)
    link(nc.vector.tensor_scalar(ai[:, 2, :], ai[:, 0, :], eb, GT - 1, ALU.logical_shift_right, ALU.bitwise_and))
    nc.vector.tensor_tensor(ai[:, 1, :], ai[:, 1, :], ai[:, 3, :], ALU.bitwise_or)
    link(nc.vector.tensor_scalar(ai[:, 4, :], ai[:, 2, :], gb, None, ALU.logical_shift_left))
    link(nc.vector.tensor_scalar(ai[:, 0, :], ai[:, 0, :], -SG * GE, None, ALU.bitwise_and))
    link(nc.vector.tensor_tensor(ai[:, 2, :], ai[:, 1, :], ai[:, 4, :], ALU.bitwise_or))
    link(nc.vector.tensor_tensor(out, ai[:, 0, :], ai[:, 2, :], ALU.bitwise_or))


def spread_er(nc, C, dram, ctx, banks):
    SE = SG * GT * H
    SR = SG * H
    NS = NG // SG
    EACH = 2 * 16
    dst = fixed(ctx, nc, "se_dst", [GH, 2], I32)
    num = fixed(ctx, nc, "se_num", [GH, 2])
    ai = fixed(ctx, nc, "se_ai", [GH, 5, 2], I32)
    at = fixed(ctx, nc, "se_at", [GH, 2], I32)
    lead = fixed(ctx, nc, "se_lead", [GH, 2, H])
    raw = fixed(ctx, nc, "se_raw", [P, 2, SE])
    pen = fixed(ctx, nc, "se_pen", [SR, 2, GE])
    go = fixed(ctx, nc, "se_go", [SR, 2, GE])
    er = fixed(ctx, nc, "se_er", [SR, 2, GE])
    pt, pb = banks[0:2], banks[2:4]
    first, made, v, fetched, led = sems(ctx, nc, "se", "first made v fetched led")
    loaded = sems(ctx, nc, "se", "l0 l1")
    turned, going, spread, back, kept, passed, passed_pe = sems(
        ctx, nc, "se", "turned going spread back kept passed passedpe")

    def steps(eng, body):
        body(0, 0, 0)
        body(1, 1, 0)
        with eng.Fori(1, NS // 2) as i:
            body(i * 2, 0, i)
            body(i * 2 + 1, 1, i)
        if NS % 2:
            body(NS - 1, 0, NS // 2)

    def by_sync(sp):
        for hf in range(2):
            sp.dma_start(dst[:, hf:hf + 1], dram["dst"].rearrange("(c p e) -> c p e", c=2, p=GH)[hf, :, 0:1],
                         allow_slow_non_contiguous=True).then_inc(first, 16)
        sp.wait_ge(led, 32)

        def step(k, q, u):
            sp.wait_ge(spread, k + 1)
            hold(sp, passed)
            sp.dma_start(raw[:, q, :], er_steps[k]).then_inc(loaded[q], 16)
            sp.dma_start(pen[:, q, :], bc(dram["pen"][bass.ds(k * SG, SG), 0:GE].unsqueeze(1), [SG, H, GE])).then_inc(loaded[q], 16)
        er_steps = dram["er_edge"].rearrange("(k p t) h -> k p (t h)", p=P, t=SG * GT)
        steps(sp, step)

    def by_pool(pool):
        pool.iota(num[:, :], [[GH, 2]], base=0, channel_multiplier=1,
                  allow_small_or_imprecise_dtypes=True).then_inc(made, 1)
        pool.wait_ge(first, 32)
        pool.wait_ge(v, 7)
        for hf in range(2):
            pool.indirect_dma_start(out=lead[:, hf, :], out_offset=None, in_=dram["ertab"],
                                    in_offset=bass.IndirectOffsetOnAxis(ap=dst[:, hf:hf + 1], axis=0)).then_inc(fetched, 16)
        pool.wait_ge(fetched, 32)
        for hf in range(2):
            pool.indirect_dma_start(out=dram["er_edge"], out_offset=bass.IndirectOffsetOnAxis(ap=at[:, hf:hf + 1], axis=0),
                                    in_=lead[:, hf, :], in_offset=None).then_inc(led, 16)

    def by_vector(dve):
        done = [0]

        def link(ins):
            done[0] += 1
            ins.then_inc(v, 1)
            dve.wait_ge(v, done[0])
        dve.wait_ge(made, 1)
        link(nc.vector.tensor_scalar(num[:, :], num[:, :], float(GE), None, ALU.mult))
        place_edges(nc, link, num[:, :], ai, at[:, :])
        assert done[0] == 7
        dve.sem_inc(spread, 2)

        def step(k, q, u):
            dve.wait_ge(loaded[q], u * EACH + EACH)
            if later(k):
                dve.wait_ge(back, k)
            nc.vector.tensor_scalar(go[:, q, :], pen[:, q, :], 0.0, None, ALU.is_equal).then_inc(going, 1)
            dve.wait_ge(going, k + 1)
            dve.wait_ge(turned, k + 1)
            nc.vector.tensor_tensor_scan(er[:, q, :], go[:, q, :], pt[q][0:SR, :], 0.0, ALU.mult, ALU.add).then_inc(spread, 1)
        steps(dve, step)
        dve.wait_ge(kept, NS + 2)

    def by_scalar(act):
        def step(k, q, u):
            act.wait_ge(back, k + 1 + 1)
            nc.scalar.activation(C["er"][:, bass.ds(k * SG * GT * H, SG * GT * H)].rearrange("p (g s h) -> p s g h", s=GT, h=H),
                                 pb[q][:, 0:SE].rearrange("p (s g h) -> p s g h", s=GT, h=H), ACT.Copy).then_inc(kept, 1)
        act.sem_inc(kept, 2)
        steps(act, step)
        act.wait_ge(kept, NS + 2)

    def by_tensor(pe):
        pe.sem_inc(back, 1)

        def forth(k, q, u):
            pe.wait_ge(loaded[q], u * EACH + EACH)
            pe.wait_ge(spread, k + 1)
            hold(pe, passed_pe)
            for s in range(GT):
                last = nc.tensor.transpose(pt[q][0:SR, s * P:(s + 1) * P],
                                           raw[:, q, s * SR:(s + 1) * SR], C["ident"][:, :])
            last.then_inc(turned, 1)

        def returned(k, q, u):
            pe.wait_ge(spread, k + 1 + 2)
            pe.wait_ge(kept, k + 1)
            hold(pe, passed_pe)
            for s in range(GT):
                last = nc.tensor.transpose(pb[q][:, s * SR:(s + 1) * SR], er[:, q, s * P:(s + 1) * P], C["ident"][0:SR, 0:SR])
            last.then_inc(back, 1)

        def step(k, q, u):
            forth(k, q, u)
            returned(k, q, u)
        steps(pe, step)
    return by_sync, by_pool, by_vector, by_scalar, by_tensor


def edge_attention(nc, C, dram):
    with Stage(nc) as ctx:
        GC = BG * H
        ix = fixed(ctx, nc, "ea_ix", [P, RS, BT], I32)
        rows = fixed(ctx, nc, "ea_rows", [P, RS, BT, VW])
        z = fixed(ctx, nc, "ea_z", [P, BT * H])
        e = fixed(ctx, nc, "ea_e", [P, BT * H])
        pen = fixed(ctx, nc, "ea_pen", [GC, RS, GE + 1])
        run = fixed(ctx, nc, "ea_run", [GC, GE])
        top = fixed(ctx, nc, "ea_top", [GC, GE])
        wt = fixed(ctx, nc, "ea_wt", [GC, GE])
        ext = fixed(ctx, nc, "ea_ext", [P, RS, BT, XW])
        hot = fixed(ctx, nc, "ea_hot", [P, 2, GT, P])
        sums = fixed(ctx, nc, "ea_sums", [P, BG, AW])
        at = fixed(ctx, nc, "ea_at", [P, BG, 1], I32)
        pz = psum(ctx, nc, "ea_pz")
        pb = psum(ctx, nc, "ea_pb")
        pn = [psum(ctx, nc, f"ea_pn{i}") for i in range(2)]
        px = [psum(ctx, nc, f"ea_px{i}") for i in range(2)]
        ix_loaded = sems(ctx, nc, "ea", " ".join(f"ix{q}" for q in range(RS)))
        gathered = sems(ctx, nc, "ea", " ".join(f"ga{q}" for q in range(RS)))
        scattered = sems(ctx, nc, "ea", " ".join(f"sc{g}" for g in range(BG)))
        (raw, scored, turned, ran, topped, scanned, weighted, back, extras, scaled, hotted, grouped,
         evacuated) = sems(ctx, nc, "ea", "raw scored turned ran topped scanned weighted back extras scaled hotted "
                                          "grouped evacuated")
        pool_passed, sp_passed, pe_passed = sems(ctx, nc, "ea", "pool_passed sp_passed pe_passed")
        spread_sync, spread_pool, spread_vector, spread_scalar, spread_tensor = spread_er(nc, C, dram, ctx, pn + px)
        block = ctx.enter_context(nc.Block())
        NB = -(-E // (BT * P))
        LOOPS = NB // RS
        assert NB == LOOPS * RS + 1
        GS = BT * 16

        def pipelined(eng, head, step):
            head(0, 0, 0)
            for q in range(RS):
                step(q, q, 0, True)
            with eng.Fori(1, LOOPS) as i:
                for q in range(RS):
                    step(i * RS + q, q, i, True)
            step(NB - 1, 0, LOOPS, False)

        def after(q, u):
            return (q + 1, u) if q + 1 < RS else (0, u + 1)

        @block.sync
        def _(sp):
            def batch(b, q, u):
                if later(u):
                    sp.wait_ge(gathered[q], u * GS)
                hold(sp, sp_passed)
                sp.wait_ge(scanned, b + 1)
                hold(sp, sp_passed)
                sp.dma_start(ix[:, q, :], dram["src_em"][b]).then_inc(ix_loaded[q], 16)
                sp.dma_start(pen[:, q, :], bc(dram["pen"][bass.ds(b * BG, BG), :].unsqueeze(1), [BG, H, GE + 1])).then_inc(ix_loaded[q], 16)
            for q in range(RS):
                batch(q, q, 0)
            spread_sync(sp)
            with sp.Fori(1, LOOPS) as i:
                for q in range(RS):
                    batch(i * RS + q, q, i)
            batch(NB - 1, 0, LOOPS)

        @block.gpsimd
        def _(pool):
            def gather(b, q, u, full):
                pool.wait_ge(ix_loaded[q], u * 32 + 32)
                hold(pool, pool_passed)
                for t in range(BT):
                    if full and t % GT == 0:
                        pool.wait_ge(grouped, (b - RS) * BG + t // GT + 1 + 2)
                        hold(pool, pool_passed)
                    pool.indirect_dma_start(out=rows[:, q, t, :], out_offset=None, in_=dram["vtab"],
                                            in_offset=bass.IndirectOffsetOnAxis(ap=ix[:, q, t:t + 1], axis=0)).then_inc(gathered[q], 16)
                    if full and t % GT == GT - 1 and t >= GT:
                        scatter(b - 2, t // GT - 1)
                if full:
                    scatter(b - 2, BG - 1)

            def scatter(b, g):
                pool.wait_ge(evacuated, b * BG + g + 1 + 2)
                hold(pool, pool_passed)
                pool.indirect_dma_start(out=dram["acc"], out_offset=bass.IndirectOffsetOnAxis(ap=at[:, g, 0:1], axis=0),
                                        in_=sums[:, g, :], in_offset=None, bounds_check=NP + NG - 1,
                                        oob_is_err=False).then_inc(scattered[g], 16)
            spread_pool(pool)
            for q in range(RS):
                gather(q, q, 0, False)
            for g in range(BG):
                scatter(0, g)
            with pool.Fori(1, LOOPS) as i:
                for q in range(RS):
                    gather(i * RS + q, q, i, True)
            gather(NB - 1, 0, LOOPS, True)
            for b in (NB - 2, NB - 1):
                for g in range(BG):
                    scatter(b, g)
            for g in range(BG):
                pool.wait_ge(scattered[g], NB * 16)

        @block.vector
        def _(dve):
            dve.sem_inc(scanned, RS)
            spread_vector(dve)

            def score(b, q, u):
                dve.wait_ge(gathered[q], u * GS + GS)
                nc.vector.tensor_tensor(z[:, :].rearrange("p (s g h) -> p s g h", s=GT, g=BG),
                                        rows[:, q, :, D:VW].rearrange("p (g s) h -> p s g h", s=GT),
                                        C["er"][:, bass.ds(b * (BT * H), BT * H)].rearrange("p (g s h) -> p s g h", s=GT, h=H), ALU.add).then_inc(raw, 1)
                dve.wait_ge(raw, b + 1)
                nc.vector.scalar_tensor_tensor(e[:, :], z[:, :], SLOPE, z[:, :], ALU.mult, ALU.max).then_inc(scored, 1)

            def scan(b, q, u):
                dve.wait_ge(turned, b + 1)
                dve.wait_ge(ix_loaded[q], u * 32 + 32)
                nc.vector.tensor_tensor_scan(run[:, :], pen[:, q, 0:GE], pz[0:GC, :], LOW, ALU.add, ALU.max).then_inc(ran, 1)
                dve.wait_ge(ran, b + 1)
                nc.vector.tensor_tensor_scan(top[:, ::-1], pen[:, q, GE:0:-1], run[:, ::-1], LOW,
                                             ALU.add, ALU.max).then_inc(topped, 1)
                dve.wait_ge(topped, b + 1)
                nc.vector.tensor_tensor(wt[:, :], pz[0:GC, :], top[:, :], ALU.subtract).then_inc(scanned, 1)

            def extend(b, q):
                dve.wait_ge(back, b + 1)
                nc.vector.tensor_copy(ext[:, q, :, 0:H].rearrange("p (g s) h -> p s g h", s=GT),
                                      pb[:, 0:BT * H].rearrange("p (s g h) -> p s g h", s=GT, g=BG))
                nc.vector.tensor_tensor(ext[:, q, :, H:2 * H].rearrange("p (g s) h -> p s g h", s=GT),
                                        pb[:, BT * H:2 * BT * H].rearrange("p (s g h) -> p s g h", s=GT, g=BG),
                                        bc(C["first"][:, bass.ds(b * BT, BT)].rearrange("p (g s) -> p s g", s=GT).unsqueeze(3),
                                           [P, GT, BG, H]), ALU.mult)
                nc.vector.tensor_copy(ext[:, q, :, 2 * H], C["target"][:, bass.ds(b * BT, BT)]).then_inc(extras, 1)

            def scale(b, q, g):
                n = b * BG + g
                part = rows[:, q, g * GT:(g + 1) * GT, 0:D].rearrange("p s (h f) -> p s h f", f=HF)
                nc.vector.tensor_tensor(part, part, bc(ext[:, q, g * GT:(g + 1) * GT, 0:H].unsqueeze(3), [P, GT, H, HF]),
                                        ALU.mult).then_inc(scaled, 1)
                dve.wait_ge(grouped, n + 1)
                nc.vector.tensor_tensor(hot[:, g % 2, :, :], bc(C["cols"][:, :].unsqueeze(1), [P, GT, P]),
                                        bc(C["rank"][:, bass.ds(n * GT, GT)].unsqueeze(2), [P, GT, P]),
                                        ALU.is_equal).then_inc(hotted, 1)

            def head(b, q, u):
                score(b, q, u)
                scan(b, q, u)
                extend(b, q)

            def step(b, q, u, more):
                nq, nu = after(q, u)
                dve.wait_ge(extras, b + 1)
                scale(b, q, 0)
                if more:
                    score(b + 1, nq, nu)
                scale(b, q, 1)
                if more:
                    scan(b + 1, nq, nu)
                scale(b, q, 2)
                scale(b, q, 3)
                if more:
                    extend(b + 1, nq)
            pipelined(dve, head, step)

        @block.scalar
        def _(act):
            spread_scalar(act)
            act.sem_inc(evacuated, 2)

            def head(b, q, u):
                act.wait_ge(scanned, b + 1 + RS)
                nc.scalar.activation(wt[:, :], wt[:, :], ACT.Exp).then_inc(weighted, 1)

            def step(b, q, u, more):
                nq, nu = after(q, u)
                for g in range(BG):
                    n = b * BG + g
                    act.wait_ge(grouped, n + 1 + 2)
                    if later(b):
                        act.wait_ge(scattered[g], b * 16)
                    nc.scalar.activation(sums[:, g, 0:D], pn[g % 2][:, :], ACT.Copy)
                    nc.scalar.activation(sums[:, g, D:AW], px[g % 2][:, 0:2 * H], ACT.Copy)
                    nc.scalar.activation(at[:, g, :], px[g % 2][:, 2 * H:XW], ACT.Copy, bias=BIG).then_inc(evacuated, 1)
                    if g == 0 and more:
                        head(b + 1, nq, nu)
            pipelined(act, head, step)

        @block.tensor
        def _(pe):
            pe.sem_inc(grouped, 2)
            spread_tensor(pe)

            def forth(b, q):
                pe.wait_ge(scored, b + 1)
                pe.wait_ge(scanned, b + RS)
                for s in range(GT):
                    last = nc.tensor.transpose(pz[0:GC, s * P:(s + 1) * P], e[:, s * GC:(s + 1) * GC], C["ident"][:, :])
                last.then_inc(turned, 1)

            def returned(b, q):
                pe.wait_ge(weighted, b + 1)
                if later(b):
                    pe.wait_ge(extras, b)
                hold(pe, pe_passed)
                for a, src in enumerate((wt, top)):
                    for s in range(GT):
                        last = nc.tensor.transpose(pb[:, a * BT * H + s * GC:a * BT * H + (s + 1) * GC],
                                                   src[:, s * P:(s + 1) * P], C["ident"][0:GC, 0:GC])
                last.then_inc(back, 1)

            def head(b, q, u):
                forth(b, q)
                returned(b, q)

            def step(b, q, u, more):
                nq, nu = after(q, u)
                for g in range(BG):
                    n = b * BG + g
                    pe.wait_ge(scaled, n + 1)
                    pe.wait_ge(hotted, n + 1)
                    pe.wait_ge(evacuated, n + 1)
                    for s in range(GT):
                        t = g * GT + s
                        nc.tensor.matmul(pn[g % 2][:, :], hot[:, g % 2, s, :], rows[:, q, t, 0:D], start=(s == 0), stop=(s == GT - 1))
                        last = nc.tensor.matmul(px[g % 2][:, 0:XW], hot[:, g % 2, s, :], ext[:, q, t, :],
                                                start=(s == 0), stop=(s == GT - 1))
                    last.then_inc(grouped, 1)
                    if g == 0 and more:
                        forth(b + 1, nq)
                    if g == 2 and more:
                        returned(b + 1, nq)
            pipelined(pe, head, step)


def merge_rows(nc, C, dram, carried):
    with Stage(nc) as ctx:
        R = GH if carried else P
        name = "mg" if carried else "me"
        part = fixed(ctx, nc, name + "_part", [R, AW])
        own = fixed(ctx, nc, name + "_own", [R, AW])
        wide = fixed(ctx, nc, name + "_wide", [R, H + 1, R])
        same = fixed(ctx, nc, name + "_same", [R, R])
        off = fixed(ctx, nc, name + "_off", [R, R])
        work = fixed(ctx, nc, name + "_work", [R, H, R])
        peak = fixed(ctx, nc, name + "_peak", [R, 4, H])
        lead = fixed(ctx, nc, name + "_lead", [R, 4])
        goal = fixed(ctx, nc, name + "_goal", [R, 1])
        ids = fixed(ctx, nc, name + "_ids", [R, 2, 1], I32)
        out = fixed(ctx, nc, name + "_out", [R, AW])
        ends = fixed(ctx, nc, name + "_ends", [R, 2], I32)
        er = fixed(ctx, nc, name + "_er", [R, 2, H])
        blank = fixed(ctx, nc, name + "_blank", [R, AW])
        pt = [psum(ctx, nc, f"{name}_pt{i}") for i in range(3)]
        pn = psum(ctx, nc, name + "_pn")
        px = psum(ctx, nc, name + "_px")
        loaded, given, fetched, stored, v, t, s, m, blanks, blanked, passed, passed_s = sems(
            ctx, nc, name, "loaded given fetched stored v t s m blanks blanked passed passeds")
        block = ctx.enter_context(nc.Block())

        A = 0 if carried else 2
        V = 12 + A

        def steps(eng, body):
            if carried:
                body(0)
                body(1)
                return
            flag = eng.value_load(C["general"][0:1, 0:1], min_val=0, max_val=1)
            with eng.If(flag > 0):
                body(0)
                with eng.Fori(1, -(-E // P)) as k:
                    body(k)
            hold(eng, passed)

        @block.sync
        def _(sp):
            def step(k):
                if carried:
                    if k:
                        sp.wait_ge(v, V)
                    sp.dma_start(part[:, :], dram["acc"][NP + k * GH:NP + (k + 1) * GH, :]).then_inc(loaded, 16)
                    return
                if not later(k):
                    sp.wait_ge(blanks, 2)
                    sp.dma_start(dram["acc"][0:NP, :].rearrange("(n p) w -> p n w", p=P),
                                 bc(blank[:, :].unsqueeze(1), [P, NT, AW])).then_inc(blanked, 16)
                else:
                    sp.wait_ge(v, k * V)
                    hold(sp, passed_s)
                sp.dma_start(ends[:, 0:1], edge_src[k]).then_inc(loaded, 16)
                sp.dma_start(ends[:, 1:2], edge_dst[k]).then_inc(loaded, 16)
            edge_src = dram["src"].rearrange("(t p c) -> t p c", p=P, c=1)
            edge_dst = dram["dst"].rearrange("(t p c) -> t p c", p=P, c=1)
            steps(sp, step)

        @block.gpsimd
        def _(pool):
            def step(k):
                if not carried:
                    pool.wait_ge(loaded, k * 32 + 32)
                    if later(k):
                        pool.wait_ge(v, k * V)
                    hold(pool, passed)
                    pool.indirect_dma_start(out=part[:, 0:VW], out_offset=None, in_=dram["vtab"],
                                            in_offset=bass.IndirectOffsetOnAxis(ap=ends[:, 0:1], axis=0)).then_inc(given, 16)
                    pool.indirect_dma_start(out=er[:, 0, :], out_offset=None, in_=dram["ertab"],
                                            in_offset=bass.IndirectOffsetOnAxis(ap=ends[:, 1:2], axis=0)).then_inc(given, 16)
                    pool.wait_ge(blanked, 16)
                pool.wait_ge(v, k * V + 1)
                hold(pool, passed)
                pool.indirect_dma_start(out=own[:, :], out_offset=None, in_=dram["acc"],
                                        in_offset=bass.IndirectOffsetOnAxis(ap=ids[:, 0, :], axis=0),
                                        bounds_check=NP - 1, oob_is_err=False).then_inc(fetched, 16)
                pool.wait_ge(v, k * V + V)
                hold(pool, passed)
                pool.indirect_dma_start(out=dram["acc"], out_offset=bass.IndirectOffsetOnAxis(ap=ids[:, 1, :], axis=0),
                                        in_=out[:, :], in_offset=None, bounds_check=NP - 1,
                                        oob_is_err=False).then_inc(stored, 16)
                pool.wait_ge(stored, k * 16 + 16)
                hold(pool, passed)
            steps(pool, step)

        @block.scalar
        def _(act):
            def step(k):
                act.wait_ge(v, k * V + A + 9)
                nc.scalar.activation(peak[:, 2:4, :], peak[:, 2:4, :], ACT.Exp).then_inc(s, 1)
            steps(act, step)

        @block.vector
        def _(dve):
            if not carried:
                nc.vector.memset(blank[:, 0:D + H], 0.0).then_inc(blanks, 1)
                nc.vector.memset(blank[:, D + H:AW], LOW).then_inc(blanks, 1)

            def step(k):
                done = [0]

                def link(ins):
                    done[0] += 1
                    ins.then_inc(v, 1)
                    dve.wait_ge(v, k * V + done[0])

                if carried:
                    if k:
                        dve.wait_ge(stored, 16)
                    nc.vector.tensor_copy(goal[:, :], C["own"][:, k:k + 1])
                    nc.vector.tensor_copy(ids[:, 0, :], C["own"][:, k:k + 1])
                else:
                    if later(k):
                        dve.wait_ge(stored, k * 16)
                    dve.wait_ge(loaded, k * 32 + 32)
                    nc.vector.tensor_copy(goal[:, :], ends[:, 1:2])
                    nc.vector.tensor_copy(ids[:, 0, :], ends[:, 1:2])
                link(nc.vector.memset(own[:, :], 0.0))
                if carried:
                    dve.wait_ge(loaded, k * 16 + 16)
                else:
                    dve.wait_ge(given, k * 32 + 32)
                    link(nc.vector.tensor_tensor(er[:, 1, :], part[:, D:VW], er[:, 0, :], ALU.add))
                    nc.vector.scalar_tensor_tensor(part[:, D + H:AW], er[:, 1, :], SLOPE, er[:, 1, :], ALU.mult, ALU.max)
                    link(nc.vector.memset(part[:, D:D + H], 1.0))
                assert done[0] == A + 1
                nc.vector.tensor_copy(wide[:, 0:H, :], bc(part[:, D + H:AW].unsqueeze(2), [R, H, R]))
                link(nc.vector.tensor_copy(wide[:, H, :], bc(goal[:, :], [R, R])))
                dve.wait_ge(t, k + 1)
                link(nc.vector.tensor_scalar(same[:, :], pt[2][0:R, 0:R], goal[:, :], None, ALU.is_equal))
                nc.vector.tensor_scalar(off[:, :], same[:, :], -1.0, -LOW, ALU.add, ALU.mult)
                for b in range(2):
                    last = nc.vector.tensor_tensor(work[:, 4 * b:4 * b + 4, :], pt[b][0:R, 0:4 * R].rearrange("p (h c) -> p h c", h=4),
                                                   bc(same[:, :].unsqueeze(1), [R, 4, R]), ALU.mult)
                link(last)
                link(nc.vector.tensor_tensor(work[:, :, :], work[:, :, :], bc(off[:, :].unsqueeze(1), [R, H, R]), ALU.add))
                link(nc.vector.tensor_reduce(peak[:, 0, :], work[:, :, :], AX.X, ALU.max))
                dve.wait_ge(fetched, k * 16 + 16)
                link(nc.vector.tensor_tensor(peak[:, 1, :], peak[:, 0, :], own[:, D + H:AW], ALU.max))
                nc.vector.tensor_tensor(peak[:, 2, :], part[:, D + H:AW], peak[:, 1, :], ALU.subtract)
                nc.vector.tensor_tensor(off[:, :], same[:, :], C["after"][0:R, 0:R], ALU.mult)
                link(nc.vector.tensor_copy(out[:, D + H:AW], peak[:, 1, :]))
                nc.vector.tensor_reduce(lead[:, 0:1], off[:, :], AX.X, ALU.add)
                link(nc.vector.tensor_tensor(peak[:, 3, :], own[:, D + H:AW], peak[:, 1, :], ALU.subtract))
                dve.wait_ge(s, k + 1)
                nc.vector.tensor_tensor(part[:, D:D + H], part[:, D:D + H], peak[:, 2, :], ALU.mult)
                nc.vector.tensor_scalar(lead[:, 1:2], lead[:, 0:1], BIG, None, ALU.mult)
                nc.vector.tensor_tensor(own[:, D:D + H], own[:, D:D + H], peak[:, 3, :], ALU.mult)
                nc.vector.tensor_tensor(own[:, 0:D].rearrange("p (h f) -> p h f", f=HF), own[:, 0:D].rearrange("p (h f) -> p h f", f=HF),
                                        bc(peak[:, 3, :].unsqueeze(2), [R, H, HF]), ALU.mult)
                link(nc.vector.tensor_tensor(part[:, 0:D].rearrange("p (h f) -> p h f", f=HF), part[:, 0:D].rearrange("p (h f) -> p h f", f=HF),
                                             bc(peak[:, 2, :].unsqueeze(2), [R, H, HF]), ALU.mult))
                link(nc.vector.tensor_tensor(lead[:, 2:3], lead[:, 1:2], goal[:, :], ALU.add))
                dve.wait_ge(m, k + 1)
                nc.vector.tensor_copy(ids[:, 1, :], lead[:, 2:3])
                nc.vector.tensor_tensor(out[:, D:D + H], px[0:R, 0:H], own[:, D:D + H], ALU.add)
                link(nc.vector.tensor_tensor(out[:, 0:D], pn[0:R, :], own[:, 0:D], ALU.add))
                assert done[0] == V
            steps(dve, step)

        @block.tensor
        def _(pe):
            def step(k):
                pe.wait_ge(v, k * V + A + 2)
                hold(pe, passed)
                for h in range(H + 1):
                    last = nc.tensor.transpose(pt[h // 4][0:R, (h % 4) * R:(h % 4 + 1) * R], wide[:, h, :], C["ident"][0:R, 0:R])
                last.then_inc(t, 1)
                pe.wait_ge(v, k * V + A + 10)
                hold(pe, passed)
                nc.tensor.matmul(pn[0:R, :], same[:, :], part[:, 0:D], start=True, stop=True)
                nc.tensor.matmul(px[0:R, 0:H], same[:, :], part[:, D:D + H], start=True, stop=True).then_inc(m, 1)
            steps(pe, step)


def load_feature_maps(nc, sp, tile, omega, loaded):
    sp.dma_start(tile[0:HF, 0:HF], omega).then_inc(loaded, 16)
    sp.dma_start(tile[HF:P, HF:P], omega).then_inc(loaded, 16)


def key_sums(nc, C, dram):
    with Stage(nc) as ctx:
        xT = fixed(ctx, nc, "ks_xT", [P, KC, MW])
        xTs = fixed(ctx, nc, "ks_xTs", [P, 2, 2, KC, MW], F32R)
        wk = fixed(ctx, nc, "ks_wk", [P, KC, D])
        wv = fixed(ctx, nc, "ks_wv", [P, KC, D])
        wks = fixed(ctx, nc, "ks_wks", [P, 2, KC, D], F32R)
        wvs = fixed(ctx, nc, "ks_wvs", [P, 2, KC, D], F32R)
        omega = fixed(ctx, nc, "ks_omega", [P, P])
        half = fixed(ctx, nc, "ks_half", [P, 2])
        kT = fixed(ctx, nc, "ks_kT", [P, KC, MW])
        k2 = fixed(ctx, nc, "ks_k2", [P, KC, MW])
        nrm = fixed(ctx, nc, "ks_nrm", [P, 2, H])
        feat = fixed(ctx, nc, "ks_feat", [P, 2, D])
        phi = fixed(ctx, nc, "ks_phi", [P, 2, D])
        vm = fixed(ctx, nc, "ks_vm", [P, 2, D])
        kv = fixed(ctx, nc, "ks_kv", [P, KC, P])
        tot = fixed(ctx, nc, "ks_tot", [P, D])
        pk = [psum(ctx, nc, f"ks_pk{i}") for i in range(2)]
        pf = psum(ctx, nc, "ks_pf")
        pq = psum(ctx, nc, "ks_pq")
        pv = [psum(ctx, nc, f"ks_pv{i}") for i in range(2)]
        pkv = psum(ctx, nc, "ks_pkv")
        pk1 = psum(ctx, nc, "ks_pone")
        blank = fixed(ctx, nc, "ks_blank", [P, 2 * D])
        loaded, wloaded, set_up, blanks, blanked = sems(ctx, nc, "ks", "loaded wloaded setup blanks blanked")
        (x_loaded, w_high, w_low, x_high, x_low, tallied, totalled, projected, kept, featured, normed, bounded, valued, cleared, mapped, copied, added, drained, masked, multiplied,
         moved, passed) = sems(ctx, nc, "ks", "xloaded whigh wlow xhigh xlow tallied totalled projected kept featured normed bounded valued cleared mapped copied added "
                                              "drained masked multiplied moved passed")
        block = ctx.enter_context(nc.Block())
        NC = 2 * KC

        @block.sync
        def _(sp):
            for w, name in ((wk, "Wk"), (wv, "Wv"), (C["wo"], "Wo")):
                sp.dma_start(w[:, :, :], dram[name].rearrange("(k p) n -> p k n", p=P)).then_inc(wloaded, 16)
            sp.wait_ge(set_up, 1)
            load_feature_maps(nc, sp, omega, dram["omega_k"], loaded)

            sp.dma_start(xT[:, :, :], dram["xnT"][0]).then_inc(x_loaded, 16)
            with sp.Fori(1, NM) as m:
                sp.wait_ge(x_low, m * KC)
                hold(sp, passed)
                sp.dma_start(xT[:, :, :], dram["xnT"][m]).then_inc(x_loaded, 16)

        @block.gpsimd
        def _(pool):
            pool.memset(blank[:, :], 0.0).then_inc(blanks, 1)
            pool.wait_ge(blanks, 1)
            for x in range(EX):
                pool.wait_ge(x_high, (x * (NM - 1) // EX) * KC + KC)
                pool.dma_start(dram["xe"].rearrange("(x p n) d -> x p (n d)", x=EX, p=P)[x].rearrange("p (n w) -> p n w", w=2 * D),
                               bc(blank[:, :].unsqueeze(1), [P, CAP // P // 2, 2 * D])).then_inc(blanked, 16)
            pool.wait_ge(blanked, 16 * EX)

        @block.scalar
        def _(act):
            act.sem_inc(copied, 1)
            act.sem_inc(mapped, 1)
            act.wait_ge(wloaded, 48)
            nc.scalar.activation(wks[:, 0, :, :], wk[:, :, :], ACT.Copy)
            nc.scalar.activation(wvs[:, 0, :, :], wv[:, :, :], ACT.Copy).then_inc(w_high, 1)

            def split(m, q, k):
                act.wait_ge(x_loaded, m * 16 + 16)
                if later(m) and later(m - 1):
                    act.wait_ge(valued, (m - 1) * TM)
                nc.scalar.activation(xTs[:, q, 0, k, :], xT[:, k, :], ACT.Copy).then_inc(x_high, 1)

            def macro(m, q, u, more=True):
                if later(m):
                    act.wait_ge(normed, m * TM)
                for c in range(NC):
                    n = m * NC + c
                    hf, k = divmod(c, KC)
                    act.wait_ge(projected, n + 1)
                    nc.scalar.activation(kT[:, k, hf * HW:(hf + 1) * HW], pk[c % 2][:, 0:HW], ACT.Copy)
                    nc.scalar.activation(k2[:, k, hf * HW:(hf + 1) * HW], pk[c % 2][:, 0:HW], ACT.Square).then_inc(kept, 1)
                for j in range(TM):
                    n = m * TM + j
                    s = (q + j) % 2
                    act.wait_ge(valued, n + 1)
                    if later(n):
                        act.wait_ge(added, n)
                    nc.scalar.activation(vm[:, s, :], pv[s][:, :], ACT.Copy).then_inc(copied, 1)
                    if more and j < KC:
                        split(m + 1, 1 - q, j)
                    act.wait_ge(featured, n + 1)
                    if later(n):
                        act.wait_ge(tallied, n)
                    nc.scalar.activation(phi[:, s, :], feat[:, s, :], ACT.Exp).then_inc(mapped, 1)
            for k in range(KC):
                split(0, 0, k)
            over_macros(act, macro, more=False)

        @block.vector
        def _(dve):
            nc.vector.memset(omega[:, :], 0.0).then_inc(set_up, 1)
            nc.vector.memset(half[:, :], 0.0).then_inc(moved, 1)
            nc.vector.memset(kv[:, :, :], 0.0)
            nc.vector.memset(tot[:, :], 0.0).then_inc(moved, 1)
            dve.wait_ge(moved, 2)
            nc.vector.memset(half[0:HF, 0:1], -0.5 / HF)
            nc.vector.memset(half[HF:P, 1:2], -0.5 / HF).then_inc(moved, 1)
            dve.wait_ge(loaded, 32)
            nc.vector.tensor_scalar(omega[:, :], omega[:, :], HF ** -0.5, None, ALU.mult).then_inc(set_up, 1)

            dve.wait_ge(w_high, 1)
            nc.vector.tensor_tensor(wks[:, 1, :, :], wk[:, :, :], wks[:, 0, :, :].bitcast(F32), ALU.subtract)
            nc.vector.tensor_tensor(wvs[:, 1, :, :], wv[:, :, :], wvs[:, 0, :, :].bitcast(F32), ALU.subtract).then_inc(w_low, 1)
            dve.sem_inc(tallied, 1)

            def split(m, q, k):
                dve.wait_ge(x_high, m * KC + k + 1)
                nc.vector.tensor_tensor(xTs[:, q, 1, k, :], xT[:, k, :], xTs[:, q, 0, k, :].bitcast(F32), ALU.subtract).then_inc(x_low, 1)

            def tally(n, s):
                dve.wait_ge(mapped, n + 1 + 1)
                dve.wait_ge(tallied, n + 1)
                nc.vector.scalar_tensor_tensor(tot[:, :], phi[:, s, :], C["valid"][:, bass.ds(n, 1)], tot[:, :],
                                               ALU.mult, ALU.add).then_inc(tallied, 1)

            def macro(m, q, u, more=True):
                for j in range(TM):
                    n = m * TM + j
                    s = (q + j) % 2
                    dve.wait_ge(normed, n + 1)
                    nc.vector.tensor_scalar(nrm[:, s, :], pq[:, 0:H], NORM_TOP, NORM_LOW, ALU.min, ALU.max).then_inc(bounded, 1)
                    dve.wait_ge(bounded, n + 1)
                    if later(n):
                        dve.wait_ge(mapped, n)
                    nc.vector.scalar_tensor_tensor(feat[:, s, :].rearrange("p (h f) -> p h f", f=HF),
                                                   pf[:, :].rearrange("p (h f) -> p h f", f=HF), CLAMP,
                                                   bc(nrm[:, s, :].unsqueeze(2), [P, H, HF]), ALU.min, ALU.add).then_inc(featured, 1)
                    if later(n):
                        tally(n - 1, 1 - s)
                    if more and j < KC:
                        split(m + 1, 1 - q, j)
                dve.wait_ge(added, m * TM + TM + 1)
                nc.vector.tensor_tensor(kv[:, :, :].rearrange("p k c -> p (k c)"), kv[:, :, :].rearrange("p k c -> p (k c)"),
                                        pkv[:, :], ALU.add).then_inc(drained, 1)
            for k in range(KC):
                split(0, 0, k)
            over_macros(dve, macro, more=False)
            tally(NT - 1, (NT - 1) % 2)
            dve.wait_ge(drained, NM)
            dve.wait_ge(totalled, 1)
            nc.vector.tensor_tensor(kv[:, :, :], kv[:, :, :], bc(C["pair"][:, :].unsqueeze(1), [P, KC, P]), ALU.mult)
            nc.vector.tensor_tensor(C["k1"][:, :, :], bc(pk1[:, 0:KC].unsqueeze(2), [P, KC, P]),
                                    bc(C["pair"][:, :].unsqueeze(1), [P, KC, P]), ALU.mult).then_inc(masked, 1)
            for c in range(KC):
                dve.wait_ge(multiplied, c + 1)
                nc.vector.tensor_copy(C["g"][:, c, :], pk[c % 2][:, :]).then_inc(cleared, 1)
            dve.wait_ge(cleared, KC)

        @block.tensor
        def _(pe):
            pe.sem_inc(added, 1)
            pe.wait_ge(wloaded, 48)
            pe.wait_ge(w_low, 1)
            pe.wait_ge(set_up, 2)
            pe.wait_ge(moved, 3)

            def add(m, q, j):
                n = m * TM + j
                s = (q + j) % 2
                pe.wait_ge(copied, n + 1 + 1)
                pe.wait_ge(mapped, n + 1 + 1)
                if j == 0:
                    if later(m):
                        pe.wait_ge(drained, m)
                for c in range(KC):
                    last = nc.tensor.matmul(pkv[:, c * P:(c + 1) * P], vm[:, s, c * P:(c + 1) * P], phi[:, s, c * P:(c + 1) * P],
                                            start=(j == 0 and c == 0), stop=(j == TM - 1), skip_group_check=True)
                last.then_inc(added, 1)

            def macro(m, q, u):
                pe.wait_ge(x_low, m * KC + KC)
                for c in range(NC):
                    n = m * NC + c
                    hf, kk = divmod(c, KC)
                    if c >= 2:
                        pe.wait_ge(kept, n - 1)
                    else:
                        if later(m):
                            pe.wait_ge(kept, m * NC)
                    for k in range(KC):
                        for i, (a, b) in enumerate(PARTS):
                            last = nc.tensor.matmul(pk[c % 2][:, 0:HW], wks[:, a, k, kk * P:(kk + 1) * P],
                                                    xTs[:, q, b, k, hf * HW:(hf + 1) * HW],
                                                    start=(k == 0 and i == 0), stop=(k == KC - 1 and i == len(PARTS) - 1))
                    last.then_inc(projected, 1)
                for j in range(TM):
                    n = m * TM + j
                    s = (q + j) % 2
                    t = slice(j * P, (j + 1) * P)
                    if later(n):
                        pe.wait_ge(copied, n)
                    for k in range(KC):
                        for i, (a, b) in enumerate(PARTS):
                            last = nc.tensor.matmul(pv[s][:, :], xTs[:, q, a, k, t], wvs[:, b, k, :],
                                                    start=(k == 0 and i == 0), stop=(k == KC - 1 and i == len(PARTS) - 1))
                    last.then_inc(valued, 1)
                    pe.wait_ge(kept, m * NC + NC)
                    if later(n):
                        pe.wait_ge(featured, n)
                    for c in range(KC):
                        nc.tensor.matmul(pf[:, c * P:(c + 1) * P], kT[:, c, t], omega[:, :], start=True, stop=True)
                    for c in range(KC):
                        last = nc.tensor.matmul(pq[:, 2 * c:2 * c + 2], k2[:, c, t], half[:, :], start=True, stop=True)
                    last.then_inc(normed, 1)
                    if j:
                        add(m, q, j - 1)
                add(m, q, TM - 1)
            over_macros(pe, macro)
            pe.wait_ge(tallied, NT + 1)
            for c in range(KC):
                last = nc.tensor.matmul(pk1[:, c:c + 1], tot[:, c * P:(c + 1) * P], C["ones"][:, 0:1], start=True, stop=True)
            last.then_inc(totalled, 1)
            pe.wait_ge(masked, 1)
            for c in range(KC):
                if c >= 2:
                    pe.wait_ge(cleared, c - 1)
                nc.tensor.matmul(pk[c % 2][:, :], kv[:, c, :], C["wo"][:, c, :], start=True, stop=True).then_inc(multiplied, 1)


def query_rows(nc, C, dram):
    with Stage(nc) as ctx:
        xT = fixed(ctx, nc, "qr_xT", [P, 2, KC, HW])
        xTs = fixed(ctx, nc, "qr_xTs", [P, 2, 2, KC, HW], F32R)
        wq = fixed(ctx, nc, "qr_wq", [P, KC, D])
        wqs = fixed(ctx, nc, "qr_wqs", [P, 2, KC, D], F32R)
        gs = fixed(ctx, nc, "qr_gs", [P, 2, KC, D], F32R)
        omega = fixed(ctx, nc, "qr_omega", [P, P])
        half = fixed(ctx, nc, "qr_half", [P, P])
        qT = fixed(ctx, nc, "qr_qT", [P, 2, HW])
        q2 = fixed(ctx, nc, "qr_q2", [P, 2, HW])
        nrm = fixed(ctx, nc, "qr_nrm", [P, 2, HW])
        phi = fixed(ctx, nc, "qr_phi", [P, 2, KC, HW])
        rec = fixed(ctx, nc, "qr_rec", [H, HW])
        recs = fixed(ctx, nc, "qr_recs", [H, 2, 2, HW], F32R)
        k1c = fixed(ctx, nc, "qr_k1c", [P, KC, H])
        pick = fixed(ctx, nc, "qr_pick", [H, KC, P])
        picks = fixed(ctx, nc, "qr_picks", [H, KC, P], F32R)
        phin = fixed(ctx, nc, "qr_phin", [P, 2, HW])
        phins = fixed(ctx, nc, "qr_phins", [P, 2, 2, KC, MW], F32R)
        xs = fixed(ctx, nc, "qr_x", [P, 2, D])
        ac = fixed(ctx, nc, "qr_ac", [P, 2, AW])
        rden = fixed(ctx, nc, "qr_rden", [P, 2, 2, H])
        x1 = fixed(ctx, nc, "qr_x1", [P, 2, D])
        st = fixed(ctx, nc, "qr_st", [P, NT, 6])
        pq = [psum(ctx, nc, f"qr_pq{i}") for i in range(2)]
        pf = psum(ctx, nc, "qr_pf")
        pn = psum(ctx, nc, "qr_pn")
        pd = psum(ctx, nc, "qr_pd")
        pb = psum(ctx, nc, "qr_pb")
        pm = [psum(ctx, nc, f"qr_pm{i}") for i in range(2)]
        loaded, wloaded, set_up = sems(ctx, nc, "qr", "loaded wloaded setup")
        x_loaded = sems(ctx, nc, "qr", "x0 x1")
        r_loaded = sems(ctx, nc, "qr", "r0 r1")
        stored = sems(ctx, nc, "qr", "s0 s1")
        NC = 2 * KC
        (picked, cleared, w_high, w_low, x_high, x_low, projected, kept, featured, bounded, argued, mapped, summed, inverted,
         r_high, r_low, carried, divided, n_high, n_low, mixed, dens, rdens, graphed, based, finished, measured, rooted,
         counted, passed) = sems(
            ctx, nc, "qr", "picked cleared whigh wlow xhigh xlow projected kept featured bounded argued mapped summed inverted "
                           "rhigh rlow carried divided nhigh nlow mixed dens rdens graphed based finished measured rooted "
                           "counted passed")
        block = ctx.enter_context(nc.Block())
        rows = dram["x"].rearrange("(n p) d -> n p d", p=P)
        acc = dram["acc"][0:NP, :].rearrange("(n p) w -> n p w", p=P)
        x1_rows = dram["x1"].rearrange("(n p) d -> n p d", p=P)

        SHARE, QUOTIENT, SPLIT = 1, KC + 2, KC + 3
        ROW = NC + SPLIT

        def there(m):
            return not isinstance(m, int) or 0 <= m < NM

        def back(m, q, c, lag):
            over = (lag - c + NC - 1) // NC
            mm = m - over
            return (m * NC + c - lag, mm, (q + over) % 2, c - lag + over * NC) if there(mm) else None

        def row_of(m, q, u, c):
            for over in (1, 2):
                j = c + over * NC - ROW
                if 0 <= j < TM and there(m - over):
                    mm, qq = m - over, (q + over) % 2
                    uu = u - 1 + (q if over == 1 else 0)
                    return mm * TM + j, (qq + j) % 2, uu * TM + (qq * TM + j) // 2, mm, qq, j
            return None

        def all_steps(eng, body):
            def macro(m, q, u):
                for c in range(NC):
                    body(m, q, u, c)
            macro(0, 0, 0)
            macro(1, 1, 0)
            with eng.Fori(1, NM // 2) as i:
                macro(i * 2, 0, i)
                macro(i * 2 + 1, 1, i)
            macro(NM - 1, 0, NM // 2)
            macro(NM, 1, NM // 2)
            for c in range(ROW + TM - 2 * NC):
                body(NM + 1, 0, NM // 2 + 1, c)

        @block.sync
        def _(sp):
            sp.dma_start(wq[:, :, :], dram["Wq"].rearrange("(k p) n -> p k n", p=P)).then_inc(wloaded, 16)
            sp.wait_ge(set_up, 1)
            load_feature_maps(nc, sp, omega, dram["omega_q"], loaded)

            def turned_rows(m, hf):
                sp.wait_ge(x_low, 2 * m + hf + 1)
                hold(sp, passed)
                sp.dma_start(xT[:, hf, :, :], dram["xnT"][m, :, :, hf * HW:(hf + 1) * HW]).then_inc(x_loaded[hf], 16)

            def step(m, q, u, c):
                if c in (0, KC) and there(m + 1):
                    turned_rows(m + 1, c // KC)
                if row_of(m, q, u, c):
                    n, s = row_of(m, q, u, c)[:2]
                    sp.wait_ge(finished, n + 1)
                    hold(sp, passed)
                    sp.dma_start(xs[:, s, :], rows[n]).then_inc(r_loaded[s], 16)
                    sp.dma_start(ac[:, s, :], acc[n]).then_inc(r_loaded[s], 16)
            turned_rows(0, 0)
            turned_rows(0, 1)
            all_steps(sp, step)

        @block.gpsimd
        def _(pool):
            pool.memset(pick[:, :, :], 1.0).then_inc(picked, 1)
            pool.wait_ge(picked, 1)
            pool.affine_select(out=pick[:, :, :], in_=pick[:, :, :], compare_op=ALU.is_gt, fill=0.0,
                               base=1, pattern=[[P, KC], [1, P]], channel_multiplier=-HF).then_inc(picked, 1)
            pool.wait_ge(picked, 2)
            pool.affine_select(out=pick[:, :, :], in_=pick[:, :, :], compare_op=ALU.is_gt, fill=0.0,
                               base=HF, pattern=[[-P, KC], [-1, P]], channel_multiplier=HF).then_inc(picked, 1)

            def macro(m, q, u):
                for j in range(TM):
                    n = m * TM + j
                    s = (q + j) % 2
                    pool.wait_ge(finished, n + 1 + 2)
                    pool.dma_start(x1_rows[n], x1[:, s, :]).then_inc(stored[s], 16)
            over_macros(pool, macro)
            pool.wait_ge(stored[0], 16 * ((NT + 1) // 2))
            pool.wait_ge(stored[1], 16 * (NT // 2))

        @block.scalar
        def _(act):
            act.sem_inc(kept, 2)
            act.sem_inc(mapped, 2)
            nc.scalar.activation(gs[:, 0, :, :], C["g"][:, :, :], ACT.Copy).then_inc(w_high, 1)
            act.wait_ge(wloaded, 16)
            nc.scalar.activation(wqs[:, 0, :, :], wq[:, :, :], ACT.Copy).then_inc(w_high, 1)

            def split(m, hf):
                act.wait_ge(x_loaded[hf], m * 16 + 16)
                act.wait_ge(projected, m * NC + (hf + 1) * KC)
                nc.scalar.activation(xTs[:, hf, 0, :, :], xT[:, hf, :, :], ACT.Copy).then_inc(x_high, 1)

            def step(m, q, u, c):
                n = m * NC + c
                hf, k = divmod(c, KC)
                if there(m):
                    act.wait_ge(projected, n + 1 + NC)
                    act.wait_ge(featured, n + 1)
                    nc.scalar.activation(qT[:, c % 2, :], pq[c % 2][:, 0:HW], ACT.Copy)
                    nc.scalar.activation(q2[:, c % 2, :], pq[c % 2][:, 0:HW], ACT.Square).then_inc(kept, 1)
                if k == 1 and back(m, q, c, KC + 1):
                    h = m * 2 + hf - 1
                    act.wait_ge(inverted, h + 1)
                    act.wait_ge(carried, h * KC + KC)
                    nc.scalar.activation(recs[:, 1 - hf, 0, :], rec[:, :], ACT.Copy).then_inc(r_high, 1)
                if back(m, q, c, SPLIT):
                    i, mm, qq, cc = back(m, q, c, SPLIT)
                    act.wait_ge(divided, i + 1 + 2 * KC)
                    act.wait_ge(mixed, mm * TM)
                    nc.scalar.activation(phins[:, qq, 0, cc % KC, cc // KC * HW:(cc // KC + 1) * HW], phin[:, cc % 2, :],
                                         ACT.Copy).then_inc(n_high, 1)
                if there(m) and c == KC - 2:
                    split(m, 1)
                if there(m + 1) and c == NC - 2:
                    split(m + 1, 0)
                if there(m):
                    act.wait_ge(argued, n + 1 + 2)
                    act.wait_ge(divided, n + 1)
                    nc.scalar.activation(phi[:, hf, k, :], nrm[:, c % 2, :], ACT.Exp).then_inc(mapped, 1)
            split(0, 0)
            all_steps(act, step)
            act.wait_ge(counted, 1)
            nc.scalar.activation(C["stats2"][:, :, 1], C["stats2"][:, :, 1], ACT.Sqrt).then_inc(rooted, 1)

        @block.vector
        def _(dve):
            nc.vector.memset(omega[:, :], 0.0).then_inc(set_up, 1)
            nc.vector.tensor_scalar(half[:, :], C["pair"][:, :], -0.5 / HF, None, ALU.mult).then_inc(set_up, 1)
            dve.sem_inc(argued, 2)
            dve.sem_inc(divided, 2 * KC)
            nc.vector.memset(k1c[:, :, :], 0.0).then_inc(cleared, 1)
            dve.sem_inc(finished, 2)
            dve.sem_inc(x_low, 2)
            dve.wait_ge(loaded, 32)
            nc.vector.tensor_scalar(omega[:, :], omega[:, :], HF ** -0.5, None, ALU.mult).then_inc(set_up, 1)
            dve.wait_ge(picked, 3)
            dve.wait_ge(cleared, 1)
            nc.vector.tensor_copy(picks[:, :, :], pick[:, :, :])
            for k in range(KC):
                nc.vector.tensor_copy(k1c[:, k, 2 * k:2 * k + 2], C["k1"][:, k, 0:P:HF])
            dve.wait_ge(w_high, 2)
            nc.vector.tensor_tensor(wqs[:, 1, :, :], wq[:, :, :], wqs[:, 0, :, :].bitcast(F32), ALU.subtract)
            nc.vector.tensor_tensor(gs[:, 1, :, :], C["g"][:, :, :], gs[:, 0, :, :].bitcast(F32), ALU.subtract).then_inc(w_low, 1)

            def split(m, hf):
                dve.wait_ge(x_high, 2 * m + hf + 1)
                nc.vector.tensor_tensor(xTs[:, hf, 1, :, :], xT[:, hf, :, :], xTs[:, hf, 0, :, :].bitcast(F32), ALU.subtract).then_inc(x_low, 1)

            def argue(n, c):
                dve.wait_ge(featured, n + 1 + 2)
                dve.wait_ge(mapped, n + 1)
                nc.vector.tensor_scalar(nrm[:, c % 2, :], pn[:, 0:HW], NORM_TOP, NORM_LOW, ALU.min, ALU.max).then_inc(bounded, 1)
                dve.wait_ge(bounded, n + 1)
                nc.vector.scalar_tensor_tensor(nrm[:, c % 2, :], pf[:, 0:HW], CLAMP, nrm[:, c % 2, :],
                                               ALU.min, ALU.add).then_inc(argued, 1)

            def row(n, s, v):
                dve.wait_ge(r_loaded[s], v * 32 + 32)
                nc.vector.tensor_scalar(rden[:, s, 0, :], ac[:, s, D:D + H], DEN_LOW, None, ALU.max).then_inc(dens, 1)
                dve.wait_ge(dens, n + 1)
                nc.vector.reciprocal(rden[:, s, 1, :], rden[:, s, 0, :]).then_inc(rdens, 1)
                dve.wait_ge(rdens, n + 1)
                part = ac[:, s, 0:D].rearrange("p (h f) -> p h f", f=HF)
                nc.vector.tensor_tensor(part, part, bc(rden[:, s, 1, :].unsqueeze(2), [P, H, HF]), ALU.mult).then_inc(graphed, 1)
                dve.wait_ge(graphed, n + 1)
                nc.vector.tensor_tensor(xs[:, s, :], xs[:, s, :], ac[:, s, 0:D], ALU.add).then_inc(based, 1)
                dve.wait_ge(based, n + 1)
                dve.wait_ge(mixed, n + 1 + TM)
                if later(v):
                    dve.wait_ge(stored[s], v * 16)
                nc.vector.tensor_tensor(x1[:, s, :], pm[s][:, :], xs[:, s, :], ALU.add).then_inc(finished, 1)
                dve.wait_ge(finished, n + 1 + 2)
                nc.vector.bn_stats(st[:, n, :], x1[:, s, :]).then_inc(measured, 1)

            def step(m, q, u, c):
                n = m * NC + c
                hf, k = divmod(c, KC)
                if there(m):
                    argue(n, c)
                if back(m, q, c, QUOTIENT):
                    i, mm, qq, cc = back(m, q, c, QUOTIENT)
                    dve.wait_ge(carried, i + 1 + 2 * KC)
                    nc.vector.tensor_tensor(phin[:, cc % 2, :], phi[:, cc // KC, cc % KC, :], pb[:, 0:HW], ALU.mult).then_inc(divided, 1)
                if back(m, q, c, SPLIT):
                    i, mm, qq, cc = back(m, q, c, SPLIT)
                    part = slice(cc // KC * HW, (cc // KC + 1) * HW)
                    dve.wait_ge(n_high, i + 1)
                    nc.vector.tensor_tensor(phins[:, qq, 1, cc % KC, part], phin[:, cc % 2, :],
                                            phins[:, qq, 0, cc % KC, part].bitcast(F32), ALU.subtract).then_inc(n_low, 1)
                if k == 1 and back(m, q, c, KC + 1):
                    h = m * 2 + hf - 1
                    dve.wait_ge(r_high, h + 1)
                    nc.vector.tensor_tensor(recs[:, 1 - hf, 1, :], rec[:, :], recs[:, 1 - hf, 0, :].bitcast(F32), ALU.subtract).then_inc(r_low, 1)
                if there(m) and c == KC - 2:
                    split(m, 1)
                if there(m + 1) and c == NC - 2:
                    split(m + 1, 0)
                if row_of(m, q, u, c):
                    row(*row_of(m, q, u, c)[:3])
                if k == 0 and back(m, q, c, KC):
                    h = m * 2 + hf - 1
                    dve.wait_ge(summed, h + 1)
                    if later(h):
                        dve.wait_ge(r_low, h)
                    nc.vector.reciprocal(rec[:, :], pd[0:H, 0:HW]).then_inc(inverted, 1)
            split(0, 0)
            all_steps(dve, step)
            dve.wait_ge(measured, NT)
            for n in range(NT):
                last = nc.vector.bn_aggr(C["stats2"][:, n, :], st[:, n, :])
            last.then_inc(dens, 1)
            dve.wait_ge(dens, NT + 1)
            nc.vector.tensor_scalar(C["stats2"][:, :, 1], C["stats2"][:, :, 1], LN_EPS, None, ALU.add).then_inc(counted, 1)
            dve.wait_ge(rooted, 1)
            nc.vector.reciprocal(C["stats2"][:, :, 1], C["stats2"][:, :, 1]).then_inc(counted, 1)
            dve.wait_ge(counted, 2)

        @block.tensor
        def _(pe):
            pe.sem_inc(projected, NC)
            pe.sem_inc(featured, 2)
            pe.sem_inc(mixed, TM)
            pe.sem_inc(carried, 2 * KC)
            pe.wait_ge(w_low, 1)
            pe.wait_ge(set_up, 3)

            def project(n, m, c):
                hf, kk = divmod(c, KC)
                pe.wait_ge(kept, n + 1)
                pe.wait_ge(x_low, 2 * m + hf + 1 + 2)
                for k in range(KC):
                    for i, (a, b) in enumerate(PARTS):
                        last = nc.tensor.matmul(pq[c % 2][:, 0:HW], wqs[:, a, k, kk * P:(kk + 1) * P], xTs[:, hf, b, k, :],
                                                start=(k == 0 and i == 0), stop=(k == KC - 1 and i == len(PARTS) - 1))
                last.then_inc(projected, 1)

            def feature(n, c):
                pe.wait_ge(kept, n + 1 + 2)
                pe.wait_ge(argued, n + 2)
                nc.tensor.matmul(pf[:, 0:HW], omega[:, :], qT[:, c % 2, :], start=True, stop=True)
                nc.tensor.matmul(pn[:, 0:HW], half[:, :], q2[:, c % 2, :], start=True, stop=True).then_inc(featured, 1)

            def step(m, q, u, c):
                n = m * NC + c
                if c + 1 < NC and there(m):
                    project(n + 1, m, c + 1)
                elif c + 1 == NC and there(m + 1):
                    project(n + 1, m + 1, 0)
                if there(m):
                    feature(n, c)
                if back(m, q, c, QUOTIENT):
                    i, mm, qq, cc = back(m, q, c, QUOTIENT)
                    pe.wait_ge(r_low, 2 * mm + cc // KC + 1)
                    pe.wait_ge(divided, i + 2 * KC)
                    for a in range(2):
                        last = nc.tensor.matmul(pb[:, 0:HW], picks[:, cc % KC, :], recs[:, cc // KC, a, :], start=(a == 0), stop=(a == 1))
                    last.then_inc(carried, 1)
                if row_of(m, q, u, c):
                    n, s, v, mm, qq, j = row_of(m, q, u, c)
                    if j == 0:
                        pe.wait_ge(n_low, mm * NC + NC)
                    pe.wait_ge(finished, n + 1)
                    for k in range(KC):
                        for i, (a, b) in enumerate(PARTS):
                            last = nc.tensor.matmul(pm[s][:, :], phins[:, qq, a, k, j * P:(j + 1) * P], gs[:, b, k, :],
                                                    start=(k == 0 and i == 0), stop=(k == KC - 1 and i == len(PARTS) - 1))
                    last.then_inc(mixed, 1)
                if back(m, q, c, SHARE):
                    i, mm, qq, cc = back(m, q, c, SHARE)
                    pe.wait_ge(mapped, i + 1 + 2)
                    if cc == 0:
                        if later(mm):
                            pe.wait_ge(inverted, 2 * mm)
                    elif cc == KC:
                        pe.wait_ge(inverted, 2 * mm + 1)
                    last = nc.tensor.matmul(pd[0:H, 0:HW], k1c[:, cc % KC, :], phi[:, cc // KC, cc % KC, :],
                                            start=(cc % KC == 0), stop=(cc % KC == KC - 1))
                    if cc % KC == KC - 1:
                        last.then_inc(summed, 1)
            project(0, 0, 0)
            all_steps(pe, step)


def route(nc, C, dram):
    with Stage(nc) as ctx:
        xs = fixed(ctx, nc, "rt_x", [P, NT, D])
        xT = fixed(ctx, nc, "rt_xT", [P, 2, KC, P])
        wr = fixed(ctx, nc, "rt_wr", [P, KC, EX])
        lg = fixed(ctx, nc, "rt_lg", [P, 2, NT, EX])
        other = fixed(ctx, nc, "rt_other", [P, NT, EX])
        rank = fixed(ctx, nc, "rt_rank", [P, NT, EX])
        top = fixed(ctx, nc, "rt_top", [P, 2, NT])
        num = fixed(ctx, nc, "rt_num", [P, 2, NT])
        hit = fixed(ctx, nc, "rt_hit", [P, 2, NT, EX])
        both = fixed(ctx, nc, "rt_both", [P, NT, EX])
        tot = fixed(ctx, nc, "rt_tot", [P, NT, EX])
        cum = fixed(ctx, nc, "rt_cum", [P, NT, EX])
        nul = fixed(ctx, nc, "rt_nul", [P, NT])
        slot = fixed(ctx, nc, "rt_slot", [P, 2, NT])
        keep = fixed(ctx, nc, "rt_keep", [P, 2, NT])
        pos = fixed(ctx, nc, "rt_pos", [P, 2, NT])
        goal = fixed(ctx, nc, "rt_goal", [P, 2, NT])
        gap = fixed(ctx, nc, "rt_gap", [P, 2, NT])
        xn = fixed(ctx, nc, "rt_xn", [P, 2, D])
        at = fixed(ctx, nc, "rt_at", [P, 2, NT], I32)
        pT = [psum(ctx, nc, f"rt_pT{i}") for i in range(2)]
        pl = psum(ctx, nc, "rt_pl")
        pp = psum(ctx, nc, "rt_pp")
        po = psum(ctx, nc, "rt_po")
        wloaded, early = sems(ctx, nc, "rt", "wloaded early")
        loaded = sems(ctx, nc, "rt", " ".join(f"ld{i}" for i in range(2)))
        (normed, turned, kept, scored, v, s, counted, indexed, settled, sent,
         passed) = sems(ctx, nc, "rt", "normed turned kept scored v s counted indexed settled sent "
                                         "passed")
        block = ctx.enter_context(nc.Block())
        macros = dram["x1"].rearrange("(m j p) d -> m p j d", j=TM, p=P)
        TOP = 11
        LAST = TOP + 14

        @block.sync
        def _(sp):
            def macro(m, q, u):
                if later(m) and later(m - 1):
                    sp.wait_ge(normed, (m - 1) * TM)
                    hold(sp, passed)
                ahead = 0 if later(m) else 1
                sp.dma_start(xs[:, bass.ds(m * TM + ahead, TM - ahead), :], macros[m][:, ahead:TM, :]).then_inc(loaded[q], 16)
            sp.dma_start(xs[:, 0, :], macros[0][:, 0, :]).then_inc(early, 16)
            sp.dma_start(wr[:, :, :], dram["router_w"].rearrange("(k p) e -> p k e", p=P)).then_inc(wloaded, 16)
            over_macros(sp, macro)

        @block.scalar
        def _(act):
            act.sem_inc(kept, 2)

            def macro(m, q, u):
                for j in range(TM):
                    n = m * TM + j
                    b = (q + j) % 2
                    act.wait_ge(turned, n + 1 + 2)
                    act.wait_ge(scored, n + 1)
                    nc.scalar.activation(xT[:, b, :, :].rearrange("p k t -> p (k t)"), pT[b][:, :], ACT.Copy).then_inc(kept, 1)
            over_macros(act, macro)
            act.wait_ge(v, TOP + 2)
            nc.scalar.activation(gap[:, 0, :], gap[:, 1, :], ACT.Exp).then_inc(s, 1)

        @block.vector
        def _(dve):
            nc.vector.memset(nul[:, :], 0.0)

            def macro(m, q, u):
                for j in range(TM):
                    n = m * TM + j
                    if j == 0 and not later(m):
                        dve.wait_ge(early, 16)
                    elif j <= 1:
                        dve.wait_ge(loaded[q], u * 16 + 16)
                    dve.wait_ge(turned, n + 1)
                    nc.vector.tensor_scalar(xn[:, (q + j) % 2, :], xs[:, n, :], C["stats2"][:, n, 0:1], C["stats2"][:, n, 1:2],
                                            ALU.subtract, ALU.mult).then_inc(normed, 1)
                    nc.vector.tensor_scalar(xs[:, n, :], xs[:, n, :], C["stats2"][:, n, 0:1], C["stats2"][:, n, 1:2],
                                            ALU.subtract, ALU.mult).then_inc(settled, 1)
            over_macros(dve, macro)
            dve.wait_ge(scored, NT + 2)
            done = [0]

            def link(ins):
                done[0] += 1
                ins.then_inc(v, 1)
                dve.wait_ge(v, done[0])

            experts_row = bc(C["cols"][:, 0:EX].unsqueeze(1), [P, NT, EX])
            link(nc.vector.tensor_copy(lg[:, 0, :, :].rearrange("p n e -> p (n e)"), pl[:, 0:NT * EX]))
            for kk in range(2):
                link(nc.vector.tensor_reduce(top[:, kk, :], lg[:, kk, :, :], AX.X, ALU.max))
                link(nc.vector.tensor_tensor(other[:, :, :], lg[:, kk, :, :], bc(top[:, kk, :].unsqueeze(2), [P, NT, EX]), ALU.not_equal))
                link(nc.vector.scalar_tensor_tensor(rank[:, :, :], other[:, :, :], float(EX), experts_row, ALU.mult, ALU.add))
                link(nc.vector.tensor_reduce(num[:, kk, :], rank[:, :, :], AX.X, ALU.min))
                link(nc.vector.tensor_tensor(hit[:, kk, :, :], bc(num[:, kk, :].unsqueeze(2), [P, NT, EX]), experts_row, ALU.is_equal))
                if kk == 0:
                    link(nc.vector.scalar_tensor_tensor(lg[:, 1, :, :], hit[:, 0, :, :], LOW, lg[:, 0, :, :], ALU.mult, ALU.add))
            assert done[0] == TOP + 1

            link(nc.vector.tensor_tensor(gap[:, 1, :], top[:, 1, :], top[:, 0, :], ALU.subtract))
            link(nc.vector.tensor_tensor(both[:, :, :], hit[:, 0, :, :], hit[:, 1, :, :], ALU.add))
            dve.wait_ge(s, 1)
            link(nc.vector.tensor_scalar(gap[:, 1, :], gap[:, 0, :], 1.0, None, ALU.add))
            link(nc.vector.reciprocal(C["weight"][:, 0, :], gap[:, 1, :]))
            nc.vector.tensor_tensor(C["weight"][:, 1, :], C["weight"][:, 0, :], gap[:, 0, :], ALU.mult)
            dve.wait_ge(counted, 1)
            link(nc.vector.tensor_copy(tot[:, :, :].rearrange("p n e -> p (n e)"), po[:, 0:NT * EX]))
            for x in range(EX):
                last = nc.vector.tensor_tensor_scan(cum[:, :, x], tot[:, :, x], nul[:, :], 0.0, ALU.add, ALU.add)
            link(last)
            link(nc.vector.tensor_tensor(cum[:, :, :], cum[:, :, :], tot[:, :, :], ALU.subtract))
            link(nc.vector.tensor_tensor(cum[:, :, :].rearrange("p n e -> p (n e)"), cum[:, :, :].rearrange("p n e -> p (n e)"),
                                         pp[:, 0:NT * EX], ALU.add))
            link(nc.vector.tensor_tensor(hit[:, :, :, :], hit[:, :, :, :], bc(cum[:, :, :].unsqueeze(1), [P, 2, NT, EX]),
                                         ALU.mult))
            nc.vector.tensor_scalar(pos[:, :, :], num[:, :, :], float(CAP), None, ALU.mult)
            link(nc.vector.tensor_reduce(slot[:, :, :], hit[:, :, :, :], AX.X, ALU.add))
            nc.vector.tensor_scalar(keep[:, :, :], slot[:, :, :], float(CAP), None, ALU.is_lt)
            nc.vector.tensor_tensor(goal[:, :, :], slot[:, :, :], pos[:, :, :], ALU.add)
            link(nc.vector.tensor_scalar(slot[:, :, :], slot[:, :, :], float(CAP - 1), None, ALU.min))
            nc.vector.tensor_tensor(C["weight"][:, :, :], C["weight"][:, :, :], keep[:, :, :], ALU.mult)
            nc.vector.tensor_tensor(slot[:, :, :], slot[:, :, :], pos[:, :, :], ALU.add)
            link(nc.vector.tensor_tensor(keep[:, :, :], keep[:, :, :], bc(C["valid"][:, :].unsqueeze(1), [P, 2, NT]), ALU.mult))
            nc.vector.tensor_copy(C["from"][:, :, :], slot[:, :, :].rearrange("p k n -> p n k"))
            link(nc.vector.tensor_scalar(keep[:, :, :], keep[:, :, :], -BIG, BIG, ALU.mult, ALU.add))
            assert done[0] == LAST
            link(nc.vector.tensor_tensor(goal[:, :, :], goal[:, :, :], keep[:, :, :], ALU.add))
            nc.vector.tensor_copy(at[:, :, :], goal[:, :, :]).then_inc(indexed, 1)
            dve.wait_ge(indexed, 1)

        @block.gpsimd
        def _(pool):
            pool.wait_ge(indexed, 1)
            pool.wait_ge(settled, NT)
            for n in range(NT):
                for kk in range(2):
                    pool.indirect_dma_start(out=dram["xe"], out_offset=bass.IndirectOffsetOnAxis(ap=at[:, kk, n:n + 1], axis=0),
                                            in_=xs[:, n, :], in_offset=None, bounds_check=EX * CAP - 1,
                                            oob_is_err=False).then_inc(sent, 16)
            pool.wait_ge(sent, 2 * NT * 16)

        @block.tensor
        def _(pe):
            pe.wait_ge(wloaded, 16)
            pe.sem_inc(turned, 2)
            pe.sem_inc(scored, 2)

            def turn(m, q, j):
                n = m * TM + j
                b = (q + j) % 2
                pe.wait_ge(normed, n + 1)
                pe.wait_ge(kept, n + 1)
                for k in range(KC):
                    last = nc.tensor.transpose(pT[b][:, k * P:(k + 1) * P], xn[:, b, k * P:(k + 1) * P], C["ident"][:, :])
                last.then_inc(turned, 1)

            def macro(m, q, u, more=True):
                for j in range(TM):
                    n = m * TM + j
                    b = (q + j) % 2
                    if j + 1 < TM:
                        turn(m, q, j + 1)
                    elif more:
                        turn(m + 1, 1 - q, 0)
                    pe.wait_ge(kept, n + 1 + 2)
                    for k in range(KC):
                        last = nc.tensor.matmul(pl[:, bass.ds(n * EX, EX)], xT[:, b, k, :], wr[:, k, :], start=(k == 0), stop=(k == KC - 1))
                    last.then_inc(scored, 1)
            turn(0, 0, 0)
            over_macros(pe, macro, more=False)
            pe.wait_ge(v, TOP + 3)
            flat = both[:, :, :].rearrange("p n e -> p (n e)")
            nc.tensor.matmul(pp[:, 0:NT * EX], C["before"][:, :], flat, start=True, stop=True)
            nc.tensor.matmul(po[:, 0:NT * EX], C["ones"][:, :], flat, start=True, stop=True).then_inc(counted, 1)


def experts(nc, C, dram):
    with Stage(nc) as ctx:
        w1 = fixed(ctx, nc, "ex_w1", [P, 2, KC * FF])
        w2 = fixed(ctx, nc, "ex_w2", [P, 2, FC * D])
        w1s = fixed(ctx, nc, "ex_w1s", [P, 2, 2, KC * FF], F32R)
        w2s = fixed(ctx, nc, "ex_w2s", [P, 2, 2, FC * D], F32R)
        xTs = fixed(ctx, nc, "ex_xTs", [P, 2, 2, KC, SW], F32R)
        hTs = fixed(ctx, nc, "ex_hTs", [P, 2, 2, FC, SW], F32R)
        b1 = fixed(ctx, nc, "ex_b1", [P, 2, FC])
        b2 = fixed(ctx, nc, "ex_b2", [P, 2, D])
        xs = fixed(ctx, nc, "ex_x", [P, 2, ST, D])
        hT = fixed(ctx, nc, "ex_hT", [P, FC, SW])
        ys = fixed(ctx, nc, "ex_y", [P, 2, ST, D])
        pT = [psum(ctx, nc, f"ex_pT{i}") for i in range(KC)]
        ph = [psum(ctx, nc, f"ex_ph{i}") for i in range(FC)]
        py = [psum(ctx, nc, f"ex_py{i}") for i in range(2)]
        w_loaded = sems(ctx, nc, "ex", "w0 w1")
        x_loaded = sems(ctx, nc, "ex", "x0 x1")
        y_stored = sems(ctx, nc, "ex", "y0 y1")
        turned, x_high, x_low, expanded, bent, h_high, h_low, reduced, biased, w_high, w_low, used, passed = sems(
            ctx, nc, "ex", "turned xhigh xlow expanded bent hhigh hlow reduced biased whigh wlow used passed")
        block = ctx.enter_context(nc.Block())
        CH = CAP // SW
        xe = dram["xe"].rearrange("(c t p) d -> c p t d", t=ST, p=P)
        ye = dram["ye"].rearrange("(c t p) d -> c p t d", t=ST, p=P)

        def chunks(eng, body, open_expert=None, close_expert=None, split=None):
            def pair(i, last):
                for w in range(2):
                    if open_expert:
                        open_expert(i * 2 + w, w, i)
                    more = not (last and w)
                    for c in range(CH):
                        body((i * 2 + w) * CH + c, c % 2, w, i * CH + (w * CH + c) // 2, more or c < CH - 1)
                        if split and more and c == CH - 2:
                            split(i * 2 + w + 1, 1 - w, i + w)
                    if close_expert:
                        close_expert(i * 2 + w)
            pair(0, False)
            with eng.Fori(1, EX // 2 - 1) as i:
                pair(i, False)
            pair(EX // 2 - 1, True)

        @block.sync
        def _(sp):
            def weights(e, w, i):
                sp.wait_ge(used, e + 1)
                hold(sp, passed)
                sp.dma_start(w1[:, w, :].rearrange("p (k f) -> p k f", k=KC), dram["w1"][e].rearrange("(k p) f -> p k f", p=P)).then_inc(w_loaded[w], 16)
                sp.dma_start(w2[:, w, :].rearrange("p (k d) -> p k d", k=FC), dram["w2"][e].rearrange("(k p) d -> p k d", p=P)).then_inc(w_loaded[w], 16)
                sp.dma_start(b1[:, w, :], dram["b1"][e]).then_inc(w_loaded[w], 16)
                sp.dma_start(b2[:, w, :], dram["b2"][e].partition_broadcast(P)).then_inc(w_loaded[w], 16)

            def chunk(n, q, w, u, more):
                sp.wait_ge(turned, n * KC + KC)
                hold(sp, passed)
                sp.dma_start(xs[:, q, :, :], xe[n]).then_inc(x_loaded[q], 16)
            weights(0, 0, 0)
            chunks(sp, chunk, split=weights)

        @block.gpsimd
        def _(pool):
            def chunk(n, q, w, u, more):
                pool.wait_ge(biased, n * ST + ST + 2)
                pool.dma_start(ye[n], ys[:, q, :, :]).then_inc(y_stored[q], 16)
            chunks(pool, chunk)
            for q in range(2):
                pool.wait_ge(y_stored[q], EX * CH // 2 * 16)

        @block.scalar
        def _(act):
            def split(e, w, i):
                act.wait_ge(w_loaded[w], i * 64 + 64)
                act.wait_ge(used, e + 1)
                nc.scalar.activation(w1s[:, w, 0, :], w1[:, w, :], ACT.Copy)
                nc.scalar.activation(w2s[:, w, 0, :], w2[:, w, :], ACT.Copy).then_inc(w_high, 1)

            def part(n, q, k):
                act.wait_ge(turned, n * KC + k + 1 + 2 * KC)
                act.wait_ge(expanded, n * FC + FC)
                nc.scalar.activation(xTs[:, q, 0, k, :], pT[k][:, :], ACT.Copy).then_inc(x_high, 1)

            def bend(n, q, w, f):
                act.wait_ge(expanded, n * FC + f + 1 + 2 * FC)
                act.wait_ge(h_low, n * FC + f + 1)
                nc.scalar.activation(hT[:, f, :], ph[f][:, :], ACT.Gelu_apprx_tanh, bias=b1[:, w, f:f + 1]).then_inc(bent, 1)
                act.wait_ge(bent, n * FC + f + 1)
                act.wait_ge(reduced, n * ST + ST)
                nc.scalar.activation(hTs[:, q, 0, f, :], hT[:, f, :], ACT.Copy).then_inc(h_high, 1)

            def chunk(n, q, w, u, more):
                for f in range(FC):
                    bend(n, q, w, f)
                    if more:
                        for k in range(f * KC // FC, (f + 1) * KC // FC):
                            part(n + 1, 1 - q, k)
            split(0, 0, 0)
            for k in range(KC):
                part(0, 0, k)
            chunks(act, chunk, split=split)

        @block.vector
        def _(dve):
            dve.sem_inc(x_low, KC)
            dve.sem_inc(h_low, FC)
            dve.sem_inc(biased, 2)

            def split(e, w, i):
                dve.wait_ge(w_high, e + 1)
                nc.vector.tensor_tensor(w1s[:, w, 1, :], w1[:, w, :], w1s[:, w, 0, :].bitcast(F32), ALU.subtract)
                nc.vector.tensor_tensor(w2s[:, w, 1, :], w2[:, w, :], w2s[:, w, 0, :].bitcast(F32), ALU.subtract).then_inc(w_low, 1)

            def part(n, q, k):
                dve.wait_ge(x_high, n * KC + k + 1)
                nc.vector.tensor_tensor(xTs[:, q, 1, k, :], pT[k][:, :], xTs[:, q, 0, k, :].bitcast(F32), ALU.subtract).then_inc(x_low, 1)

            def chunk(n, q, w, u, more):
                for f in range(FC):
                    dve.wait_ge(h_high, n * FC + f + 1)
                    nc.vector.tensor_tensor(hTs[:, q, 1, f, :], hT[:, f, :], hTs[:, q, 0, f, :].bitcast(F32), ALU.subtract).then_inc(h_low, 1)
                    if more:
                        for k in range(f * KC // FC, (f + 1) * KC // FC):
                            part(n + 1, 1 - q, k)
                if later(u):
                    dve.wait_ge(y_stored[q], u * 16)
                for t in range(ST):
                    m = n * ST + t
                    dve.wait_ge(reduced, m + 1 + 2 * ST)
                    nc.vector.tensor_tensor(ys[:, q, t, :], py[t % 2][:, :], b2[:, w, :], ALU.add).then_inc(biased, 1)
            split(0, 0, 0)
            for k in range(KC):
                part(0, 0, k)
            chunks(dve, chunk, split=split)

        @block.tensor
        def _(pe):
            pe.sem_inc(turned, 2 * KC)
            pe.sem_inc(expanded, 2 * FC)
            pe.sem_inc(reduced, 2 * ST)
            pe.sem_inc(used, 2)

            def turn(n, q, u, k):
                if k == 0:
                    pe.wait_ge(x_loaded[q], u * 16 + 16)
                pe.wait_ge(x_low, n * KC + k + 1)
                for t in range(ST):
                    last = nc.tensor.transpose(pT[k][:, t * P:(t + 1) * P], xs[:, q, t, k * P:(k + 1) * P], C["ident"][:, :])
                last.then_inc(turned, 1)

            def open_expert(e, w, i):
                pe.wait_ge(w_low, e + 1)

            def chunk(n, q, w, u, more):
                pe.wait_ge(x_low, (n + 1) * KC + KC)
                for f in range(FC):
                    if later(n):
                        pe.wait_ge(bent, (n - 1) * FC + f + 1)
                    for k in range(KC):
                        for i, (a, b) in enumerate(PARTS):
                            last = nc.tensor.matmul(ph[f][:, :], w1s[:, w, a, k * FF + f * P:k * FF + (f + 1) * P], xTs[:, q, b, k, :],
                                                    start=(k == 0 and i == 0), stop=(k == KC - 1 and i == len(PARTS) - 1))
                    last.then_inc(expanded, 1)
                    if more:
                        for k in range(f * KC // FC, (f + 1) * KC // FC):
                            turn(n + 1, 1 - q, u + q, k)
                for t0 in range(0, ST, 2):
                    for f in range(FC):
                        if t0 == 0:
                            pe.wait_ge(h_low, n * FC + f + 1 + FC)
                        for t in (t0, t0 + 1):
                            if f == 0:
                                pe.wait_ge(biased, n * ST + t + 1)
                            for i, (a, b) in enumerate(PARTS):
                                last = nc.tensor.matmul(py[t % 2][:, :], hTs[:, q, a, f, t * P:(t + 1) * P],
                                                        w2s[:, w, b, f * D:(f + 1) * D],
                                                        start=(f == 0 and i == 0), stop=(f == FC - 1 and i == len(PARTS) - 1))
                            if f == FC - 1:
                                last.then_inc(reduced, 1)

            def close_expert(e):
                pe.wait_ge(biased, ((e + 1) * CH) * ST + 2)
                hold(pe, used)
            for k in range(KC):
                turn(0, 0, 0, k)
            chunks(pe, chunk, open_expert, close_expert)


def combine(nc, C, dram):
    with Stage(nc) as ctx:
        xs = fixed(ctx, nc, "co_x", [P, TM, D])
        ya = fixed(ctx, nc, "co_ya", [P, 2, TM, D])
        at = fixed(ctx, nc, "co_at", [P, TM, 2], I32)
        os = fixed(ctx, nc, "co_o", [P, TM, D])
        loaded = sems(ctx, nc, "co", " ".join(f"ld{j}" for j in range(TM)))
        fetched = sems(ctx, nc, "co", " ".join(f"fe{j}" for j in range(TM)))
        stored = sems(ctx, nc, "co", " ".join(f"st{j}" for j in range(TM)))
        indexed, halved, summed, passed, passed_p = sems(ctx, nc, "co", "indexed halved summed passed passedp")
        block = ctx.enter_context(nc.Block())
        rows = dram["x1"].rearrange("(n p) d -> n p d", p=P)
        out = dram["out"].rearrange("(n p) d -> n p d", p=P)

        @block.sync
        def _(sp):
            def load(n, j):
                sp.dma_start(xs[:, j, :], rows[n]).then_inc(loaded[j], 16)

            def store(n, j):
                sp.wait_ge(summed, n + 1)
                hold(sp, passed)
                sp.dma_start(out[n], os[:, j, :]).then_inc(stored[j], 16)
            for j in range(TM):
                load(j, j)
            with sp.Fori(0, NM - 1) as m:
                for j in range(TM):
                    store(m * TM + j, j)
                    load(m * TM + j + TM, j)
            for j in range(TM):
                store((NM - 1) * TM + j, j)
            for j in range(TM):
                sp.wait_ge(stored[j], 16 * NM)

        @block.gpsimd
        def _(pool):
            def macro(m):
                pool.wait_ge(indexed, m + 1)
                for j in range(TM):
                    if later(m):
                        pool.wait_ge(summed, m * TM)
                    hold(pool, passed_p)
                    for kk in range(2):
                        pool.indirect_dma_start(out=ya[:, kk, j, :], out_offset=None, in_=dram["ye"],
                                                in_offset=bass.IndirectOffsetOnAxis(ap=at[:, j, kk:kk + 1], axis=0)).then_inc(fetched[j], 16)
            macro(0)
            with pool.Fori(1, NM) as m:
                macro(m)

        @block.vector
        def _(dve):
            def macro(m):
                for j in range(TM):
                    if later(m):
                        dve.wait_ge(fetched[j], m * 32)
                nc.vector.tensor_copy(at[:, :, :], C["from"][:, bass.ds(m * TM, TM), :]).then_inc(indexed, 1)
                for j in range(TM):
                    n = m * TM + j
                    dve.wait_ge(loaded[j], m * 16 + 16)
                    dve.wait_ge(fetched[j], m * 32 + 32)
                    nc.vector.scalar_tensor_tensor(xs[:, j, :], ya[:, 0, j, :], C["weight"][:, 0, bass.ds(n, 1)], xs[:, j, :],
                                                   ALU.mult, ALU.add).then_inc(halved, 1)
                    dve.wait_ge(halved, n + 1)
                    if later(m):
                        dve.wait_ge(stored[j], m * 16)
                    nc.vector.scalar_tensor_tensor(os[:, j, :], ya[:, 1, j, :], C["weight"][:, 1, bass.ds(n, 1)], xs[:, j, :],
                                                   ALU.mult, ALU.add).then_inc(summed, 1)
            macro(0)
            with dve.Fori(1, NM) as m:
                macro(m)


_INS = {"x": (NP, D), "src": (EP,), "src_em": (ET // BT, P, BT), "dst": (EP,), "dst_before": (EP,),
        "W_src": (D, D), "b_src": (D,), "W_dst": (D, D), "b_dst": (D,), "W_val": (D, D), "b_val": (D,),
        "attn_l": (D,), "attn_r": (D,),
        "Wq": (D, D), "Wk": (D, D), "Wv": (D, D), "Wo": (D, D), "omega_q": (HF, HF), "omega_k": (HF, HF),
        "router_w": (D, EX), "w1": (EX, D, FF), "b1": (EX, P, FC), "w2": (EX, FF, D), "b2": (EX, D)}


def build(nc, dram):
    with ExitStack() as ctx:
        C = {
            "ident": fixed(ctx, nc, "c_ident", [P, P]),
            "before": fixed(ctx, nc, "c_before", [P, P]),
            "ones": fixed(ctx, nc, "c_ones", [P, P]),
            "cols": fixed(ctx, nc, "c_cols", [P, P]),
            "pair": fixed(ctx, nc, "c_pair", [P, P]),
            "after": fixed(ctx, nc, "c_after", [P, P]),
            "valid": fixed(ctx, nc, "c_valid", [P, NT]),
            "stats2": fixed(ctx, nc, "c_stats2", [P, NT, 2]),
        }
        with ExitStack() as edges:
            C["rank"] = fixed(edges, nc, "c_rank", [P, ET])
            C["target"] = fixed(edges, nc, "c_target", [P, ET])
            C["first"] = fixed(edges, nc, "c_first", [P, ET])
            C["own"] = fixed(edges, nc, "c_own", [GH, 2])
            C["orderly"] = fixed(edges, nc, "c_orderly", [P, 2])
            C["general"] = fixed(edges, nc, "c_general", [1, 1], I32)
            with ExitStack() as nodes:
                C["wval"] = fixed(nodes, nc, "c_wval", [P, KC, D + 2 * H])
                C["vbias"] = fixed(nodes, nc, "c_vbias", [P, D + 2 * H])
                C["begin"] = fixed(nodes, nc, "c_begin", [P, NG])
                prep_weights(nc, C, dram)
                prep_edges(nc, C, dram)
                project_nodes(nc, C, dram)
            C["er"] = fixed(edges, nc, "c_er", [P, ET * H])
            edge_attention(nc, C, dram)
            merge_rows(nc, C, dram, carried=True)
            merge_rows(nc, C, dram, carried=False)
        with ExitStack() as inner:
            C["g"] = fixed(inner, nc, "c_g", [P, KC, D])
            C["k1"] = fixed(inner, nc, "c_k1", [P, KC, P])
            with ExitStack() as keys:
                C["wo"] = fixed(keys, nc, "c_wo", [P, KC, D])
                key_sums(nc, C, dram)
            query_rows(nc, C, dram)
        C["weight"] = fixed(ctx, nc, "c_weight", [P, 2, NT])
        C["from"] = fixed(ctx, nc, "c_from", [P, NT, 2], I32)
        route(nc, C, dram)
        experts(nc, C, dram)
        combine(nc, C, dram)


def scratch(nc, dram):
    dram["xnT"] = nc.dram_tensor("xnT", (NM, P, KC, MW), F32).ap()
    dram["vtab"] = nc.dram_tensor("vtab", (NP, VW), F32).ap()
    dram["ertab"] = nc.dram_tensor("ertab", (NP, H), F32).ap()
    dram["dst_f"] = nc.dram_tensor("dst_f", (NG, GE), F32).ap()
    dram["er_edge"] = nc.dram_tensor("er_edge", (EP, H), F32).ap()
    dram["acc"] = nc.dram_tensor("acc", (NP + NG, AW), F32).ap()
    dram["pen"] = nc.dram_tensor("pen", (NG, GE + 1), F32).ap()
    dram["x1"] = nc.dram_tensor("x1", (NP, D), F32).ap()
    dram["xe"] = nc.dram_tensor("xe", (EX * CAP, D), F32).ap()
    dram["ye"] = nc.dram_tensor("ye", (EX * CAP, D), F32).ap()
    dram["out"] = nc.dram_tensor("out_0_dram", (NP, D), F32, kind="ExternalOutput").ap()


def kernel(**inputs):
    import numpy as np
    import concourse.bacc as bacc
    from concourse.bass_utils import run_bass_kernel_spmd as run

    def given(name):
        return np.ascontiguousarray(inputs[name])

    def batches(edges):
        return np.ascontiguousarray(edges.reshape(ET // BT, BT, P).transpose(0, 2, 1))

    dst = np.pad(given("dst").astype(np.int32), (0, EP - E), constant_values=N)
    src = np.pad(given("src").astype(np.int32), (0, EP - E))
    arrays = {
        "x": np.pad(given("x"), ((0, NP - N), (0, 0))),
        "src": src, "src_em": batches(src),
        "dst": dst, "dst_before": np.concatenate([np.full(1, -1, np.int32), dst[:-1]]),
        "b1": np.ascontiguousarray(given("L0_ffn_b1").reshape(EX, FC, P).transpose(0, 2, 1)),
    }
    for part in ("gnn", "mix", "ffn"):
        for name in inputs:
            short = name.removeprefix(f"L0_{part}_")
            if short != name and short in _INS and short not in arrays:
                arrays[short] = given(name).reshape(_INS[short])
    nc = bacc.Bacc("TRN2", target_bir_lowering=False, num_devices=1)
    dram = {name: nc.dram_tensor(f"in_{name}", a.shape, mybir.dt.from_np(a.dtype), kind="ExternalInput").ap()
            for name, a in arrays.items()}
    scratch(nc, dram)
    build(nc, dram)
    result = run(nc, [{f"in_{name}": a for name, a in arrays.items()}], core_ids=[0])
    return result.results[0]["out_0_dram"][:N]
```
